# Optimizing a Trainium2 kernel written in Bass

```python
import numpy as np
import jax
import jax.numpy as jnp

def _softmax(x, axis=-1):
    return jax.nn.softmax(x, axis=axis)

def _gelu(x):
    return jax.nn.gelu(x, approximate=True)

def _silu(x):
    return jax.nn.silu(x)

def _sigmoid(x):
    return jax.nn.sigmoid(x)

def _layernorm(x, axis=-1, eps=1e-05):
    m = jnp.mean(x, axis=axis, keepdims=True)
    v = jnp.var(x, axis=axis, keepdims=True)
    return (x - m) / jnp.sqrt(v + eps)

def _scatter_add(tgt, idx, src, axis=0):
    return tgt.at[idx].add(src)

def _segment_sum(src, seg, n):
    return jax.ops.segment_sum(src, seg, n)
kernel_name = 'mk_hybrid_d1_jaxref_r8_1bbb9c'

def setup_inputs(seed: int=0):
    np.random.seed(seed)
    _w = jnp.asarray

    def _L0_attn_a_setup():
        import jax, jax.numpy as jnp
        import numpy as np
        NUM_HEADS = 16
        SM_SCALE = 0.5

        def _split_heads(t):
            B, S, E = t.shape
            D = E // NUM_HEADS
            return t.reshape(B, S, NUM_HEADS, D).transpose(0, 2, 1, 3)
        key = jax.random.key(seed)
        ks = jax.random.split(key, 5)
        B, S, E = (4, 256, 256)
        std = 1.0 / np.sqrt(E)
        return {'x': jax.random.normal(ks[0], (B, S, E), dtype=jnp.float32), 'Wq': jax.random.normal(ks[1], (E, E), dtype=jnp.float32) * std, 'bq': jnp.zeros((E,), dtype=jnp.float32), 'Wk': jax.random.normal(ks[2], (E, E), dtype=jnp.float32) * std, 'bk': jnp.zeros((E,), dtype=jnp.float32), 'Wv': jax.random.normal(ks[3], (E, E), dtype=jnp.float32) * std, 'bv': jnp.zeros((E,), dtype=jnp.float32), 'Wo': jax.random.normal(ks[4], (E, E), dtype=jnp.float32) * std, 'bo': jnp.zeros((E,), dtype=jnp.float32)}
    _L0_attn_a_in = _L0_attn_a_setup()

    def _L0_attn_b_setup():
        import jax, jax.numpy as jnp
        import numpy as np
        HIDDEN = 256
        NUM_V = 16
        NUM_K = 8
        HK = 128
        HV = 128
        KCONV = 4
        KEY_DIM = NUM_K * HK
        VALUE_DIM = NUM_V * HV
        CONV_DIM = 2 * KEY_DIM + VALUE_DIM
        R = NUM_V // NUM_K
        L2_EPS = 1e-06
        NORM_EPS = 1e-06
        key = jax.random.key(seed)
        ks = jax.random.split(key, 8)
        s = 0.02
        return {'hidden_states': jax.random.normal(ks[0], (1, 128, HIDDEN), jnp.float32), 'w_qkvz': jax.random.normal(ks[1], (2 * KEY_DIM + 2 * VALUE_DIM, HIDDEN), jnp.float32) * s, 'w_ba': jax.random.normal(ks[2], (2 * NUM_V, HIDDEN), jnp.float32) * s, 'conv_w': jax.random.normal(ks[3], (CONV_DIM, KCONV), jnp.float32) * s, 'dt_bias': jnp.ones((NUM_V,), jnp.float32), 'A_log': jnp.log(jax.random.uniform(ks[4], (NUM_V,), jnp.float32, 0.001, 16.0)), 'norm_weight': jnp.ones((HV,), jnp.float32), 'w_out': jax.random.normal(ks[5], (HIDDEN, VALUE_DIM), jnp.float32) * s}
    _L0_attn_b_in = _L0_attn_b_setup()

    def _L0_ffn_setup():
        import jax, jax.numpy as jnp
        import numpy as np
        B, L, D = (2, 128, 256)
        E, K = (8, 2)
        H, HS = (176, 352)
        key = jax.random.key(seed)
        ks = jax.random.split(key, 9)
        s = 0.02
        return {'x': jax.random.normal(ks[0], (B, L, D), dtype=jnp.float32), 'gate_w': jax.random.normal(ks[1], (E, D), dtype=jnp.float32) * s, 'w_gate': jax.random.normal(ks[2], (E, D, H), dtype=jnp.float32) * s, 'w_up': jax.random.normal(ks[3], (E, D, H), dtype=jnp.float32) * s, 'w_down': jax.random.normal(ks[4], (E, H, D), dtype=jnp.float32) * s, 'shgate_w': jax.random.normal(ks[5], (D,), dtype=jnp.float32) * s, 'shw_gate': jax.random.normal(ks[6], (D, HS), dtype=jnp.float32) * s, 'shw_up': jax.random.normal(ks[7], (D, HS), dtype=jnp.float32) * s, 'shw_down': jax.random.normal(ks[8], (HS, D), dtype=jnp.float32) * s}
    _L0_ffn_in = _L0_ffn_setup()
    _d = {'L0_attn_a_x': _L0_attn_a_in['x'], 'L0_attn_a_Wq': _L0_attn_a_in['Wq'], 'L0_attn_a_bq': _L0_attn_a_in['bq'], 'L0_attn_a_Wk': _L0_attn_a_in['Wk'], 'L0_attn_a_bk': _L0_attn_a_in['bk'], 'L0_attn_a_Wv': _L0_attn_a_in['Wv'], 'L0_attn_a_bv': _L0_attn_a_in['bv'], 'L0_attn_a_Wo': _L0_attn_a_in['Wo'], 'L0_attn_a_bo': _L0_attn_a_in['bo'], 'L0_attn_b_w_qkvz': _L0_attn_b_in['w_qkvz'], 'L0_attn_b_w_ba': _L0_attn_b_in['w_ba'], 'L0_attn_b_conv_w': _L0_attn_b_in['conv_w'], 'L0_attn_b_dt_bias': _L0_attn_b_in['dt_bias'], 'L0_attn_b_A_log': _L0_attn_b_in['A_log'], 'L0_attn_b_norm_weight': _L0_attn_b_in['norm_weight'], 'L0_attn_b_w_out': _L0_attn_b_in['w_out'], 'L0_ffn_gate_w': _L0_ffn_in['gate_w'], 'L0_ffn_w_gate': _L0_ffn_in['w_gate'], 'L0_ffn_w_up': _L0_ffn_in['w_up'], 'L0_ffn_w_down': _L0_ffn_in['w_down'], 'L0_ffn_shgate_w': _L0_ffn_in['shgate_w'], 'L0_ffn_shw_gate': _L0_ffn_in['shw_gate'], 'L0_ffn_shw_up': _L0_ffn_in['shw_up'], 'L0_ffn_shw_down': _L0_ffn_in['shw_down']}
    _x0 = _d['L0_attn_a_x']
    _d['L0_attn_a_x'] = jax.random.normal(jax.random.fold_in(jax.random.key(seed), 1), (8, 256, 256), dtype=_x0.dtype)
    del _x0
    return _d

def reference(L0_attn_a_x, L0_attn_a_Wq, L0_attn_a_bq, L0_attn_a_Wk, L0_attn_a_bk, L0_attn_a_Wv, L0_attn_a_bv, L0_attn_a_Wo, L0_attn_a_bo, L0_attn_b_w_qkvz, L0_attn_b_w_ba, L0_attn_b_conv_w, L0_attn_b_dt_bias, L0_attn_b_A_log, L0_attn_b_norm_weight, L0_attn_b_w_out, L0_ffn_gate_w, L0_ffn_w_gate, L0_ffn_w_up, L0_ffn_w_down, L0_ffn_shgate_w, L0_ffn_shw_gate, L0_ffn_shw_up, L0_ffn_shw_down):

    def _L0_attn_a_ref(x, Wq, bq, Wk, bk, Wv, bv, Wo, bo):
        import jax, jax.numpy as jnp
        import numpy as np
        NUM_HEADS = 16
        SM_SCALE = 0.5

        def _split_heads(t):
            B, S, E = t.shape
            D = E // NUM_HEADS
            return t.reshape(B, S, NUM_HEADS, D).transpose(0, 2, 1, 3)
        B, S, E = x.shape
        q = _split_heads(x @ Wq.T + bq)
        k = _split_heads(x @ Wk.T + bk)
        v = _split_heads(x @ Wv.T + bv)
        scores = jnp.einsum('bhqd,bhkd->bhqk', q, k) * SM_SCALE
        attn = jax.nn.softmax(scores, axis=-1)
        out = jnp.einsum('bhqk,bhkd->bhqd', attn, v)
        out = out.transpose(0, 2, 1, 3).reshape(B, S, E)
        return out @ Wo.T + bo

    def _L0_attn_b_ref(hidden_states, w_qkvz, w_ba, conv_w, dt_bias, A_log, norm_weight, w_out):
        import jax, jax.numpy as jnp
        import numpy as np
        HIDDEN = 256
        NUM_V = 16
        NUM_K = 8
        HK = 128
        HV = 128
        KCONV = 4
        KEY_DIM = NUM_K * HK
        VALUE_DIM = NUM_V * HV
        CONV_DIM = 2 * KEY_DIM + VALUE_DIM
        R = NUM_V // NUM_K
        L2_EPS = 1e-06
        NORM_EPS = 1e-06
        B, T, _ = hidden_states.shape
        qkvz = hidden_states @ w_qkvz.T
        ba = hidden_states @ w_ba.T
        qkvz = qkvz.reshape(B, T, NUM_K, 2 * HK + 2 * R * HV)
        q, k, v, z = jnp.split(qkvz, [HK, 2 * HK, 2 * HK + R * HV], axis=3)
        v = v.reshape(B, T, NUM_V, HV)
        z = z.reshape(B, T, NUM_V, HV)
        ba = ba.reshape(B, T, NUM_K, 2 * R)
        b = ba[..., :R].reshape(B, T, NUM_V)
        a = ba[..., R:].reshape(B, T, NUM_V)
        mixed = jnp.concatenate([q.reshape(B, T, KEY_DIM), k.reshape(B, T, KEY_DIM), v.reshape(B, T, VALUE_DIM)], axis=-1)
        xc = mixed.transpose(0, 2, 1)
        yc = jax.lax.conv_general_dilated(xc, conv_w[:, None, :], (1,), [(KCONV - 1, 0)], feature_group_count=CONV_DIM, dimension_numbers=('NCH', 'OIH', 'NCH'))
        yc = jax.nn.silu(yc).transpose(0, 2, 1)
        q, k, v = jnp.split(yc, [KEY_DIM, 2 * KEY_DIM], axis=-1)
        q = q.reshape(B, T, NUM_K, HK)
        k = k.reshape(B, T, NUM_K, HK)
        v = v.reshape(B, T, NUM_V, HV)
        beta = jax.nn.sigmoid(b)
        g = -jnp.exp(A_log) * jax.nn.softplus(a + dt_bias)
        q = jnp.repeat(q, R, axis=2)
        k = jnp.repeat(k, R, axis=2)
        q = q * jax.lax.rsqrt(jnp.sum(q * q, -1, keepdims=True) + L2_EPS)
        k = k * jax.lax.rsqrt(jnp.sum(k * k, -1, keepdims=True) + L2_EPS)
        scale = HK ** (-0.5)

        def step(S, xs):
            qt, kt, vt, gt, bt = xs
            S = S * jnp.exp(gt)[..., None, None]
            kv = jnp.einsum('bhk,bhkv->bhv', kt, S)
            delta = (vt - kv) * bt[..., None]
            S = S + jnp.einsum('bhk,bhv->bhkv', kt, delta)
            o = jnp.einsum('bhk,bhkv->bhv', qt * scale, S)
            return (S, o)
        S0 = jnp.zeros((B, NUM_V, HK, HV), hidden_states.dtype)
        xs = (q.transpose(1, 0, 2, 3), k.transpose(1, 0, 2, 3), v.transpose(1, 0, 2, 3), g.transpose(1, 0, 2), beta.transpose(1, 0, 2))
        _, o = jax.lax.scan(step, S0, xs)
        o = o.transpose(1, 0, 2, 3)
        xf = o.astype(jnp.float32) * jax.nn.silu(z.astype(jnp.float32))
        var = jnp.mean(xf * xf, -1, keepdims=True)
        xn = xf * jax.lax.rsqrt(var + NORM_EPS) * norm_weight
        return xn.reshape(B, T, VALUE_DIM) @ w_out.T

    def _L0_ffn_ref(x, gate_w, w_gate, w_up, w_down, shgate_w, shw_gate, shw_up, shw_down):
        import jax, jax.numpy as jnp
        import numpy as np
        B, L, D = (2, 128, 256)
        E, K = (8, 2)
        H, HS = (176, 352)
        b, l, d = x.shape
        xf = x.reshape(-1, d)
        logits = jnp.einsum('td,ed->te', xf.astype(jnp.float32), gate_w)
        probs = jax.nn.softmax(logits.astype(jnp.float32), axis=-1)
        weights, indices = jax.lax.top_k(probs, K)
        weights = (weights / weights.sum(-1, keepdims=True)).astype(x.dtype)
        onehot = jax.nn.one_hot(indices, E, dtype=x.dtype)
        combine = jnp.einsum('tk,tke->te', weights, onehot)
        g = jnp.einsum('td,edh->teh', xf, w_gate)
        u = jnp.einsum('td,edh->teh', xf, w_up)
        h = jax.nn.silu(g) * u
        out = jnp.einsum('teh,ehd,te->td', h.astype(jnp.float32), w_down.astype(jnp.float32), combine.astype(jnp.float32))
        sgate = jax.nn.sigmoid(xf @ shgate_w)[:, None]
        sh = jax.nn.silu(xf @ shw_gate) * (xf @ shw_up) @ shw_down
        out = out + (sgate * sh).astype(jnp.float32)
        return out.astype(x.dtype).reshape(b, l, d)
    x = L0_attn_a_x
    x = x + _L0_attn_a_ref(_layernorm(x, axis=-1), L0_attn_a_Wq, L0_attn_a_bq, L0_attn_a_Wk, L0_attn_a_bk, L0_attn_a_Wv, L0_attn_a_bv, L0_attn_a_Wo, L0_attn_a_bo)
    x = x + _L0_ffn_ref(_layernorm(x, axis=-1), L0_ffn_gate_w, L0_ffn_w_gate, L0_ffn_w_up, L0_ffn_w_down, L0_ffn_shgate_w, L0_ffn_shw_gate, L0_ffn_shw_up, L0_ffn_shw_down)
    x = x + _L0_attn_b_ref(_layernorm(x, axis=-1), L0_attn_b_w_qkvz, L0_attn_b_w_ba, L0_attn_b_conv_w, L0_attn_b_dt_bias, L0_attn_b_A_log, L0_attn_b_norm_weight, L0_attn_b_w_out)
    x = x + _L0_ffn_ref(_layernorm(x, axis=-1), L0_ffn_gate_w, L0_ffn_w_gate, L0_ffn_w_up, L0_ffn_w_down, L0_ffn_shgate_w, L0_ffn_shw_gate, L0_ffn_shw_up, L0_ffn_shw_down)
    return x

_drawn_inputs = setup_inputs


def setup_inputs(seed=0):
    import zlib

    import numpy as np

    out = dict(_drawn_inputs(seed))
    spreads = {'L0_attn_a_bq': (0.0, 0.1),
     'L0_attn_a_bk': (0.0, 0.8),
     'L0_attn_a_bv': (0.0, 0.1),
     'L0_attn_a_bo': (0.0, 0.1),
     'L0_attn_b_dt_bias': (1.0, 0.6),
     'L0_attn_b_norm_weight': (1.0, 0.6)}
    factors = {'L0_attn_b_w_qkvz': 8.0,
     'L0_attn_b_w_ba': 8.0,
     'L0_attn_b_conv_w': 8.0,
     'L0_attn_b_A_log': 8.0,
     'L0_attn_b_w_out': 8.0,
     'L0_ffn_gate_w': 3.426,
     'L0_ffn_w_gate': 3.032,
     'L0_ffn_w_up': 2.995,
     'L0_ffn_w_down': 2.986,
     'L0_ffn_shgate_w': 8.0,
     'L0_ffn_shw_gate': 2.943,
     'L0_ffn_shw_up': 2.892,
     'L0_ffn_shw_down': 2.899}
    for name, (base, spread) in spreads.items():
        noise = np.random.default_rng([zlib.crc32(name.encode()), seed]).standard_normal(out[name].shape)
        drawn = base * np.exp(spread * noise) if base else spread * noise
        out[name] = jnp.asarray(drawn.astype(out[name].dtype))
    for name, factor in factors.items():
        out[name] = (out[name] * factor).astype(out[name].dtype)
    return out
```

```python
from contextlib import ExitStack

import numpy as np

import concourse.bass as bass
from concourse import mybir
from concourse.alu_op_type import AluOpType as ALU

F32 = mybir.dt.float32
BF16 = mybir.dt.bfloat16
I32 = mybir.dt.int32
ACT = mybir.ActivationFunctionType
AX = mybir.AxisListType

P = 128
NBATCH = 8
T = 256
D = 256
KD = D // P
TT = T // P
NTILE = NBATCH * TT
LN_EPS = 1e-5

HEADS, HD = 16, 16
HP = 32
QB = HEADS * HP // P
SM_SCALE = 0.5

E, HID, HSH = 8, 176, 352
NE = E + HSH // HID
FH = NE * HID
NB = -(-FH // P)
BLK = [min(P, FH - P * j) for j in range(NB)]

NK, R, NV = 8, 2, 16
GROUP = 2 + 2 * R
TAPS = 4
L2_EPS = 1e-6
LEVELS = 7
MID = LEVELS - 1

STEPS_ATTN, STEPS_FFN, STEPS_GDN, STEPS_POOL = 18, 36, 71, 216


class Steps:

    def __init__(self, eng, sem, after_wait=None):
        self.eng, self.sem, self.base, self.n, self.after_wait = eng, sem, 0, 0, after_wait

    def link(self, ins):
        self.n += 1
        ins.then_inc(self.sem, 1)
        self.eng.wait_ge(self.sem, self.base + self.n)
        if self.after_wait is not None:
            self.after_wait()

    def turn(self, base):
        self.base, self.n = base, 0


def build(nc, io, stages=4):
    ctx = ExitStack()
    with ctx:
        def sb(name, shape, dt=F32):
            return ctx.enter_context(nc.sbuf_tensor(name, shape, dt))

        def sem(name):
            return ctx.enter_context(nc.semaphore(name))

        x = sb("x", [P, NTILE, D])
        xT = sb("xT", [P, KD, T])
        xn = sb("xn", [P, TT, D])
        stats = sb("stats", [P, TT, 6])
        mean = sb("mean", [P, TT, 1])
        varp, newt, rstd = sb("varp", [P, TT, 1]), sb("newt", [P, TT, 1]), sb("rstd", [P, TT, 1])
        ident = sb("ident", [P, P])
        identb = sb("identb", [P, P], BF16)
        upto = sb("upto", [P, P])
        merge = sb("merge", [P, LEVELS, P], I32)
        carried = sb("carried", [P, 4])
        merge0 = sb("merge0", [P, P])
        pick = sb("pick", [96, 16])
        selF = sb("selF", [96, NE, HID], BF16)
        selG = sb("selG", [96, NV, P], BF16)
        desc = sb("desc", [P, TT, E])
        parts = sb("parts", [P, TT, 96], BF16)
        partsT = sb("partsT", [96, T], BF16)
        wout = sb("wout", [P, NV, D])
        wba = sb("wba", [P, KD, 2 * NV])
        convw = sb("convw", [P, NK, 4, TAPS])
        dtb = sb("dtb", [P, NV])
        negA = sb("negA", [P, NV])
        normw = sb("normw", [P, 1])
        big = sb("big", [P, KD * NK * GROUP * P])
        small = sb("small", [P, 1280])
        ARENA = 21760
        arena = sb("arena", [P, ARENA])

        used = {"arena": 0, "small": 0}

        def carve(n, where="arena"):
            a = used[where]
            used[where] = a + n
            t = arena if where == "arena" else small
            assert used[where] <= (ARENA if where == "arena" else 1280), used
            return t[:, a:a + n]

        def view(ap, pattern, **k):
            return ap.rearrange(pattern, **k)

        NW = KD * FH

        def ffn_weights(t):
            return (view(t[:, 0:NW], "p (k n) -> p k n", k=KD), view(t[:, NW:2 * NW], "p (k n) -> p k n", k=KD),
                    view(t[:, 2 * NW:2 * NW + NB * D], "p (j n) -> p j n", j=NB))
        wr = sb("wr", [P, KD, E + 1])
        ffnw = [ffn_weights(carve(2 * NW + NB * D)), ffn_weights(big)]
        wq = view(carve(KD * QB * P), "p (k n) -> p k n", k=KD)
        wk = view(carve(KD * QB * P), "p (k n) -> p k n", k=KD)
        wv = view(carve(KD * D), "p (k n) -> p k n", k=KD)
        wo = view(carve(KD * D), "p (k n) -> p k n", k=KD)
        bq, bk = carve(QB), carve(QB)
        bv, bo = carve(D), carve(D)
        after_attn_weights = used["arena"]
        qT = view(carve(QB * T), "p (b n) -> p b n", b=QB)
        kT = view(carve(QB * T), "p (b n) -> p b n", b=QB)
        v = view(carve(TT * D), "p (t n) -> p t n", t=TT)
        probs = view(carve(2 * TT * T), "p (s t n) -> p s t n", s=2, t=TT)
        probsT = view(carve(2 * TT * T), "p (s t n) -> p s t n", s=2, t=TT)
        o = view(carve(TT * D), "p (t n) -> p t n", t=TT)
        oT = view(carve(KD * T), "p (k n) -> p k n", k=KD)
        negmax = sb("negmax", [P, 2, TT])
        sums = sb("sums", [P, TT, HEADS])
        rsums = sb("rsums", [P, TT, HEADS])
        used["arena"] = after_attn_weights
        gact = view(carve(2 * T), "p (s n) -> p s n", s=2)
        hid = view(carve(2 * T), "p (s n) -> p s n", s=2)
        hidT = view(carve(2 * T), "p (s n) -> p s n", s=2)
        used["arena"] = 0
        yc = view(carve(4 * T), "p (b n) -> p b n", b=4)
        sq = carve(4 * P)
        qkn = view(carve(4 * 4 * P), "p (s m n) -> p s m n", s=4, m=4)
        vt = view(carve(4 * 4 * P), "p (s m n) -> p s m n", s=4, m=4)
        kqT = view(carve(4 * 4 * P), "p (s c m n) -> p s c m n", s=4, c=2, m=2)
        UP = view(carve(4 * 8 * P), "p (s m a n) -> p s m a n", s=4, m=4, a=2)
        sz = view(carve(4 * 4 * P), "p (s m n) -> p s m n", s=4, m=4)
        DT = view(carve(4 * P), "p (m n) -> p m n", m=4)
        dlast = view(carve(4 * 4), "p (s m) -> p s m", s=4)
        Y = view(carve(4 * 4 * P), "p (s m n) -> p s m n", s=4, m=4)
        X = view(carve(2 * 4 * P), "p (s m n) -> p s m n", s=2, m=4)
        NX = view(carve(2 * 4 * P), "p (s m n) -> p s m n", s=2, m=4)
        w01 = view(carve(4 * P), "p (m n) -> p m n", m=4)
        w0s = view(carve(2 * P), "p (m n) -> p m n", m=2)
        st = carve(2 * P)
        rhs1 = view(carve(2 * P), "p (m n) -> p m n", m=2)
        qst = view(carve(2 * P), "p (m n) -> p m n", m=2)
        xf = view(carve(4 * P), "p (m n) -> p m n", m=4)
        xfn = view(carve(4 * P), "p (m n) -> p m n", m=4)
        xnT = view(carve(2 * T), "p (r n) -> p r n", r=R)

        def tiny(*shape):
            n = int(np.prod(shape))
            ap = carve(n, "small")
            return view(ap, "p (a b) -> p a b", a=shape[0]) if len(shape) == 2 else ap

        wz = view(big[:, :], "p (k n) -> p k n", k=KD)

        banks = [ctx.enter_context(nc.psum_tensor(f"bank{n}", [P, 512], F32)) for n in range(8)]

        def bank(n, pattern=None, **k):
            return banks[n][:, :] if pattern is None else banks[n][:, :].rearrange(pattern, **k)

        x_in, w_attn, w_ffn, w_ffn2, w_gdn, c_in = (sem(n) for n in ("x_in", "w_attn", "w_ffn", "w_ffn2", "w_gdn", "c_in"))
        consts, out_done = sem("consts"), sem("out_done")
        vstep, astep = sem("vstep"), sem("astep")
        normed, xt_ps, xt_ready, x_done = (sem(n) for n in ("normed", "xt_ps", "xt_ready", "x_done"))
        q_ps, k_ps, v_ps, q_sb, k_sb, v_sb = (sem(n) for n in ("q_ps", "k_ps", "v_ps", "q_sb", "k_sb", "v_sb"))
        s_ps, mx_done, exp_done, pt_ps, pt_sb, pv_done = (sem(n) for n in ("s_ps", "mx_done", "exp_done", "pt_ps", "pt_sb", "pv_done"))
        o_sb, ot_ps, ot_sb, out_ps, xb_done = (sem(n) for n in ("o_sb", "ot_ps", "ot_sb", "out_ps", "xb_done"))
        rt_ps, gap_done, th_done, parts_done, ct_ps, ct_sb = (sem(n) for n in ("rt_ps", "gap_done", "th_done", "parts_done", "ct_ps", "ct_sb"))
        gu_ps, gact_done, h_done, cb_ps, ht_done, dn_done = (sem(n) for n in ("gu_ps", "gact_done", "h_done", "cb_ps", "ht_done", "dn_done"))
        ba_ps, ba_sb, g_to_act, g_to_dve, g_done, gc_ps, eg_done = (sem(n) for n in ("ba_ps", "ba_sb", "g_to_act", "g_to_dve", "g_done", "gc_ps", "eg_done"))
        gparts_done, at_ps, at_sb, nbeta_done = (sem(n) for n in ("gparts_done", "at_ps", "at_sb", "nbeta_done"))
        qk_ps, vp_ps, z_ps, tap_qk, tap_v, conv_qk, conv_v, yc_done, z_sb = (
            sem(n) for n in ("qk_ps", "vp_ps", "z_ps", "tap_qk", "tap_v", "conv_qk", "conv_v", "yc_done", "z_sb"))
        qkt_ps, vt_ps, sq_done, vt_sb, qkn_done, kq_ps, kq_sb, kk_ps, ab_ps, dt_done, up_done = (
            sem(n) for n in ("qkt_ps", "vt_ps", "sq_done", "vt_sb", "qkn_done", "kq_ps", "kq_sb", "kk_ps", "ab_ps", "dt_done", "up_done"))
        y_pre, y_done, xx_ps, xx_sb, nx_ps, nx_sb, yuy_ps = (
            sem(n) for n in ("y_pre", "y_done", "xx_ps", "xx_sb", "nx_ps", "nx_sb", "yuy_ps"))
        y_first = sem("y_first")
        w0_ps, w0_sb, st_ps, st_sb, ks_ps, r_done, w1_ps, w1_sb, og_ps, xf_done, sqx_done, xfn_done, xnt_ps, xnt_sb, acc_done = (
            sem(n) for n in ("w0_ps", "w0_sb", "st_ps", "st_sb", "ks_ps", "r_done", "w1_ps", "w1_sb", "og_ps", "xf_done",
                             "sqx_done", "xfn_done", "xnt_ps", "xnt_sb", "acc_done"))

        ssq_done, rn_done, ssx_done, rx_done, pstep, gmove_done, wout_scaled = (
            sem(n) for n in ("ssq_done", "rn_done", "ssx_done", "rx_done", "pstep", "gmove_done", "wout_scaled"))

        def at_least(eng, s, value):
            if not isinstance(value, int) or value > 0:
                eng.wait_ge(s, value)

        XT_BANK = 7
        E0, E1, E2, ACC = 7, 6, 5, 4

        block = ctx.enter_context(nc.Block())

        @block.sync
        def _(sp):
            xin = io["x"].rearrange("(n p) d -> p n d", p=P)
            sp.dma_start(x[:, 0:TT, :], xin[:, 0:TT, :]).then_inc(x_in, 16)
            for name, dst in (("ident", ident[:, :]), ("upto", upto[:, :]), ("merge", merge[:, :, :]), ("pick", pick[:, :]),
                              ("desc", desc[:, :, :]), ("normw", normw[:, :]), ("A_log", negA[:, :]), ("dt_bias", dtb[:, :])):
                sp.dma_start(dst, io[name]).then_inc(c_in, 16)
            for name, dst in (("wq", wq), ("wk", wk), ("wv", wv), ("bq", bq), ("bk", bk), ("bv", bv), ("bo", bo), ("wo", wo)):
                sp.dma_start(dst, io[name]).then_inc(w_attn, 16)
            sp.dma_start(x[:, TT:, :], xin[:, TT:, :]).then_inc(x_in, 16)
            for name, dst in (("wg", ffnw[0][0]), ("wu", ffnw[0][1]), ("wd", ffnw[0][2]), ("wr", wr[:, :, :])):
                sp.dma_start(dst, io[name]).then_inc(w_ffn, 16)
            for name, dst in (("wout", wout[:, :, :]), ("wba", wba[:, :, :]), ("convw", convw[:, :, :, :]), ("wz", wz)):
                sp.dma_start(dst, io[name]).then_inc(w_gdn, 16)
            if stages > 3:
                sp.wait_ge(z_ps, NK * NBATCH)
                for name, dst in (("wg", ffnw[1][0]), ("wu", ffnw[1][1]), ("wd", ffnw[1][2])):
                    sp.dma_start(dst, io[name]).then_inc(w_ffn2, 16)
            out = io["out"].rearrange("(n p) d -> p n d", p=P)
            with sp.Fori(0, NBATCH) as i:
                sp.wait_ge(x_done, (stages - 1) * NBATCH + 1 + i)
                sp.dma_start(out[:, bass.ds(2 * i, TT), :], x[:, bass.ds(2 * i, TT), :]).then_inc(out_done, 16)
            sp.wait_ge(out_done, 16 * NBATCH)

        def pool_waits():
            nc.gpsimd.tensor_tensor(carried[:, 2:3], ident[:, 0:1], ident[:, 0:1], ALU.add)

        def rsqrt(steps, vec, y, val, t, done=None):
            steps.link(vec.tensor_scalar(y.bitcast(I32), val.bitcast(I32), -0.5, float(0x5F375A86), ALU.mult, ALU.add))
            for step in range(3):
                steps.link(vec.tensor_tensor(t, y, y, ALU.mult))
                steps.link(vec.tensor_tensor(t, t, val, ALU.mult))
                steps.link(vec.tensor_scalar(t, t, -0.5, 1.5, ALU.mult, ALU.add))
                ins = vec.tensor_tensor(y, y, t, ALU.mult)
                if step < 2 or done is None:
                    steps.link(ins)
                else:
                    ins.then_inc(done, 1)

        def prep_norm(dve, steps, c, b):
            for t in range(TT):
                ins = nc.vector.bn_stats(stats[:, t, :], x[:, 2 * b + t, :])
            steps.link(ins)
            nc.vector.tensor_tensor(mean[:, :, :], stats[:, :, 1:2], stats[:, :, 4:5], ALU.add)
            nc.vector.tensor_tensor(newt[:, :, :], stats[:, :, 1:2], stats[:, :, 4:5], ALU.subtract)
            steps.link(nc.vector.tensor_tensor(varp[:, :, :], stats[:, :, 2:3], stats[:, :, 5:6], ALU.add))
            nc.vector.tensor_scalar(mean[:, :, :], mean[:, :, :], 0.5, None, ALU.mult)
            nc.vector.tensor_scalar(varp[:, :, :], varp[:, :, :], 1.0 / D, LN_EPS, ALU.mult, ALU.add)
            steps.link(nc.vector.scalar_tensor_tensor(newt[:, :, :], newt[:, :, :], 0.25, newt[:, :, :], ALU.mult, ALU.mult))
            steps.link(nc.vector.tensor_tensor(varp[:, :, :], varp[:, :, :], newt[:, :, :], ALU.add))
            rsqrt(steps, nc.vector, rstd[:, :, :], varp[:, :, :], newt[:, :, :])
            at_least(dve, xt_ps, c)
            for t in range(TT):
                ins = nc.vector.tensor_scalar(xn[:, t, :], x[:, 2 * b + t, :], mean[:, t, 0:1], rstd[:, t, 0:1],
                                              ALU.subtract, ALU.mult)
            ins.then_inc(normed, 1)

        def prep_turn(pe, c):
            pe.wait_ge(normed, c + 1)
            at_least(pe, xt_ready, c)
            b = bank(XT_BANK, "p (k n) -> p k n", k=KD)
            for t in range(TT):
                for k in range(KD):
                    ins = nc.tensor.transpose(b[:, k, t * P:(t + 1) * P], xn[:, t, k * P:(k + 1) * P], ident[:, :])
            ins.then_inc(xt_ps, 1)

        def prep_copy(act, c):
            act.wait_ge(xt_ps, c + 1)
            nc.scalar.activation(xT[:, :, :], bank(XT_BANK, "p (k n) -> p k n", k=KD), ACT.Copy).then_inc(xt_ready, 1)

        def split_parts(steps, src, rest, n):
            steps.link(nc.vector.tensor_copy(parts[:, :, 0:n], src))
            steps.link(nc.vector.tensor_tensor(rest, src, parts[:, :, 0:n], ALU.subtract))
            steps.link(nc.vector.tensor_copy(parts[:, :, 32:32 + n], rest))
            steps.link(nc.vector.tensor_tensor(rest, rest, parts[:, :, 32:32 + n], ALU.subtract))
            return nc.vector.tensor_copy(parts[:, :, 64:64 + n], rest)

        def turn_parts(pe, b):
            bb = banks[b][0:96, 0:T // 2].bitcast(BF16)
            for t in range(TT):
                ins = nc.tensor.transpose(bb[:, t * P:(t + 1) * P], parts[:, t, :], identb[:, :])
            return ins

        QBANK, KBANK, VBANK, SBANK, PBANK, OBANK, YBANK = (2, 3), (4, 5), 1, (2, 3), (4, 5), 6, 0

        def attn_pe(pe, a, nxt):
            pe.wait_ge(xt_ready, a + 1)
            for half, (w, bks, done) in enumerate(((wq, QBANK, q_ps), (wk, KBANK, k_ps))):
                for pair in range(2):
                    bb = bank(bks[pair], "p (b n) -> p b n", b=2)
                    for j in range(2):
                        blk = 2 * pair + j
                        for k in range(KD):
                            ins = nc.tensor.matmul(bb[:, j, :], w[:, k, blk * P:(blk + 1) * P], xT[:, k, :],
                                                   start=(k == 0), stop=(k == KD - 1))
                    ins.then_inc(done, 1)
            bb = bank(VBANK, "p (t n) -> p t n", t=TT)
            for t in range(TT):
                for k in range(KD):
                    ins = nc.tensor.matmul(bb[:, t, :], xT[:, k, t * P:(t + 1) * P], wv[:, k, :],
                                           start=(k == 0), stop=(k == KD - 1))
            ins.then_inc(v_ps, 1)

            def scores(h):
                if h == 0:
                    pe.wait_ge(q_sb, a + 1)
                    pe.wait_ge(k_sb, a + 1)
                if h >= 2:
                    pe.wait_ge(exp_done, HEADS * a + h - 1)
                r = HP * (h % 4)
                bb = bank(SBANK[h % 2], "p (t n) -> p t n", t=TT)
                for t in range(TT):
                    ins = nc.tensor.matmul(bb[:, t, :], qT[r:r + HD, h // 4, t * P:(t + 1) * P], kT[r:r + HD, h // 4, :],
                                           start=True, stop=True)
                ins.then_inc(s_ps, 1)

            def turn(h):
                pe.wait_ge(exp_done, HEADS * a + h + 1)
                if h >= 2:
                    pe.wait_ge(pt_sb, HEADS * a + h - 1)
                bb = bank(PBANK[h % 2], "p (t n) -> p t n", t=TT)
                for t in range(TT):
                    for kt in range(TT):
                        ins = nc.tensor.transpose(bb[:, kt, t * P:(t + 1) * P], probs[:, h % 2, t, kt * P:(kt + 1) * P],
                                                  ident[:, :])
                ins.then_inc(pt_ps, 1)

            def values(h):
                pe.wait_ge(pt_sb, HEADS * a + h + 1)
                if h == 0:
                    pe.wait_ge(v_sb, a + 1)
                    at_least(pe, o_sb, a)
                bb = bank(OBANK, "p (t n) -> p t n", t=TT)
                for t in range(TT):
                    for kt in range(TT):
                        ins = nc.tensor.matmul(bb[:, t, h * HD:(h + 1) * HD], probsT[:, h % 2, kt, t * P:(t + 1) * P],
                                               v[:, kt, h * HD:(h + 1) * HD], start=(kt == 0), stop=(kt == TT - 1))
                ins.then_inc(pv_done, 1)

            for s in range(HEADS + 2):
                if s < HEADS:
                    scores(s)
                if 1 <= s <= HEADS:
                    turn(s - 1)
                if s >= 2:
                    values(s - 2)
                if s == HEADS // 2 and nxt is not None:
                    prep_turn(pe, a + 1)
            pe.wait_ge(o_sb, a + 1)
            bb = bank(VBANK, "p (k n) -> p k n", k=KD)
            for t in range(TT):
                for k in range(KD):
                    ins = nc.tensor.transpose(bb[:, k, t * P:(t + 1) * P], o[:, t, k * P:(k + 1) * P], ident[:, :])
            ins.then_inc(ot_ps, 1)
            pe.wait_ge(ot_sb, a + 1)
            at_least(pe, x_done, a)
            bb = bank(YBANK, "p (t n) -> p t n", t=TT)
            for t in range(TT):
                for k in range(KD):
                    ins = nc.tensor.matmul(bb[:, t, :], oT[:, k, t * P:(t + 1) * P], wo[:, k, :],
                                           start=(k == 0), stop=(k == KD - 1))
            ins.then_inc(out_ps, 1)

        def attn_dve(dve, steps, a, i, nxt):
            for pair in range(2):
                dve.wait_ge(q_ps, 2 * a + pair + 1)
                bb = bank(QBANK[pair], "p (b n) -> p b n", b=2)
                for j in range(2):
                    blk = 2 * pair + j
                    ins = nc.vector.tensor_scalar(qT[:, blk, :], bb[:, j, :], bq[:, blk:blk + 1], SM_SCALE, ALU.add, ALU.mult)
            ins.then_inc(q_sb, 1)
            dve.wait_ge(v_ps, a + 1)
            nc.vector.tensor_tensor(v[:, :, :], bank(VBANK, "p (t n) -> p t n", t=TT),
                                    bv.unsqueeze(1).to_broadcast([P, TT, D]), ALU.add).then_inc(v_sb, 1)

            def top(h):
                dve.wait_ge(s_ps, HEADS * a + h + 1)
                nc.vector.tensor_reduce(negmax[:, h % 2, :], bank(SBANK[h % 2], "p (t n) -> p t n", t=TT), AX.X, ALU.max,
                                        negate=True).then_inc(mx_done, 1)

            def copy(h):
                dve.wait_ge(pt_ps, HEADS * a + h + 1)
                if h >= 2:
                    dve.wait_ge(pv_done, HEADS * a + h - 1)
                nc.vector.tensor_copy(probsT[:, h % 2, :, :], bank(PBANK[h % 2], "p (t n) -> p t n", t=TT)).then_inc(pt_sb, 1)

            for s in range(HEADS + 1):
                if s < HEADS:
                    top(s)
                if s >= 1:
                    copy(s - 1)
                if s == HEADS // 2 - 2 and nxt is not None:
                    prep_norm(dve, steps, a + 1, nxt)
            steps.link(nc.vector.reciprocal(rsums[:, :, :], sums[:, :, :]))
            dve.wait_ge(pv_done, HEADS * a + HEADS)
            hv = "p t (h e) -> p t h e"
            for t in range(TT):
                ob = bank(OBANK, "p (t h e) -> p t h e", t=TT, h=HEADS)
                ins = nc.vector.tensor_tensor(o[:, t, :].rearrange("p (h e) -> p h e", h=HEADS), ob[:, t, :, :],
                                              rsums[:, t, :].unsqueeze(2).to_broadcast([P, HEADS, HD]), ALU.mult)
            ins.then_inc(o_sb, 1)
            dve.wait_ge(out_ps, a + 1)
            dve.wait_ge(xb_done, a + 1)
            xs = x[:, bass.ds(2 * i, TT), :]
            nc.vector.tensor_tensor(xs, bank(YBANK, "p (t n) -> p t n", t=TT), xs, ALU.add).then_inc(x_done, 1)

        def attn_act(act, a, nxt):
            for pair in range(2):
                act.wait_ge(k_ps, 2 * a + pair + 1)
                bb = bank(KBANK[pair], "p (b n) -> p b n", b=2)
                for j in range(2):
                    blk = 2 * pair + j
                    ins = nc.scalar.activation(kT[:, blk, :], bb[:, j, :], ACT.Identity, bias=bk[:, blk:blk + 1])
            ins.then_inc(k_sb, 1)
            for h in range(HEADS):
                act.wait_ge(mx_done, HEADS * a + h + 1)
                if h >= 2:
                    act.wait_ge(pt_ps, HEADS * a + h - 1)
                bb = bank(SBANK[h % 2], "p (t n) -> p t n", t=TT)
                for t in range(TT):
                    ins = nc.scalar.activation(probs[:, h % 2, t, :], bb[:, t, :], ACT.Exp, bias=negmax[:, h % 2, t:t + 1],
                                               accum_out=sums[:, t, h:h + 1])
                ins.then_inc(exp_done, 1)
                if h == HEADS // 2 and nxt is not None:
                    prep_copy(act, a + 1)
            act.wait_ge(ot_ps, a + 1)
            nc.scalar.activation(oT[:, :, :], bank(VBANK, "p (k n) -> p k n", k=KD), ACT.Copy).then_inc(ot_sb, 1)

        GUB, CBB, DNB, RTB = (0, 1, 2), (3, 4), 5, 6

        def ffn_pe(pe, c, f, w, nxt):
            wg, wu, wd = w
            pe.wait_ge(xt_ready, c + 1)
            rt = banks[RTB][:, 0:TT * 16].rearrange("p (t n) -> p t n", t=TT)
            for t in range(TT):
                for k in range(KD):
                    ins = nc.tensor.matmul(rt[:, t, 0:E + 1], xT[:, k, t * P:(t + 1) * P], wr[:, k, :],
                                           start=(k == 0), stop=(k == KD - 1))
            ins.then_inc(rt_ps, 1)

            def gate_up(j):
                at_least(pe, h_done, NB * f + max(j - 2, 0))
                bb = bank(GUB[j % 3], "p (g n) -> p g n", g=2)
                m = BLK[j]
                for g, wt in enumerate((wg, wu)):
                    for k in range(KD):
                        ins = nc.tensor.matmul(bb[0:m, g, :], wt[:, k, j * P:j * P + m], xT[:, k, :],
                                               start=(k == 0), stop=(k == KD - 1))
                ins.then_inc(gu_ps, 1)

            def spread(j):
                at_least(pe, ht_done, NB * f + max(j - 1, 0))
                m = BLK[j]
                sel = selF[:, :, :].rearrange("p e n -> p (e n)")[:, j * P:j * P + m]
                nc.tensor.matmul(banks[CBB[j % 2]][0:m, 0:T], sel, partsT[:, :], start=True, stop=True).then_inc(cb_ps, 1)

            def down(j):
                pe.wait_ge(ht_done, NB * f + j + 1)
                if j == 0:
                    at_least(pe, x_done, c)
                bb = bank(DNB, "p (t n) -> p t n", t=TT)
                m = BLK[j]
                for t in range(TT):
                    ins = nc.tensor.matmul(bb[:, t, :], hidT[0:m, j % 2, t * P:(t + 1) * P], wd[0:m, j, :],
                                           start=(j == 0 and t == 0), stop=(j == NB - 1), skip_group_check=True)
                ins.then_inc(dn_done, 1)

            for s in range(NB + 3):
                if s < NB:
                    gate_up(s)
                if s == 2:
                    pe.wait_ge(parts_done, f + 1)
                    turn_parts(pe, RTB).then_inc(ct_ps, 1)
                    pe.wait_ge(ct_sb, f + 1)
                if 0 <= s - 2 < NB:
                    spread(s - 2)
                if s >= 3:
                    down(s - 3)
                if s == NB // 2 and nxt is not None:
                    prep_turn(pe, c + 1)

        def ffn_dve(dve, steps, c, f, i, nxt):
            lg, eq, oh1, oh2 = fl["lg"], fl["eq"], fl["oh1"], fl["oh2"]
            l8 = lg[:, :, 0:E]

            def first_max(m, src, oh):
                steps.link(nc.vector.tensor_reduce(m, src, AX.X, ALU.max))
                steps.link(nc.vector.tensor_tensor(eq, src, m.to_broadcast([P, TT, E]), ALU.is_equal))
                steps.link(nc.vector.tensor_tensor(eq, eq, desc[:, :, :], ALU.mult))
                steps.link(nc.vector.tensor_reduce(fl["mw"], eq, AX.X, ALU.max))
                steps.link(nc.vector.tensor_tensor(oh, eq, fl["mw"].to_broadcast([P, TT, E]), ALU.is_equal))

            dve.wait_ge(rt_ps, f + 1)
            rt = banks[RTB][:, 0:TT * 16].rearrange("p (t n) -> p t n", t=TT)
            steps.link(nc.vector.tensor_copy(lg[:, :, 0:E + 1], rt[:, :, 0:E + 1]))
            first_max(fl["m1"], l8, oh1)
            steps.link(nc.vector.scalar_tensor_tensor(fl["l2"], oh1, -1e30, l8, ALU.mult, ALU.add))
            first_max(fl["m2"], fl["l2"], oh2)
            nc.vector.tensor_copy(fl["gap"][:, :, 1:2], lg[:, :, E:E + 1])
            nc.vector.tensor_tensor(fl["gap"][:, :, 0:1], fl["m1"], fl["m2"], ALU.subtract).then_inc(gap_done, 1)
            dve.wait_ge(th_done, f + 1)
            nc.vector.tensor_scalar(fl["wt"][:, :, 0:2], fl["th"], 0.5, 0.5, ALU.mult, ALU.add)
            steps.link(nc.vector.tensor_scalar(fl["wt"][:, :, 2:3], fl["th"][:, :, 0:1], -0.5, 0.5, ALU.mult, ALU.add))
            wt = fl["wt"]
            cmb = fl["cmb"]
            nc.vector.tensor_copy(cmb[:, :, E:NE], wt[:, :, 1:2].to_broadcast([P, TT, NE - E]))
            nc.vector.tensor_tensor(oh1, oh1, wt[:, :, 0:1].to_broadcast([P, TT, E]), ALU.mult)
            steps.link(nc.vector.tensor_tensor(oh2, oh2, wt[:, :, 2:3].to_broadcast([P, TT, E]), ALU.mult))
            steps.link(nc.vector.tensor_tensor(cmb[:, :, 0:E], oh1, oh2, ALU.add))
            split_parts(steps, cmb, fl["rest"], NE).then_inc(parts_done, 1)

            def mul_up(j):
                dve.wait_ge(gact_done, NB * f + j + 1)
                at_least(dve, ht_done, NB * f + max(j - 1, 0))
                m = BLK[j]
                nc.vector.tensor_tensor(hid[0:m, j % 2, :], gact[0:m, j % 2, :], bank(GUB[j % 3])[0:m, T:2 * T], ALU.mult)\
                    .then_inc(h_done, 1)

            def weigh(j):
                dve.wait_ge(cb_ps, NB * f + j + 1)
                dve.wait_ge(h_done, NB * f + j + 1)
                at_least(dve, dn_done, NB * f + max(j - 1, 0))
                m = BLK[j]
                nc.vector.tensor_tensor(hidT[0:m, j % 2, :], hid[0:m, j % 2, :], banks[CBB[j % 2]][0:m, 0:T], ALU.mult)\
                    .then_inc(ht_done, 1)

            mul_up(0)
            for j in range(NB):
                if j + 1 < NB:
                    mul_up(j + 1)
                weigh(j)
                if j == NB // 2 - 2 and nxt is not None:
                    prep_norm(dve, steps, c + 1, nxt)
            dve.wait_ge(dn_done, NB * f + NB)
            xs = x[:, bass.ds(2 * i, TT), :]
            nc.vector.tensor_tensor(xs, bank(DNB, "p (t n) -> p t n", t=TT), xs, ALU.add).then_inc(x_done, 1)

        def ffn_act(act, c, f, nxt):
            act.wait_ge(gap_done, f + 1)
            nc.scalar.activation(fl["th"], fl["gap"], ACT.Tanh, scale=0.5).then_inc(th_done, 1)
            for j in range(NB):
                if j == 2:
                    act.wait_ge(ct_ps, f + 1)
                    nc.scalar.activation(partsT[:, :], banks[RTB][0:96, 0:T // 2].bitcast(BF16), ACT.Copy).then_inc(ct_sb, 1)
                act.wait_ge(gu_ps, NB * f + j + 1)
                at_least(act, h_done, NB * f + max(j - 1, 0))
                m = BLK[j]
                nc.scalar.activation(gact[0:m, j % 2, :], bank(GUB[j % 3])[0:m, 0:T], ACT.Silu).then_inc(gact_done, 1)
            if nxt is not None:
                prep_copy(act, c + 1)

        fl = {"lg": tiny(TT, 16), "eq": tiny(TT, E), "oh1": tiny(TT, E), "oh2": tiny(TT, E), "l2": tiny(TT, E),
              "m1": tiny(TT, 1), "m2": tiny(TT, 1), "mw": tiny(TT, 1), "gap": tiny(TT, 2), "th": tiny(TT, 2),
              "wt": tiny(TT, 4), "cmb": tiny(TT, NE), "rest": tiny(TT, NE)}

        SCALE_Q = float(P) ** -0.5
        gt = {n: tiny(TT, NV) for n in ("ad", "neg", "th", "e", "u", "ln", "d", "z", "r", "g", "rest", "alpha")}
        ba = tiny(TT, 2 * NV)
        nbeta = {False: tiny(TT, NV), True: tiny(TT, NV)}
        eG = {False: tiny(NV), True: tiny(NV)}
        ssq, rn, rtmp = tiny(4), tiny(4), tiny(4)
        ssx, rx, rxt = tiny(4), tiny(4), tiny(4)

        def ebank(e, pattern=None, **k):
            return bank((E0, E1, E2)[e], pattern, **k)

        def mm4(b, m, n):
            return bank(b, "p (m n) -> p m n", m=4)[:, m, :]

        def gates_pe_ba(pe, g):
            pe.wait_ge(xt_ready, 2 * NBATCH + g + 1)
            at_least(pe, xnt_sb, NK * g - 2)
            b = ebank(1)[:, 0:TT * 2 * NV].rearrange("p (t n) -> p t n", t=TT)
            for t in range(TT):
                for k in range(KD):
                    ins = nc.tensor.matmul(b[:, t, :], xT[:, k, t * P:(t + 1) * P], wba[:, k, :],
                                           start=(k == 0), stop=(k == KD - 1))
            ins.then_inc(ba_ps, 1)

        def gates_dve_ba(dve, g):
            dve.wait_ge(ba_ps, g + 1)
            at_least(dve, nbeta_done, g)
            nc.vector.tensor_copy(ba, ebank(1)[:, 0:TT * 2 * NV].rearrange("p (t n) -> p t n", t=TT)).then_inc(ba_sb, 1)

        def gates_dve(dve, steps, g):
            dve.wait_ge(ba_sb, g + 1)
            steps.link(nc.vector.tensor_tensor(gt["ad"], ba[:, :, NV:], dtb[:, :].unsqueeze(1).to_broadcast([P, TT, NV]), ALU.add))
            steps.link(nc.vector.tensor_scalar(gt["neg"], gt["ad"], -1.0, None, ALU.mult))
            nc.vector.tensor_tensor(gt["neg"], gt["neg"], gt["ad"], ALU.min).then_inc(g_to_act, 1)
            dve.wait_ge(g_to_dve, 3 * g + 1)
            nc.vector.tensor_scalar(gt["u"], gt["e"], 1.0, None, ALU.add).then_inc(g_to_act, 1)
            dve.wait_ge(g_to_act, 2 * g + 2)
            steps.link(nc.vector.tensor_scalar(gt["d"], gt["u"], -1.0, None, ALU.add))
            steps.link(nc.vector.tensor_scalar(gt["z"], gt["d"], 0.0, None, ALU.is_equal))
            steps.link(nc.vector.tensor_tensor(gt["d"], gt["d"], gt["z"], ALU.add))
            steps.link(nc.vector.reciprocal(gt["r"], gt["d"]))
            steps.link(nc.vector.tensor_tensor(gt["r"], gt["r"], gt["e"], ALU.mult))
            dve.wait_ge(g_to_dve, 3 * g + 2)
            steps.link(nc.vector.tensor_tensor(gt["z"], gt["z"], gt["ln"], ALU.add))
            steps.link(nc.vector.tensor_tensor(gt["z"], gt["z"], gt["r"], ALU.mult))
            steps.link(nc.vector.scalar_tensor_tensor(gt["z"], gt["ad"], 0.0, gt["z"], ALU.max, ALU.add))
            nc.vector.tensor_tensor(gt["g"], gt["z"], negA[:, :].unsqueeze(1).to_broadcast([P, TT, NV]), ALU.mult)\
                .then_inc(g_done, 1)
            nc.vector.tensor_scalar(nbeta[True], gt["th"], -0.5, -0.5, ALU.mult, ALU.add).then_inc(nbeta_done, 1)
            dve.wait_ge(g_to_dve, 3 * g + 3)
            at_least(dve, at_ps, g)
            split_parts(steps, gt["alpha"], gt["rest"], NV).then_inc(gparts_done, 1)

        def gates_act(act, g):
            act.wait_ge(ba_sb, g + 1)
            nc.scalar.activation(gt["th"], ba[:, :, 0:NV], ACT.Tanh, scale=0.5)
            act.wait_ge(g_to_act, 2 * g + 1)
            nc.scalar.activation(gt["e"], gt["neg"], ACT.Exp).then_inc(g_to_dve, 1)
            act.wait_ge(g_to_act, 2 * g + 2)
            nc.scalar.activation(gt["ln"], gt["u"], ACT.Ln).then_inc(g_to_dve, 1)
            act.wait_ge(g_done, g + 1)
            nc.scalar.activation(gt["alpha"], gt["g"], ACT.Exp).then_inc(g_to_dve, 1)

        def gates_pe_rest(pe, g):
            pe.wait_ge(z_sb, NK * g + 1)
            pe.wait_ge(g_done, g + 1)
            nc.tensor.matmul(ebank(2)[:, 0:NV], upto[:, :], gt["g"][:, 1, :], start=True, stop=True).then_inc(gc_ps, 1)
            pe.wait_ge(gparts_done, g + 1)
            pe.wait_ge(eg_done, g + 1)
            turn_parts(pe, E2).then_inc(at_ps, 1)

        def gates_act_rest(act, g):
            act.wait_ge(gc_ps, g + 1)
            at_least(act, gmove_done, g)
            nc.scalar.activation(eG[True], ebank(2)[:, 0:NV], ACT.Exp).then_inc(eg_done, 1)
            act.wait_ge(at_ps, g + 1)
            nc.scalar.activation(partsT[:, :], banks[E2][0:96, 0:T // 2].bitcast(BF16), ACT.Copy).then_inc(at_sb, 1)

        def gates_move(dve, g):
            dve.wait_ge(eg_done, g + 1)
            dve.wait_ge(nbeta_done, g + 1)
            nc.vector.tensor_copy(nbeta[False], nbeta[True])
            nc.vector.tensor_copy(eG[False], eG[True]).then_inc(gmove_done, 1)
            dve.wait_ge(gmove_done, g + 1)

        def project_pe(pe, H, n, gates):
            odd = n % 2
            w0 = (n % NK) * GROUP * P
            if odd:
                pe.wait_ge(kq_sb, H)
            else:
                at_least(pe, xf_done, H - 2)
            b = ebank(0, "p (b n) -> p b n", b=2)
            for j in range(2):
                for k in range(KD):
                    ins = nc.tensor.matmul(b[:, j, :], wz[:, k, w0 + j * P:w0 + (j + 1) * P], xT[:, k, :],
                                           start=(k == 0), stop=(k == KD - 1))
            ins.then_inc(qk_ps, 1)
            if odd:
                pe.wait_ge(up_done, H)
            else:
                at_least(pe, xnt_sb, H - 2)
            if n % NK == 0:
                pe.wait_ge(ba_sb, gates)
            b = ebank(1, "p (b n) -> p b n", b=2)
            for j in range(2):
                for k in range(KD):
                    ins = nc.tensor.matmul(b[:, j, :], wz[:, k, w0 + (2 + j) * P:w0 + (3 + j) * P], xT[:, k, :],
                                           start=(k == 0), stop=(k == KD - 1))
            ins.then_inc(vp_ps, 1)
            if odd:
                pe.wait_ge(dt_done, H)
            else:
                at_least(pe, w1_sb, H - 2)
            b = ebank(2, "p (c n) -> p c n", c=TT)
            for c in range(TT):
                for k in range(KD):
                    ins = nc.tensor.matmul(b[:, c, :], xT[:, k, c * P:(c + 1) * P], wz[:, k, w0 + 4 * P:w0 + 6 * P],
                                           start=(k == 0), stop=(k == KD - 1))
            ins.then_inc(z_ps, 1)

        def taps_act(act, H, n):
            at_least(act, vt_ps, H)
            for e, ready, done in ((0, qk_ps, tap_qk), (1, vp_ps, tap_v)):
                act.wait_ge(ready, H + 1)
                b = ebank(e, "p (b n) -> p b n", b=2)
                for j in range(2):
                    blk = 2 * e + j
                    ins = nc.scalar.activation(yc[:, blk, :], b[:, j, :], ACT.Copy, scale=convw[:, n % NK, blk, TAPS - 1:TAPS])
                ins.then_inc(done, 1)

        def conv_dve(dve, steps, H, n, e):
            dve.wait_ge((tap_qk, tap_v)[e], H + 1)
            b = ebank(e, "p (b n) -> p b n", b=2)
            for back in range(1, TAPS):
                for j in range(2):
                    blk = 2 * e + j
                    ins = nc.vector.scalar_tensor_tensor(yc[:, blk, back:], b[:, j, 0:T - back],
                                                         convw[:, n % NK, blk, TAPS - 1 - back:TAPS - back],
                                                         yc[:, blk, back:], ALU.mult, ALU.add)
                if back < TAPS - 1:
                    steps.link(ins)
            ins.then_inc((conv_qk, conv_v)[e], 1)

        def z_act(act, H, n):
            act.wait_ge(z_ps, H + 1)
            nc.scalar.activation(sz[:, n % 4, :, :].rearrange("p m n -> p (m n)"), ebank(2), ACT.Silu).then_inc(z_sb, 1)

        def silu_act(act, H, n):
            act.wait_ge(conv_qk, H + 1)
            act.wait_ge(conv_v, H + 1)
            nc.scalar.activation(yc[:, :, :], yc[:, :, :], ACT.Silu).then_inc(yc_done, 1)

        def turn_pe(pe, H, n):
            pe.wait_ge(yc_done, H + 1)
            for j in range(2):
                for c in range(TT):
                    ins = nc.tensor.transpose(mm4(E0, 2 * j + c, P), yc[:, j, c * P:(c + 1) * P], ident[:, :])
            ins.then_inc(qkt_ps, 1)
            for c in range(TT):
                for r in range(R):
                    ins = nc.tensor.transpose(mm4(E1, 2 * c + r, P), yc[:, 2 + r, c * P:(c + 1) * P], ident[:, :])
            ins.then_inc(vt_ps, 1)

        def squares_act(act, H, n):
            act.wait_ge(qkt_ps, H + 1)
            at_least(act, qkn_done, H)
            nc.scalar.activation(sq, ebank(0), ACT.Square).then_inc(sq_done, 1)
            act.wait_ge(vt_ps, H + 1)
            nc.scalar.activation(vt[:, n % 4, :, :].rearrange("p m n -> p (m n)"), ebank(1), ACT.Copy).then_inc(vt_sb, 1)

        def norm_dve(dve, H, n):
            dve.wait_ge(sq_done, H + 1)
            nc.vector.tensor_reduce(ssq, sq.rearrange("p (m n) -> p m n", m=4), AX.X, ALU.add).then_inc(ssq_done, 1)
            dve.wait_ge(rn_done, H + 1)
            nc.vector.tensor_tensor(qkn[:, n % 4, :, :], ebank(0, "p (m n) -> p m n", m=4),
                                    rn.unsqueeze(2).to_broadcast([P, 4, P]), ALU.mult).then_inc(qkn_done, 1)

        def norm_pool(pool, psteps, H, n):
            pool.wait_ge(ssq_done, H + 1)
            pool_waits()
            psteps.link(nc.gpsimd.tensor_scalar(ssq, ssq, L2_EPS, None, ALU.add))
            rsqrt(psteps, nc.gpsimd, rn, ssq, rtmp)
            nc.gpsimd.tensor_scalar(rn[:, 0:2], rn[:, 0:2], SCALE_Q, None, ALU.mult).then_inc(rn_done, 1)
            pool.wait_ge(rn_done, H + 1)

        def turn_back_pe(pe, H, n):
            pe.wait_ge(qkn_done, H + 1)
            for c in range(TT):
                for a in range(2):
                    ins = nc.tensor.transpose(mm4(E0, 2 * c + a, P), qkn[:, n % 4, 2 * (1 - a) + c, :], ident[:, :])
            ins.then_inc(kq_ps, 1)

        def turn_back_act(act, H, n):
            act.wait_ge(kq_ps, H + 1)
            nc.scalar.activation(kqT[:, n % 4, :, :, :].rearrange("p c a n -> p (c a n)"), ebank(0), ACT.Copy).then_inc(kq_sb, 1)

        def products_pe(pe, H, n, gates):
            pe.wait_ge(kq_sb, H + 1)
            pe.wait_ge(vt_sb, H + 1)
            b = ebank(1, "p (c n) -> p c n", c=TT)
            for c in range(TT):
                ins = nc.tensor.matmul(b[:, c, :], kqT[:, n % 4, c, 0, :],
                                       kqT[:, n % 4, c, :, :].rearrange("p a n -> p (a n)"), start=True, stop=True)
            ins.then_inc(kk_ps, 1)
            pe.wait_ge(z_sb, H + 1)
            if n % NK == 0:
                pe.wait_ge(at_sb, gates)
            b = ebank(2, "p (r n) -> p r n", r=R)
            for r in range(R):
                ins = nc.tensor.matmul(b[:, r, :], selG[:, R * (n % NK) + r, :], partsT[:, :], start=True, stop=True)
            ins.then_inc(ab_ps, 1)

        def decay_dve(dve, H, n, gates):
            nxt = n >= NK
            dve.wait_ge(ab_ps, H + 1)
            at_least(dve, up_done, H)
            b = ebank(2, "p (r c n) -> p r c n", r=R, c=TT)
            for c in range(TT):
                for r in range(R):
                    ins = nc.vector.tensor_tensor_scan(DT[:, 2 * c + r, :], b[:, r, c, :], ident[:, :], 0.0, ALU.mult, ALU.add)
            ins.then_inc(dt_done, 1)
            dve.wait_ge(kk_ps, H + 1)
            dve.wait_ge(dt_done, H + 1)
            if n % NK == 0:
                dve.wait_ge(nbeta_done, gates)
            b = ebank(1, "p (c a n) -> p c a n", c=TT, a=2)
            for c in range(TT):
                for r in range(R):
                    hh = R * (n % NK) + r
                    nc.vector.scalar_tensor_tensor(UP[:, n % 4, 2 * c + r, :, :], b[:, c, :, :], nbeta[nxt][:, c, hh:hh + 1],
                                                   DT[:, 2 * c + r, :].unsqueeze(1).to_broadcast([P, 2, P]), ALU.mult, ALU.mult)
            nc.vector.tensor_copy(dlast[:, n % 4, :].unsqueeze(2), DT[:, :, P - 1:P]).then_inc(up_done, 1)

        def first_pool(pool, H, n):
            pool.wait_ge(up_done, H + 1)
            yy = Y[:, n % 4, :, :]
            nc.gpsimd.tensor_tensor(yy, UP[:, n % 4, :, 0, :], merge0[:, :].unsqueeze(1).to_broadcast([P, 4, P]), ALU.mult)\
                .then_inc(y_first, 1)
            pool.wait_ge(y_first, H + 1)
            nc.gpsimd.tensor_tensor(yy, yy, ident[:, :].unsqueeze(1).to_broadcast([P, 4, P]), ALU.add).then_inc(y_pre, 1)

        def turn_of(H, n, k):
            return MID * (H - n % 2) + 2 * k + n % 2 + 1

        def x_pe(pe, H, n, lv):
            if lv == 0:
                pe.wait_ge(y_pre, H + 1)
            else:
                pe.wait_ge(y_done, turn_of(H, n, lv - 1))
            for m in range(4):
                ins = nc.tensor.transpose(mm4(2 * (n % 2), m, P), Y[:, n % 4, m, :], ident[:, :])
            ins.then_inc(xx_ps, 1)

        def x_act(act, H, n, lv):
            act.wait_ge(xx_ps, turn_of(H, n, lv))
            nc.scalar.activation(X[:, n % 2, :, :].rearrange("p m n -> p (m n)"), bank(2 * (n % 2)), ACT.Copy).then_inc(xx_sb, 1)

        def nx_pe(pe, H, n, lv):
            pe.wait_ge(xx_sb, turn_of(H, n, lv - 1))
            for m in range(4):
                ins = nc.tensor.matmul(mm4(2 * (n % 2), m, P), UP[:, n % 4, m, 0, :], X[:, n % 2, m, :], start=True, stop=True)
            ins.then_inc(nx_ps, 1)

        def nx_act(act, H, n, lv):
            act.wait_ge(nx_ps, turn_of(H, n, lv - 1))
            nc.scalar.activation(NX[:, n % 2, :, :].rearrange("p m n -> p (m n)"), bank(2 * (n % 2)), ACT.Copy).then_inc(nx_sb, 1)

        def yuy_pe(pe, H, n, lv):
            pe.wait_ge(nx_sb, turn_of(H, n, lv - 1))
            for m in range(4):
                ins = nc.tensor.matmul(mm4(2 * (n % 2) + 1, m, P), NX[:, n % 2, m, :], Y[:, n % 4, m, :], start=True, stop=True)
            ins.then_inc(yuy_ps, 1)

        def merge_dve(dve, H, n, lv):
            dve.wait_ge(yuy_ps, turn_of(H, n, lv - 1))
            dve.wait_ge(y_pre, H + 1)
            if lv > 1:
                dve.wait_ge(y_done, turn_of(H, n, lv - 2))
            nc.vector.tensor_copy(carried[:, n % 2:n % 2 + 1], ident[:, 0:1])
            nc.vector.copy_predicated(Y[:, n % 4, :, :], merge[:, lv, :].unsqueeze(1).to_broadcast([P, 4, P]),
                                      bank(2 * (n % 2) + 1, "p (m n) -> p m n", m=4)).then_inc(y_done, 1)

        def walk_pe(pe, H, n, c_x, last, turned):
            s4 = n % 4
            even = n % 2 == 0

            def freed(e, seconds, firsts):
                if even:
                    pe.wait_ge(firsts, last if last is not None else H + 4)
                else:
                    pe.wait_ge(seconds, H)
            pe.wait_ge(y_done, turn_of(H, n, MID - 1))
            freed(2, w1_sb, dt_done)
            b = ebank(2)
            for r in range(R):
                ins = nc.tensor.matmul(b[:, r * P:(r + 1) * P], Y[:, s4, r, :], vt[:, s4, r, :], start=True, stop=True)
            ins.then_inc(w0_ps, 1)
            pe.wait_ge(w0_sb, H + 1)
            freed(0, xf_done, kq_sb)
            if turned is not None and even:
                pe.wait_ge(xt_ready, turned)
            nc.tensor.matmul(ebank(0)[:, 0:R * P], qkn[:, s4, 2, :], w0s.rearrange("p m n -> p (m n)"), start=True, stop=True)\
                .then_inc(st_ps, 1)
            pe.wait_ge(st_sb, H + 1)
            freed(1, xnt_sb, up_done)
            for a in range(2):
                ins = nc.tensor.matmul(ebank(1)[:, a * R * P:(a + 1) * R * P], kqT[:, s4, 1, a, :], st, start=True, stop=True)
            ins.then_inc(ks_ps, 1)
            pe.wait_ge(r_done, H + 1)
            for r in range(R):
                ins = nc.tensor.matmul(b[:, r * P:(r + 1) * P], Y[:, s4, 2 + r, :], rhs1[:, r, :], start=True, stop=True)
            ins.then_inc(w1_ps, 1)
            pe.wait_ge(w1_sb, H + 1)
            for m in range(4):
                ins = nc.tensor.matmul(mm4(E0, m, P), UP[:, s4, m, 1, :], w01[:, m, :], start=True, stop=True)
            ins.then_inc(og_ps, 1)
            pe.wait_ge(xfn_done, H + 1)
            for r in range(R):
                for c in range(TT):
                    ins = nc.tensor.transpose(mm4(E1, 2 * r + c, P), xfn[:, 2 * c + r, :], ident[:, :])
            ins.then_inc(xnt_ps, 1)
            pe.wait_ge(xnt_sb, H + 1)
            if n == 0:
                pe.wait_ge(x_done, c_x)
            b = bank(ACC, "p (t n) -> p t n", t=TT)
            for r in range(R):
                for t in range(TT):
                    ins = nc.tensor.matmul(b[:, t, :], xnT[:, r, t * P:(t + 1) * P], wout[:, R * n + r, :],
                                           start=(n == 0 and r == 0 and t == 0), stop=(n == NK - 1 and r == R - 1),
                                           skip_group_check=True)
            ins.then_inc(acc_done, 1)

        def walk_dve(dve, steps, H, n):
            s4 = n % 4
            hh = R * n
            dve.wait_ge(w0_ps, H + 1)
            b = ebank(2, "p (m n) -> p m n", m=4)
            nc.vector.tensor_copy(w01[:, 0:2, :], b[:, 0:2, :])
            for r in range(R):
                ins = nc.vector.tensor_scalar(w0s[:, r, :], b[:, r, :], nbeta[False][:, 0, hh + r:hh + r + 1],
                                              dlast[:, s4, r:r + 1], ALU.mult, ALU.mult)
            ins.then_inc(w0_sb, 1)
            dve.wait_ge(ks_ps, H + 1)
            b = ebank(1, "p (m n) -> p m n", m=4)
            for r in range(R):
                ins = nc.vector.scalar_tensor_tensor(rhs1[:, r, :], b[:, r, :], eG[False][:, hh + r:hh + r + 1],
                                                     vt[:, s4, 2 + r, :], ALU.mult, ALU.add)
            nc.vector.tensor_tensor(qst, b[:, 2:4, :], eG[False][:, hh:hh + 2].unsqueeze(2).to_broadcast([P, 2, P]), ALU.mult)\
                .then_inc(r_done, 1)
            dve.wait_ge(r_done, H + 1)
            dve.wait_ge(og_ps, H + 1)
            at_least(dve, xfn_done, H)
            b = ebank(0, "p (m n) -> p m n", m=4)
            steps.link(nc.vector.tensor_tensor(xf[:, 2:4, :], b[:, 2:4, :], qst, ALU.add))
            nc.vector.tensor_tensor(xf[:, 0:2, :], b[:, 0:2, :], sz[:, s4, 0:2, :], ALU.mult)
            nc.vector.tensor_tensor(xf[:, 2:4, :], xf[:, 2:4, :], sz[:, s4, 2:4, :], ALU.mult).then_inc(xf_done, 1)
            dve.wait_ge(sqx_done, H + 1)
            nc.vector.tensor_reduce(ssx, xfn[:, :, :], AX.X, ALU.add).then_inc(ssx_done, 1)
            dve.wait_ge(rx_done, H + 1)
            nc.vector.tensor_tensor(xfn[:, :, :], xf[:, :, :], rx.unsqueeze(2).to_broadcast([P, 4, P]), ALU.mult)\
                .then_inc(xfn_done, 1)

        def walk_pool(pool, psteps, H, n):
            pool.wait_ge(ssx_done, H + 1)
            pool_waits()
            psteps.link(nc.gpsimd.tensor_scalar(ssx, ssx, P * 1e-6, None, ALU.add))
            rsqrt(psteps, nc.gpsimd, rx, ssx, rxt, rx_done)

        def walk_act(act, H, n):
            act.wait_ge(st_ps, H + 1)
            nc.scalar.activation(st, ebank(0)[:, 0:R * P], ACT.Copy).then_inc(st_sb, 1)
            act.wait_ge(w1_ps, H + 1)
            nc.scalar.activation(w01[:, 2:4, :].rearrange("p m n -> p (m n)"), ebank(2)[:, 0:R * P], ACT.Copy).then_inc(w1_sb, 1)
            act.wait_ge(xf_done, H + 1)
            nc.scalar.activation(xfn[:, :, :], xf[:, :, :], ACT.Square).then_inc(sqx_done, 1)
            act.wait_ge(xnt_ps, H + 1)
            nc.scalar.activation(xnT[:, :, :].rearrange("p r n -> p (r n)"), ebank(1), ACT.Copy).then_inc(xnt_sb, 1)

        def gdn_pe(pe, g, nxt, prep):
            c = 2 * NBATCH + g
            for p in range(NK // 2):
                pair = (2 * p, 2 * p + 1)
                more = p < NK // 2 - 1 or nxt
                q0, q1 = 2 * p + 2, 2 * p + 3
                if p == NK // 2 - 1 and (nxt or prep):
                    pe.wait_ge(xf_done, NK * g + 2 * p)
                    prep_turn(pe, c + 1)
                    if nxt:
                        gates_pe_ba(pe, g + 1)
                for n in pair:
                    x_pe(pe, NK * g + n, n, 0)
                for lv in range(1, LEVELS):
                    if more and lv == 1:
                        project_pe(pe, NK * g + q0, q0, g + 2)
                    if more and lv == 3:
                        turn_pe(pe, NK * g + q0, q0)
                    if more and lv == 4:
                        turn_back_pe(pe, NK * g + q0, q0)
                    if more and lv == 5:
                        project_pe(pe, NK * g + q1, q1, g + 2)
                    for n in pair:
                        nx_pe(pe, NK * g + n, n, lv)
                    for n in pair:
                        yuy_pe(pe, NK * g + n, n, lv)
                    if lv == 3 and p == NK // 2 - 1 and nxt:
                        gates_pe_rest(pe, g + 1)
                    if more and lv == 4:
                        products_pe(pe, NK * g + q0, q0, g + 2)
                    if lv < LEVELS - 1:
                        for n in pair:
                            x_pe(pe, NK * g + n, n, lv)
                if more:
                    turn_pe(pe, NK * g + q1, q1)
                    turn_back_pe(pe, NK * g + q1, q1)
                    products_pe(pe, NK * g + q1, q1, g + 2)
                for n in pair:
                    walk_pe(pe, NK * g + n, n, c, None if more else NK * (g + 1), c + 2 if (not more and prep) else None)

        def gdn_dve(dve, steps, g, i, nxt, prep):
            c = 2 * NBATCH + g
            for p in range(NK // 2):
                pair = (2 * p, 2 * p + 1)
                more = p < NK // 2 - 1 or nxt
                q0, q1 = 2 * p + 2, 2 * p + 3
                if p == NK // 2 - 2 and prep is not None:
                    prep_norm(dve, steps, c + 1, prep)
                if p == NK // 2 - 1 and nxt:
                    gates_dve_ba(dve, g + 1)
                for lv in range(1, LEVELS):
                    if more and lv in (1, 2):
                        conv_dve(dve, steps, NK * g + q0, q0, lv - 1)
                    if more and lv in (5, 6):
                        conv_dve(dve, steps, NK * g + q1, q1, lv - 5)
                    if lv == 3 and p == NK // 2 - 1 and nxt:
                        gates_dve(dve, steps, g + 1)
                    for n in pair:
                        merge_dve(dve, NK * g + n, n, lv)
                    if more and lv == 3:
                        norm_dve(dve, NK * g + q0, q0)
                    if more and lv == 4:
                        decay_dve(dve, NK * g + q0, q0, g + 2)
                if more:
                    norm_dve(dve, NK * g + q1, q1)
                    decay_dve(dve, NK * g + q1, q1, g + 2)
                for n in pair:
                    walk_dve(dve, steps, NK * g + n, n)
            dve.wait_ge(acc_done, NK * g + NK)
            xs = x[:, bass.ds(2 * i, TT), :]
            nc.vector.tensor_tensor(xs, bank(ACC, "p (t n) -> p t n", t=TT), xs, ALU.add).then_inc(x_done, 1)
            if nxt:
                gates_move(dve, g + 1)

        def gdn_act(act, g, nxt, prep):
            c = 2 * NBATCH + g
            for p in range(NK // 2):
                pair = (2 * p, 2 * p + 1)
                more = p < NK // 2 - 1 or nxt
                q0, q1 = 2 * p + 2, 2 * p + 3
                if p == NK // 2 - 1 and (nxt or prep):
                    prep_copy(act, c + 1)
                for n in pair:
                    x_act(act, NK * g + n, n, 0)
                for lv in range(1, LEVELS):
                    if more and lv == 1:
                        taps_act(act, NK * g + q0, q0)
                    if more and lv == 2:
                        z_act(act, NK * g + q0, q0)
                    if lv == 3 and p == NK // 2 - 1 and nxt:
                        gates_act(act, g + 1)
                    if more and lv == 3:
                        silu_act(act, NK * g + q0, q0)
                    if more and lv == 4:
                        turn_back_act(act, NK * g + q0, q0)
                    if more and lv == 5:
                        taps_act(act, NK * g + q1, q1)
                    if more and lv == 6:
                        z_act(act, NK * g + q1, q1)
                    for n in pair:
                        nx_act(act, NK * g + n, n, lv)
                    if more and lv == 3:
                        squares_act(act, NK * g + q0, q0)
                    if lv == 3 and p == NK // 2 - 1 and nxt:
                        gates_act_rest(act, g + 1)
                    if lv < LEVELS - 1:
                        for n in pair:
                            x_act(act, NK * g + n, n, lv)
                if more:
                    silu_act(act, NK * g + q1, q1)
                    squares_act(act, NK * g + q1, q1)
                    turn_back_act(act, NK * g + q1, q1)
                for n in pair:
                    walk_act(act, NK * g + n, n)

        def gdn_pool(pool, psteps, g, nxt):
            for p in range(NK // 2):
                if p < NK // 2 - 1 or nxt:
                    for n in (2 * p + 2, 2 * p + 3):
                        norm_pool(pool, psteps, NK * g + n, n)
                        first_pool(pool, NK * g + n, n)
                for n in (2 * p, 2 * p + 1):
                    walk_pool(pool, psteps, NK * g + n, n)

        def gdn_all_pe(pe):
            pe.wait_ge(x_done, 2 * NBATCH)
            pe.wait_ge(w_gdn, 4 * 16)
            pe.wait_ge(wout_scaled, 1)
            gates_pe_ba(pe, 0)
            project_pe(pe, 0, 0, 1)
            gates_pe_rest(pe, 0)
            for n in range(2):
                if n:
                    project_pe(pe, n, n, 1)
                turn_pe(pe, n, n)
                turn_back_pe(pe, n, n)
                products_pe(pe, n, n, 1)
            gdn_pe(pe, 0, True, True)
            with pe.Fori(1, NBATCH - 1) as g:
                gdn_pe(pe, g, True, True)
            gdn_pe(pe, NBATCH - 1, False, stages > 3)

        def gdn_all_dve(dve, steps):
            dve.wait_ge(x_done, 2 * NBATCH)
            gates_dve_ba(dve, 0)
            gates_dve(dve, steps, 0)
            gates_move(dve, 0)
            for n in range(2):
                conv_dve(dve, steps, n, n, 0)
                conv_dve(dve, steps, n, n, 1)
                norm_dve(dve, n, n)
                decay_dve(dve, n, n, 1)
            base = steps.base + steps.n
            steps.turn(base)
            gdn_dve(dve, steps, 0, 0, True, 1)
            assert steps.n == STEPS_GDN, steps.n
            with dve.Fori(1, NBATCH - 1) as g:
                steps.turn(base + STEPS_GDN * g)
                gdn_dve(dve, steps, g, g, True, g + 1)
            steps.turn(base + STEPS_GDN * (NBATCH - 1))
            gdn_dve(dve, steps, NBATCH - 1, NBATCH - 1, False, 0 if stages > 3 else None)

        def gdn_all_act(act):
            act.wait_ge(x_done, 2 * NBATCH)
            act.wait_ge(w_gdn, 4 * 16)
            gates_act(act, 0)
            gates_act_first(act)
            for n in range(2):
                if n:
                    taps_act(act, n, n)
                    z_act(act, n, n)
                silu_act(act, n, n)
                squares_act(act, n, n)
                turn_back_act(act, n, n)
            gdn_act(act, 0, True, True)
            with act.Fori(1, NBATCH - 1) as g:
                gdn_act(act, g, True, True)
            gdn_act(act, NBATCH - 1, False, stages > 3)

        def gates_act_first(act):
            z_act(act, 0, 0)
            gates_act_rest(act, 0)
            taps_act(act, 0, 0)

        def gdn_all_pool(pool):
            psteps = Steps(pool, pstep, pool_waits)
            for n in range(2):
                norm_pool(pool, psteps, n, n)
                first_pool(pool, n, n)
            base = psteps.n
            psteps.turn(base)
            gdn_pool(pool, psteps, 0, True)
            assert psteps.n == STEPS_POOL, psteps.n
            with pool.Fori(1, NBATCH - 1) as g:
                psteps.turn(base + STEPS_POOL * g)
                gdn_pool(pool, psteps, g, True)
            psteps.turn(base + STEPS_POOL * (NBATCH - 1))
            gdn_pool(pool, psteps, NBATCH - 1, False)

        @block.gpsimd
        def _(pool):
            pool.wait_ge(w_attn, 8 * 16)
            pool.wait_ge(x_in, 32)

            def add_bo(i):
                pool.wait_ge(normed, i + 1)
                for t in range(TT):
                    ins = nc.gpsimd.tensor_tensor(x[:, 2 * i + t, :], x[:, 2 * i + t, :], bo, ALU.add)
                ins.then_inc(xb_done, 1)
            with pool.Fori(0, NBATCH) as i:
                add_bo(i)
            pool.wait_ge(w_gdn, 4 * 16)
            pool.wait_ge(consts, 1)
            pool.wait_ge(c_in, 8 * 16)
            nc.gpsimd.tensor_scalar(wout[:, :, :], wout[:, :, :], normw[:, 0:1], -float(P) ** 0.5, ALU.mult, ALU.mult)\
                .then_inc(wout_scaled, 1)
            if stages > 2:
                gdn_all_pool(pool)

        ffn_layers = [(1, 0)] + ([(3, 1)] if stages > 3 else [])

        @block.tensor
        def _(pe):
            pe.wait_ge(consts, 1)
            pe.wait_ge(w_attn, 8 * 16)
            prep_turn(pe, 0)
            attn_pe(pe, 0, True)
            with pe.Fori(1, NBATCH - 1) as i:
                attn_pe(pe, i, True)
            attn_pe(pe, NBATCH - 1, True if stages > 1 else None)
            for layer, rep in ffn_layers:
                if layer >= stages:
                    break
                if layer == 3:
                    gdn_all_pe(pe)
                pe.wait_ge(x_done, layer * NBATCH)
                pe.wait_ge(*((w_ffn, 4 * 16) if rep == 0 else (w_ffn2, 3 * 16)))
                ffn_pe(pe, layer * NBATCH, rep * NBATCH, ffnw[rep], True)
                with pe.Fori(1, NBATCH - 1) as i:
                    ffn_pe(pe, layer * NBATCH + i, rep * NBATCH + i, ffnw[rep], True)
                ffn_pe(pe, layer * NBATCH + 7, rep * NBATCH + 7, ffnw[rep], True if layer + 1 < stages else None)
            if stages == 3:
                gdn_all_pe(pe)

        @block.vector
        def _(dve):
            steps = Steps(dve, vstep)
            nc.vector.memset(parts[:, :, :], 0.0)
            dve.wait_ge(c_in, 8 * 16)
            nc.vector.tensor_copy(identb[:, :], ident[:, :])
            nc.vector.tensor_copy(merge0[:, :], merge[:, 0, :])
            nc.vector.tensor_copy(selF[:, :, :], pick[:, 0:NE].unsqueeze(2).to_broadcast([96, NE, HID]))
            nc.vector.tensor_copy(selG[:, :, :], pick[:, 0:NV].unsqueeze(2).to_broadcast([96, NV, P])).then_inc(consts, 1)
            dve.wait_ge(astep, 1)
            steps.link(nc.vector.tensor_scalar(negA[:, :], negA[:, :], -1.0, None, ALU.mult))
            dve.wait_ge(x_in, 32)
            dve.wait_ge(w_attn, 8 * 16)
            prep_norm(dve, steps, 0, 0)
            start = steps.n
            steps.turn(start)
            attn_dve(dve, steps, 0, 0, 1)
            with dve.Fori(1, NBATCH - 1) as i:
                steps.turn(start + STEPS_ATTN * i)
                attn_dve(dve, steps, i, i, i + 1)
            assert steps.n == STEPS_ATTN, steps.n
            steps.turn(start + STEPS_ATTN * (NBATCH - 1))
            attn_dve(dve, steps, NBATCH - 1, NBATCH - 1, 0 if stages > 1 else None)
            for layer, rep in ffn_layers:
                if layer >= stages:
                    break
                if layer == 3:
                    gdn_all_dve(dve, steps)
                start = steps.base + steps.n
                dve.wait_ge(x_done, layer * NBATCH)
                steps.turn(start)
                ffn_dve(dve, steps, layer * NBATCH, rep * NBATCH, 0, 1)
                with dve.Fori(1, NBATCH - 1) as i:
                    steps.turn(start + STEPS_FFN * i)
                    ffn_dve(dve, steps, layer * NBATCH + i, rep * NBATCH + i, i, i + 1)
                assert steps.n == STEPS_FFN, steps.n
                steps.turn(start + STEPS_FFN * (NBATCH - 1))
                ffn_dve(dve, steps, layer * NBATCH + 7, rep * NBATCH + 7, 7, 0 if layer + 1 < stages else None)
            if stages == 3:
                gdn_all_dve(dve, steps)

        @block.scalar
        def _(act):
            act.wait_ge(c_in, 8 * 16)
            nc.scalar.activation(negA[:, :], negA[:, :], ACT.Exp).then_inc(astep, 1)
            act.wait_ge(w_attn, 8 * 16)
            prep_copy(act, 0)
            attn_act(act, 0, True)
            with act.Fori(1, NBATCH - 1) as i:
                attn_act(act, i, True)
            attn_act(act, NBATCH - 1, True if stages > 1 else None)
            for layer, rep in ffn_layers:
                if layer >= stages:
                    break
                if layer == 3:
                    gdn_all_act(act)
                act.wait_ge(x_done, layer * NBATCH)
                ffn_act(act, layer * NBATCH, rep * NBATCH, True)
                with act.Fori(1, NBATCH - 1) as i:
                    ffn_act(act, layer * NBATCH + i, rep * NBATCH + i, True)
                ffn_act(act, layer * NBATCH + 7, rep * NBATCH + 7, True if layer + 1 < stages else None)
            if stages == 3:
                gdn_all_act(act)


def consts():
    p = np.arange(P)
    upto = (p[:, None] <= p[None, :]).astype(np.float32)
    merge = np.zeros((P, LEVELS, P), np.int32)
    for lv in range(LEVELS):
        b = 1 << lv
        same = p[:, None] // (2 * b) == p[None, :] // (2 * b)
        merge[:, lv, :] = same & ((p[:, None] // b) % 2 == 0) & ((p[None, :] // b) % 2 == 1)
    pick = (np.arange(96)[:, None] % 32 == np.arange(16)[None, :]).astype(np.float32)
    desc = np.ascontiguousarray(np.broadcast_to(np.arange(E, 0, -1, dtype=np.float32), (P, TT, E)))
    return {"ident": np.eye(P, dtype=np.float32), "upto": upto, "merge": merge, "pick": pick, "desc": desc}


def laid_out(inp):
    def g(n):
        return np.asarray(inp[n])

    def by_rows(w):
        return np.ascontiguousarray(w.reshape(KD, P, -1).transpose(1, 0, 2))

    def padded(w):
        out = np.zeros((w.shape[0], HEADS, HP), w.dtype)
        out[:, :, :HD] = w.reshape(-1, HEADS, HD)
        return out.reshape(w.shape[0], HEADS * HP)

    def spread(v):
        return np.ascontiguousarray(np.broadcast_to(v, (P, v.shape[-1])))

    a = "L0_attn_a_"
    b = "L0_attn_b_"
    f = "L0_ffn_"
    r = {"x": np.ascontiguousarray(g(a + "x").reshape(NBATCH * T, D))}
    r["wq"], r["wk"] = by_rows(padded(g(a + "Wq").T)), by_rows(padded(g(a + "Wk").T))
    r["wv"], r["wo"] = by_rows(g(a + "Wv").T), by_rows(g(a + "Wo").T)
    for n in ("bq", "bk"):
        r[n] = np.ascontiguousarray(padded(g(a + n)[None, :]).reshape(QB, P).T)
    r["bv"], r["bo"] = spread(g(a + "bv")), spread(g(a + "bo"))
    for n, ew, sw in (("wg", "w_gate", "shw_gate"), ("wu", "w_up", "shw_up")):
        r[n] = by_rows(np.concatenate([g(f + ew).transpose(1, 0, 2).reshape(D, E * HID), g(f + sw)], 1))
    wd = np.zeros((NB * P, D), np.float32)
    wd[:E * HID] = g(f + "w_down").reshape(E * HID, D)
    wd[E * HID:FH] = g(f + "shw_down")
    r["wd"] = np.ascontiguousarray(wd.reshape(NB, P, D).transpose(1, 0, 2))
    r["wr"] = by_rows(np.concatenate([g(f + "gate_w"), g(f + "shgate_w")[None]], 0).T)
    r["wz"] = by_rows(g(b + "w_qkvz").T)
    ba = g(b + "w_ba").reshape(NK, 2, R, D).transpose(1, 0, 2, 3).reshape(2 * NV, D)
    r["wba"] = by_rows(ba.T)
    r["wout"] = np.ascontiguousarray(g(b + "w_out").T.reshape(NV, P, D).transpose(1, 0, 2))
    cw = g(b + "conv_w")
    r["convw"] = np.ascontiguousarray(np.concatenate([
        cw[:NK * P].reshape(NK, 1, P, TAPS), cw[NK * P:2 * NK * P].reshape(NK, 1, P, TAPS),
        cw[2 * NK * P:].reshape(NK, R, P, TAPS)], 1).transpose(2, 0, 1, 3))
    r["dt_bias"], r["A_log"] = spread(g(b + "dt_bias")), spread(g(b + "A_log"))
    r["normw"] = np.ascontiguousarray(g(b + "norm_weight")[:, None])
    r.update(consts())
    return r


def kernel(**inputs):
    import concourse.bacc as bacc
    from concourse.bass_utils import run_bass_kernel_spmd as run

    nc = bacc.Bacc("TRN2", target_bir_lowering=False, num_devices=1)
    arrays, io = {}, {}
    for name, a in laid_out(inputs).items():
        arrays[f"in_{name}"] = a
        io[name] = nc.dram_tensor(f"in_{name}", a.shape, mybir.dt.from_np(a.dtype), kind="ExternalInput").ap()
    io["out"] = nc.dram_tensor("out", (NBATCH * T, D), F32, kind="ExternalOutput").ap()
    build(nc, io)
    r = run(nc, [arrays], core_ids=[0])
    return r.results[0]["out"].reshape(NBATCH, T, D)
```

```python
from contextlib import ExitStack

import numpy as np

import concourse.bass as bass
from concourse import mybir
from concourse.alu_op_type import AluOpType as ALU

F32 = mybir.dt.float32
BF16 = mybir.dt.bfloat16
I32 = mybir.dt.int32
ACT = mybir.ActivationFunctionType
AX = mybir.AxisListType

P = 128
NBATCH = 8
T = 256
D = 256
KD = D // P
TT = T // P
NTILE = NBATCH * TT
LN_EPS = 1e-5

HEADS, HD = 16, 16
HP = 32
QB = HEADS * HP // P
SM_SCALE = 0.5

E, HID, HSH = 8, 176, 352
NE = E + HSH // HID
FH = NE * HID
NB = -(-FH // P)
BLK = [min(P, FH - P * j) for j in range(NB)]

NK, R, NV = 8, 2, 16
GROUP = 2 + 2 * R
TAPS = 4
L2_EPS = 1e-6
NORM_EPS = 1e-6
LEVELS = 7
MID = LEVELS - 1

STEPS_ATTN, STEPS_FFN, STEPS_GDN, STEPS_POOL = 18, 36, 75, 168


class Steps:

    def __init__(self, eng, sem):
        self.eng, self.sem, self.base, self.n = eng, sem, 0, 0

    def link(self, ins):
        self.n += 1
        ins.then_inc(self.sem, 1)
        self.eng.wait_ge(self.sem, self.base + self.n)

    def turn(self, base):
        self.base, self.n = base, 0


def build(nc, io, stages=4):
    ctx = ExitStack()
    with ctx:
        def sb(name, shape, dt=F32):
            return ctx.enter_context(nc.sbuf_tensor(name, shape, dt))

        def sem(name):
            return ctx.enter_context(nc.semaphore(name))

        x = sb("x", [P, NTILE, D])
        xT = sb("xT", [P, KD, T])
        xn = sb("xn", [P, TT, D])
        stats = sb("stats", [P, TT, 6])
        mean = sb("mean", [P, TT, 1])
        varp, newt, rstd = sb("varp", [P, TT, 1]), sb("newt", [P, TT, 1]), sb("rstd", [P, TT, 1])
        ident = sb("ident", [P, P])
        identb = sb("identb", [P, P], BF16)
        upto = sb("upto", [P, P])
        merge = sb("merge", [P, LEVELS, P], I32)
        carried = sb("carried", [P, 4])
        onehalf = sb("onehalf", [P, 8])
        eps_qk, eps_x = sb("eps_qk", [P, 4]), sb("eps_x", [P, 8])
        scale_qk = sb("scale_qk", [P, 4])
        merge0 = sb("merge0", [P, P])
        pick = sb("pick", [96, 16])
        selF = sb("selF", [96, NE, HID], BF16)
        selG = sb("selG", [96, NV, P], BF16)
        desc = sb("desc", [P, TT, E])
        parts = sb("parts", [P, TT, 96], BF16)
        partsT = sb("partsT", [96, T], BF16)
        wout = sb("wout", [P, NV, D])
        wba = sb("wba", [P, KD, 2 * NV])
        convw = sb("convw", [P, NK, 4, TAPS])
        dtb = sb("dtb", [P, NV])
        negA = sb("negA", [P, NV])
        normw = sb("normw", [P, 1])
        big = sb("big", [P, KD * NK * GROUP * P])
        small = sb("small", [P, 1280])
        ARENA = 24640
        arena = sb("arena", [P, ARENA])

        used = {"arena": 0, "small": 0}

        def carve(n, where="arena"):
            a = used[where]
            used[where] = a + n
            t = arena if where == "arena" else small
            assert used[where] <= (ARENA if where == "arena" else 1280), used
            return t[:, a:a + n]

        def view(ap, pattern, **k):
            return ap.rearrange(pattern, **k)

        NW = KD * FH

        def ffn_weights(t):
            return (view(t[:, 0:NW], "p (k n) -> p k n", k=KD), view(t[:, NW:2 * NW], "p (k n) -> p k n", k=KD),
                    view(t[:, 2 * NW:2 * NW + NB * D], "p (j n) -> p j n", j=NB))
        wr = sb("wr", [P, KD, E + 1])
        ffnw = [ffn_weights(carve(2 * NW + NB * D)), ffn_weights(big)]
        wq = view(carve(KD * QB * P), "p (k n) -> p k n", k=KD)
        wk = view(carve(KD * QB * P), "p (k n) -> p k n", k=KD)
        wv = view(carve(KD * D), "p (k n) -> p k n", k=KD)
        wo = view(carve(KD * D), "p (k n) -> p k n", k=KD)
        bq, bk = carve(QB), carve(QB)
        bv, bo = carve(D), carve(D)
        after_attn_weights = used["arena"]
        qT = view(carve(QB * T), "p (b n) -> p b n", b=QB)
        kT = view(carve(QB * T), "p (b n) -> p b n", b=QB)
        v = view(carve(TT * D), "p (t n) -> p t n", t=TT)
        probs = view(carve(2 * TT * T), "p (s t n) -> p s t n", s=2, t=TT)
        probsT = view(carve(2 * TT * T), "p (s t n) -> p s t n", s=2, t=TT)
        o = view(carve(TT * D), "p (t n) -> p t n", t=TT)
        oT = view(carve(KD * T), "p (k n) -> p k n", k=KD)
        negmax = sb("negmax", [P, 2, TT])
        sums = sb("sums", [P, TT, HEADS])
        rsums = sb("rsums", [P, TT, HEADS])
        used["arena"] = after_attn_weights
        gact = view(carve(2 * T), "p (s n) -> p s n", s=2)
        hid = view(carve(2 * T), "p (s n) -> p s n", s=2)
        hidT = view(carve(2 * T), "p (s n) -> p s n", s=2)
        used["arena"] = 0
        yc = view(carve(4 * T), "p (b n) -> p b n", b=4)
        sq = carve(4 * P)
        qkn = view(carve(4 * 4 * P), "p (s m n) -> p s m n", s=4, m=4)
        vt = view(carve(4 * 4 * P), "p (s m n) -> p s m n", s=4, m=4)
        kqT = view(carve(4 * 4 * P), "p (s c m n) -> p s c m n", s=4, c=2, m=2)
        UP = view(carve(4 * 8 * P), "p (s m a n) -> p s m a n", s=4, m=4, a=2)
        sz = view(carve(4 * 4 * P), "p (s m n) -> p s m n", s=4, m=4)
        DT = view(carve(4 * P), "p (m n) -> p m n", m=4)
        dlast = view(carve(4 * 4), "p (s m) -> p s m", s=4)
        Y = view(carve(4 * 4 * P), "p (s m n) -> p s m n", s=4, m=4)
        X = view(carve(2 * 4 * P), "p (s m n) -> p s m n", s=2, m=4)
        NX = view(carve(2 * 4 * P), "p (s m n) -> p s m n", s=2, m=4)
        w01 = view(carve(8 * P), "p (s c r n) -> p s c r n", s=2, c=TT, r=R)
        w0s = view(carve(4 * P), "p (s r n) -> p s r n", s=2, r=R)
        st = view(carve(4 * P), "p (s n) -> p s n", s=2)
        rhs1 = view(carve(4 * P), "p (s r n) -> p s r n", s=2, r=R)
        qst = view(carve(4 * P), "p (s r n) -> p s r n", s=2, r=R)
        xf = view(carve(8 * P), "p (s c r n) -> p s c r n", s=2, c=TT, r=R)
        xfn = view(carve(8 * P), "p (s c r n) -> p s c r n", s=2, c=TT, r=R)
        xnT = view(carve(4 * T), "p (s r n) -> p s r n", s=2, r=R)

        def tiny(*shape):
            n = int(np.prod(shape))
            ap = carve(n, "small")
            return view(ap, "p (a b) -> p a b", a=shape[0]) if len(shape) == 2 else ap

        wz = view(big[:, :], "p (k n) -> p k n", k=KD)

        banks = [ctx.enter_context(nc.psum_tensor(f"bank{n}", [P, 512], F32)) for n in range(8)]

        def bank(n, pattern=None, **k):
            return banks[n][:, :] if pattern is None else banks[n][:, :].rearrange(pattern, **k)

        x_in, w_attn, w_ffn, w_ffn2, w_gdn, c_in = (sem(n) for n in ("x_in", "w_attn", "w_ffn", "w_ffn2", "w_gdn", "c_in"))
        consts, out_done = sem("consts"), sem("out_done")
        vstep, astep = sem("vstep"), sem("astep")
        normed, xt_ps, xt_ready, x_done = (sem(n) for n in ("normed", "xt_ps", "xt_ready", "x_done"))
        q_ps, k_ps, v_ps, q_sb, k_sb, v_sb = (sem(n) for n in ("q_ps", "k_ps", "v_ps", "q_sb", "k_sb", "v_sb"))
        s_ps, mx_done, exp_done, pt_ps, pt_sb, pv_done = (sem(n) for n in ("s_ps", "mx_done", "exp_done", "pt_ps", "pt_sb", "pv_done"))
        o_sb, ot_ps, ot_sb, out_ps, xb_done = (sem(n) for n in ("o_sb", "ot_ps", "ot_sb", "out_ps", "xb_done"))
        rt_ps, gap_done, th_done, parts_done, ct_ps, ct_sb = (sem(n) for n in ("rt_ps", "gap_done", "th_done", "parts_done", "ct_ps", "ct_sb"))
        gu_ps, gact_done, h_done, cb_ps, ht_done, dn_done = (sem(n) for n in ("gu_ps", "gact_done", "h_done", "cb_ps", "ht_done", "dn_done"))
        ba_ps, ba_sb, g_to_act, g_to_dve, g_done, gc_ps, eg_done = (sem(n) for n in ("ba_ps", "ba_sb", "g_to_act", "g_to_dve", "g_done", "gc_ps", "eg_done"))
        gparts_done, at_ps, at_sb, nbeta_done = (sem(n) for n in ("gparts_done", "at_ps", "at_sb", "nbeta_done"))
        qk_ps, vp_ps, z_ps, tap_qk, tap_v, conv_qk, conv_v, yc_done, z_sb = (
            sem(n) for n in ("qk_ps", "vp_ps", "z_ps", "tap_qk", "tap_v", "conv_qk", "conv_v", "yc_done", "z_sb"))
        qkt_ps, vt_ps, sq_done, vt_sb, qkn_done, kq_ps, kq_sb, kk_ps, ab_ps, dt_done, up_done = (
            sem(n) for n in ("qkt_ps", "vt_ps", "sq_done", "vt_sb", "qkn_done", "kq_ps", "kq_sb", "kk_ps", "ab_ps", "dt_done", "up_done"))
        y_pre, y_done, xx_ps, xx_sb, nx_ps, nx_sb, yuy_ps = (
            sem(n) for n in ("y_pre", "y_done", "xx_ps", "xx_sb", "nx_ps", "nx_sb", "yuy_ps"))
        y_first = sem("y_first")
        w0_ps, w0_sb, st_ps, st_sb, ks_ps, r_done, w1_ps, w1_sb, og_ps, xf_done, sqx_done, xfn_done, xnt_ps, xnt_sb, acc_done = (
            sem(n) for n in ("w0_ps", "w0_sb", "st_ps", "st_sb", "ks_ps", "r_done", "w1_ps", "w1_sb", "og_ps", "xf_done",
                             "sqx_done", "xfn_done", "xnt_ps", "xnt_sb", "acc_done"))

        ssq_done, rn_done, ssx_done, rx_done, pstep, gmove_done, wout_scaled = (
            sem(n) for n in ("ssq_done", "rn_done", "ssx_done", "rx_done", "pstep", "gmove_done", "wout_scaled"))
        qs_ps, qst_done, pconsts = (sem(n) for n in ("qs_ps", "qst_done", "pconsts"))

        def at_least(eng, s, value):
            if not isinstance(value, int) or value > 0:
                eng.wait_ge(s, value)

        XT_BANK = 7
        E0, E1, E2, ACC = 7, 6, 5, 4

        block = ctx.enter_context(nc.Block())

        @block.sync
        def _(sp):
            xin = io["x"].rearrange("(n p) d -> p n d", p=P)
            sp.dma_start(x[:, 0:TT, :], xin[:, 0:TT, :]).then_inc(x_in, 16)
            for name, dst in (("ident", ident[:, :]), ("upto", upto[:, :]), ("merge", merge[:, :, :]), ("pick", pick[:, :]),
                              ("desc", desc[:, :, :]), ("normw", normw[:, :]), ("A_log", negA[:, :]), ("dt_bias", dtb[:, :])):
                sp.dma_start(dst, io[name]).then_inc(c_in, 16)
            for name, dst in (("wq", wq), ("wk", wk), ("wv", wv), ("bq", bq), ("bk", bk), ("bv", bv), ("bo", bo), ("wo", wo)):
                sp.dma_start(dst, io[name]).then_inc(w_attn, 16)
            sp.dma_start(x[:, TT:, :], xin[:, TT:, :]).then_inc(x_in, 16)
            for name, dst in (("wg", ffnw[0][0]), ("wu", ffnw[0][1]), ("wd", ffnw[0][2]), ("wr", wr[:, :, :])):
                sp.dma_start(dst, io[name]).then_inc(w_ffn, 16)
            for name, dst in (("wout", wout[:, :, :]), ("wba", wba[:, :, :]), ("convw", convw[:, :, :, :]), ("wz", wz)):
                sp.dma_start(dst, io[name]).then_inc(w_gdn, 16)
            if stages > 3:
                sp.wait_ge(z_ps, NK * NBATCH)
                for name, dst in (("wg", ffnw[1][0]), ("wu", ffnw[1][1]), ("wd", ffnw[1][2])):
                    sp.dma_start(dst, io[name]).then_inc(w_ffn2, 16)
            out = io["out"].rearrange("(n p) d -> p n d", p=P)
            with sp.Fori(0, NBATCH) as i:
                sp.wait_ge(x_done, (stages - 1) * NBATCH + 1 + i)
                sp.dma_start(out[:, bass.ds(2 * i, TT), :], x[:, bass.ds(2 * i, TT), :]).then_inc(out_done, 16)
            sp.wait_ge(out_done, 16 * NBATCH)

        def pool_waits():
            nc.gpsimd.tensor_tensor(carried[:, 2:3], ident[:, 0:1], ident[:, 0:1], ALU.add)

        def rsqrt(steps, vec, y, val, t):
            steps.link(vec.tensor_scalar(y.bitcast(I32), val.bitcast(I32), -0.5, float(0x5F375A86), ALU.mult, ALU.add))
            for step in range(3):
                steps.link(vec.tensor_tensor(t, y, y, ALU.mult))
                steps.link(vec.tensor_tensor(t, t, val, ALU.mult))
                steps.link(vec.tensor_scalar(t, t, -0.5, 1.5, ALU.mult, ALU.add))
                steps.link(vec.tensor_tensor(y, y, t, ALU.mult))

        def rsqrt_pool(steps, y, half, eps, t):
            steps.link(nc.gpsimd.tensor_tensor(half, half, eps, ALU.add))
            pool_waits()
            steps.link(nc.gpsimd.tensor_scalar(y.bitcast(I32), half.bitcast(I32), -0.5, float(0x5F375A86 - (1 << 22)),
                                               ALU.mult, ALU.add))
            for step in range(3):
                steps.link(nc.gpsimd.tensor_tensor(t, y, y, ALU.mult))
                steps.link(nc.gpsimd.tensor_tensor(t, t, half, ALU.mult))
                steps.link(nc.gpsimd.tensor_tensor(t, onehalf[:, 0:t.shape[1]], t, ALU.subtract))
                if step < 2:
                    steps.link(nc.gpsimd.tensor_tensor(y, y, t, ALU.mult))

        def prep_norm(dve, steps, c, b):
            for t in range(TT):
                ins = nc.vector.bn_stats(stats[:, t, :], x[:, 2 * b + t, :])
            steps.link(ins)
            nc.vector.tensor_tensor(mean[:, :, :], stats[:, :, 1:2], stats[:, :, 4:5], ALU.add)
            nc.vector.tensor_tensor(newt[:, :, :], stats[:, :, 1:2], stats[:, :, 4:5], ALU.subtract)
            steps.link(nc.vector.tensor_tensor(varp[:, :, :], stats[:, :, 2:3], stats[:, :, 5:6], ALU.add))
            nc.vector.tensor_scalar(mean[:, :, :], mean[:, :, :], 0.5, None, ALU.mult)
            nc.vector.tensor_scalar(varp[:, :, :], varp[:, :, :], 1.0 / D, LN_EPS, ALU.mult, ALU.add)
            steps.link(nc.vector.scalar_tensor_tensor(newt[:, :, :], newt[:, :, :], 0.25, newt[:, :, :], ALU.mult, ALU.mult))
            steps.link(nc.vector.tensor_tensor(varp[:, :, :], varp[:, :, :], newt[:, :, :], ALU.add))
            rsqrt(steps, nc.vector, rstd[:, :, :], varp[:, :, :], newt[:, :, :])
            at_least(dve, xt_ps, c)
            for t in range(TT):
                ins = nc.vector.tensor_scalar(xn[:, t, :], x[:, 2 * b + t, :], mean[:, t, 0:1], rstd[:, t, 0:1],
                                              ALU.subtract, ALU.mult)
            ins.then_inc(normed, 1)

        def prep_turn(pe, c):
            pe.wait_ge(normed, c + 1)
            at_least(pe, xt_ready, c)
            b = bank(XT_BANK, "p (k n) -> p k n", k=KD)
            for t in range(TT):
                for k in range(KD):
                    ins = nc.tensor.transpose(b[:, k, t * P:(t + 1) * P], xn[:, t, k * P:(k + 1) * P], ident[:, :])
            ins.then_inc(xt_ps, 1)

        def prep_copy(act, c):
            act.wait_ge(xt_ps, c + 1)
            nc.scalar.activation(xT[:, :, :], bank(XT_BANK, "p (k n) -> p k n", k=KD), ACT.Copy).then_inc(xt_ready, 1)

        def split_parts(steps, src, rest, n):
            steps.link(nc.vector.tensor_copy(parts[:, :, 0:n], src))
            steps.link(nc.vector.tensor_tensor(rest, src, parts[:, :, 0:n], ALU.subtract))
            steps.link(nc.vector.tensor_copy(parts[:, :, 32:32 + n], rest))
            steps.link(nc.vector.tensor_tensor(rest, rest, parts[:, :, 32:32 + n], ALU.subtract))
            return nc.vector.tensor_copy(parts[:, :, 64:64 + n], rest)

        def turn_parts(pe, b):
            bb = banks[b][0:96, 0:T // 2].bitcast(BF16)
            for t in range(TT):
                ins = nc.tensor.transpose(bb[:, t * P:(t + 1) * P], parts[:, t, :], identb[:, :])
            return ins

        QBANK, KBANK, VBANK, SBANK, PBANK, OBANK, YBANK = (2, 3), (4, 5), 1, (2, 3), (4, 5), 6, 0

        def attn_pe(pe, a, nxt):
            pe.wait_ge(xt_ready, a + 1)
            for half, (w, bks, done) in enumerate(((wq, QBANK, q_ps), (wk, KBANK, k_ps))):
                for pair in range(2):
                    bb = bank(bks[pair], "p (b n) -> p b n", b=2)
                    for j in range(2):
                        blk = 2 * pair + j
                        for k in range(KD):
                            ins = nc.tensor.matmul(bb[:, j, :], w[:, k, blk * P:(blk + 1) * P], xT[:, k, :],
                                                   start=(k == 0), stop=(k == KD - 1))
                    ins.then_inc(done, 1)
            bb = bank(VBANK, "p (t n) -> p t n", t=TT)
            for t in range(TT):
                for k in range(KD):
                    ins = nc.tensor.matmul(bb[:, t, :], xT[:, k, t * P:(t + 1) * P], wv[:, k, :],
                                           start=(k == 0), stop=(k == KD - 1))
            ins.then_inc(v_ps, 1)

            def scores(h):
                if h == 0:
                    pe.wait_ge(q_sb, a + 1)
                    pe.wait_ge(k_sb, a + 1)
                if h >= 2:
                    pe.wait_ge(exp_done, HEADS * a + h - 1)
                r = HP * (h % 4)
                bb = bank(SBANK[h % 2], "p (t n) -> p t n", t=TT)
                for t in range(TT):
                    ins = nc.tensor.matmul(bb[:, t, :], qT[r:r + HD, h // 4, t * P:(t + 1) * P], kT[r:r + HD, h // 4, :],
                                           start=True, stop=True)
                ins.then_inc(s_ps, 1)

            def turn(h):
                pe.wait_ge(exp_done, HEADS * a + h + 1)
                if h >= 2:
                    pe.wait_ge(pt_sb, HEADS * a + h - 1)
                bb = bank(PBANK[h % 2], "p (t n) -> p t n", t=TT)
                for t in range(TT):
                    for kt in range(TT):
                        ins = nc.tensor.transpose(bb[:, kt, t * P:(t + 1) * P], probs[:, h % 2, t, kt * P:(kt + 1) * P],
                                                  ident[:, :])
                ins.then_inc(pt_ps, 1)

            def values(h):
                pe.wait_ge(pt_sb, HEADS * a + h + 1)
                if h == 0:
                    pe.wait_ge(v_sb, a + 1)
                    at_least(pe, o_sb, a)
                bb = bank(OBANK, "p (t n) -> p t n", t=TT)
                for t in range(TT):
                    for kt in range(TT):
                        ins = nc.tensor.matmul(bb[:, t, h * HD:(h + 1) * HD], probsT[:, h % 2, kt, t * P:(t + 1) * P],
                                               v[:, kt, h * HD:(h + 1) * HD], start=(kt == 0), stop=(kt == TT - 1))
                ins.then_inc(pv_done, 1)

            for s in range(HEADS + 2):
                if s < HEADS:
                    scores(s)
                if 1 <= s <= HEADS:
                    turn(s - 1)
                if s >= 2:
                    values(s - 2)
                if s == HEADS // 2 and nxt is not None:
                    prep_turn(pe, a + 1)
            pe.wait_ge(o_sb, a + 1)
            bb = bank(VBANK, "p (k n) -> p k n", k=KD)
            for t in range(TT):
                for k in range(KD):
                    ins = nc.tensor.transpose(bb[:, k, t * P:(t + 1) * P], o[:, t, k * P:(k + 1) * P], ident[:, :])
            ins.then_inc(ot_ps, 1)
            pe.wait_ge(ot_sb, a + 1)
            at_least(pe, x_done, a)
            bb = bank(YBANK, "p (t n) -> p t n", t=TT)
            for t in range(TT):
                for k in range(KD):
                    ins = nc.tensor.matmul(bb[:, t, :], oT[:, k, t * P:(t + 1) * P], wo[:, k, :],
                                           start=(k == 0), stop=(k == KD - 1))
            ins.then_inc(out_ps, 1)

        def attn_dve(dve, steps, a, i, nxt):
            for pair in range(2):
                dve.wait_ge(q_ps, 2 * a + pair + 1)
                bb = bank(QBANK[pair], "p (b n) -> p b n", b=2)
                for j in range(2):
                    blk = 2 * pair + j
                    ins = nc.vector.tensor_scalar(qT[:, blk, :], bb[:, j, :], bq[:, blk:blk + 1], SM_SCALE, ALU.add, ALU.mult)
            ins.then_inc(q_sb, 1)
            dve.wait_ge(v_ps, a + 1)
            nc.vector.tensor_tensor(v[:, :, :], bank(VBANK, "p (t n) -> p t n", t=TT),
                                    bv.unsqueeze(1).to_broadcast([P, TT, D]), ALU.add).then_inc(v_sb, 1)

            def top(h):
                dve.wait_ge(s_ps, HEADS * a + h + 1)
                nc.vector.tensor_reduce(negmax[:, h % 2, :], bank(SBANK[h % 2], "p (t n) -> p t n", t=TT), AX.X, ALU.max,
                                        negate=True).then_inc(mx_done, 1)

            def copy(h):
                dve.wait_ge(pt_ps, HEADS * a + h + 1)
                if h >= 2:
                    dve.wait_ge(pv_done, HEADS * a + h - 1)
                nc.vector.tensor_copy(probsT[:, h % 2, :, :], bank(PBANK[h % 2], "p (t n) -> p t n", t=TT)).then_inc(pt_sb, 1)

            for s in range(HEADS + 1):
                if s < HEADS:
                    top(s)
                if s >= 1:
                    copy(s - 1)
                if s == HEADS // 2 - 2 and nxt is not None:
                    prep_norm(dve, steps, a + 1, nxt)
            steps.link(nc.vector.reciprocal(rsums[:, :, :], sums[:, :, :]))
            dve.wait_ge(pv_done, HEADS * a + HEADS)
            hv = "p t (h e) -> p t h e"
            for t in range(TT):
                ob = bank(OBANK, "p (t h e) -> p t h e", t=TT, h=HEADS)
                ins = nc.vector.tensor_tensor(o[:, t, :].rearrange("p (h e) -> p h e", h=HEADS), ob[:, t, :, :],
                                              rsums[:, t, :].unsqueeze(2).to_broadcast([P, HEADS, HD]), ALU.mult)
            ins.then_inc(o_sb, 1)
            dve.wait_ge(out_ps, a + 1)
            dve.wait_ge(xb_done, a + 1)
            xs = x[:, bass.ds(2 * i, TT), :]
            nc.vector.tensor_tensor(xs, bank(YBANK, "p (t n) -> p t n", t=TT), xs, ALU.add).then_inc(x_done, 1)

        def attn_act(act, a, nxt):
            for pair in range(2):
                act.wait_ge(k_ps, 2 * a + pair + 1)
                bb = bank(KBANK[pair], "p (b n) -> p b n", b=2)
                for j in range(2):
                    blk = 2 * pair + j
                    ins = nc.scalar.activation(kT[:, blk, :], bb[:, j, :], ACT.Identity, bias=bk[:, blk:blk + 1])
            ins.then_inc(k_sb, 1)
            for h in range(HEADS):
                act.wait_ge(mx_done, HEADS * a + h + 1)
                if h >= 2:
                    act.wait_ge(pt_ps, HEADS * a + h - 1)
                bb = bank(SBANK[h % 2], "p (t n) -> p t n", t=TT)
                for t in range(TT):
                    ins = nc.scalar.activation(probs[:, h % 2, t, :], bb[:, t, :], ACT.Exp, bias=negmax[:, h % 2, t:t + 1],
                                               accum_out=sums[:, t, h:h + 1])
                ins.then_inc(exp_done, 1)
                if h == HEADS // 2 and nxt is not None:
                    prep_copy(act, a + 1)
            act.wait_ge(ot_ps, a + 1)
            nc.scalar.activation(oT[:, :, :], bank(VBANK, "p (k n) -> p k n", k=KD), ACT.Copy).then_inc(ot_sb, 1)

        GUB, CBB, DNB, RTB = (0, 1, 2), (3, 4), 5, 6

        def ffn_pe(pe, c, f, w, nxt):
            wg, wu, wd = w
            pe.wait_ge(xt_ready, c + 1)
            rt = banks[RTB][:, 0:TT * 16].rearrange("p (t n) -> p t n", t=TT)
            for t in range(TT):
                for k in range(KD):
                    ins = nc.tensor.matmul(rt[:, t, 0:E + 1], xT[:, k, t * P:(t + 1) * P], wr[:, k, :],
                                           start=(k == 0), stop=(k == KD - 1))
            ins.then_inc(rt_ps, 1)

            def gate_up(j):
                at_least(pe, h_done, NB * f + max(j - 2, 0))
                bb = bank(GUB[j % 3], "p (g n) -> p g n", g=2)
                m = BLK[j]
                for g, wt in enumerate((wg, wu)):
                    for k in range(KD):
                        ins = nc.tensor.matmul(bb[0:m, g, :], wt[:, k, j * P:j * P + m], xT[:, k, :],
                                               start=(k == 0), stop=(k == KD - 1))
                ins.then_inc(gu_ps, 1)

            def spread(j):
                at_least(pe, ht_done, NB * f + max(j - 1, 0))
                m = BLK[j]
                sel = selF[:, :, :].rearrange("p e n -> p (e n)")[:, j * P:j * P + m]
                nc.tensor.matmul(banks[CBB[j % 2]][0:m, 0:T], sel, partsT[:, :], start=True, stop=True).then_inc(cb_ps, 1)

            def down(j):
                pe.wait_ge(ht_done, NB * f + j + 1)
                if j == 0:
                    at_least(pe, x_done, c)
                bb = bank(DNB, "p (t n) -> p t n", t=TT)
                m = BLK[j]
                for t in range(TT):
                    ins = nc.tensor.matmul(bb[:, t, :], hidT[0:m, j % 2, t * P:(t + 1) * P], wd[0:m, j, :],
                                           start=(j == 0 and t == 0), stop=(j == NB - 1), skip_group_check=True)
                ins.then_inc(dn_done, 1)

            for s in range(NB + 3):
                if s < NB:
                    gate_up(s)
                if s == 2:
                    pe.wait_ge(parts_done, f + 1)
                    turn_parts(pe, RTB).then_inc(ct_ps, 1)
                    pe.wait_ge(ct_sb, f + 1)
                if 0 <= s - 2 < NB:
                    spread(s - 2)
                if s >= 3:
                    down(s - 3)
                if s == NB // 2 and nxt is not None:
                    prep_turn(pe, c + 1)

        def ffn_dve(dve, steps, c, f, i, nxt):
            lg, eq, oh1, oh2 = fl["lg"], fl["eq"], fl["oh1"], fl["oh2"]
            l8 = lg[:, :, 0:E]

            def first_max(m, src, oh):
                steps.link(nc.vector.tensor_reduce(m, src, AX.X, ALU.max))
                steps.link(nc.vector.tensor_tensor(eq, src, m.to_broadcast([P, TT, E]), ALU.is_equal))
                steps.link(nc.vector.tensor_tensor(eq, eq, desc[:, :, :], ALU.mult))
                steps.link(nc.vector.tensor_reduce(fl["mw"], eq, AX.X, ALU.max))
                steps.link(nc.vector.tensor_tensor(oh, eq, fl["mw"].to_broadcast([P, TT, E]), ALU.is_equal))

            dve.wait_ge(rt_ps, f + 1)
            rt = banks[RTB][:, 0:TT * 16].rearrange("p (t n) -> p t n", t=TT)
            steps.link(nc.vector.tensor_copy(lg[:, :, 0:E + 1], rt[:, :, 0:E + 1]))
            first_max(fl["m1"], l8, oh1)
            steps.link(nc.vector.scalar_tensor_tensor(fl["l2"], oh1, -1e30, l8, ALU.mult, ALU.add))
            first_max(fl["m2"], fl["l2"], oh2)
            nc.vector.tensor_copy(fl["gap"][:, :, 1:2], lg[:, :, E:E + 1])
            nc.vector.tensor_tensor(fl["gap"][:, :, 0:1], fl["m1"], fl["m2"], ALU.subtract).then_inc(gap_done, 1)
            dve.wait_ge(th_done, f + 1)
            nc.vector.tensor_scalar(fl["wt"][:, :, 0:2], fl["th"], 0.5, 0.5, ALU.mult, ALU.add)
            steps.link(nc.vector.tensor_scalar(fl["wt"][:, :, 2:3], fl["th"][:, :, 0:1], -0.5, 0.5, ALU.mult, ALU.add))
            wt = fl["wt"]
            cmb = fl["cmb"]
            nc.vector.tensor_copy(cmb[:, :, E:NE], wt[:, :, 1:2].to_broadcast([P, TT, NE - E]))
            nc.vector.tensor_tensor(oh1, oh1, wt[:, :, 0:1].to_broadcast([P, TT, E]), ALU.mult)
            steps.link(nc.vector.tensor_tensor(oh2, oh2, wt[:, :, 2:3].to_broadcast([P, TT, E]), ALU.mult))
            steps.link(nc.vector.tensor_tensor(cmb[:, :, 0:E], oh1, oh2, ALU.add))
            split_parts(steps, cmb, fl["rest"], NE).then_inc(parts_done, 1)

            def mul_up(j):
                dve.wait_ge(gact_done, NB * f + j + 1)
                at_least(dve, ht_done, NB * f + max(j - 1, 0))
                m = BLK[j]
                nc.vector.tensor_tensor(hid[0:m, j % 2, :], gact[0:m, j % 2, :], bank(GUB[j % 3])[0:m, T:2 * T], ALU.mult)\
                    .then_inc(h_done, 1)

            def weigh(j):
                dve.wait_ge(cb_ps, NB * f + j + 1)
                dve.wait_ge(h_done, NB * f + j + 1)
                at_least(dve, dn_done, NB * f + max(j - 1, 0))
                m = BLK[j]
                nc.vector.tensor_tensor(hidT[0:m, j % 2, :], hid[0:m, j % 2, :], banks[CBB[j % 2]][0:m, 0:T], ALU.mult)\
                    .then_inc(ht_done, 1)

            mul_up(0)
            for j in range(NB):
                if j + 1 < NB:
                    mul_up(j + 1)
                weigh(j)
                if j == NB // 2 - 2 and nxt is not None:
                    prep_norm(dve, steps, c + 1, nxt)
            dve.wait_ge(dn_done, NB * f + NB)
            xs = x[:, bass.ds(2 * i, TT), :]
            nc.vector.tensor_tensor(xs, bank(DNB, "p (t n) -> p t n", t=TT), xs, ALU.add).then_inc(x_done, 1)

        def ffn_act(act, c, f, nxt):
            act.wait_ge(gap_done, f + 1)
            nc.scalar.activation(fl["th"], fl["gap"], ACT.Tanh, scale=0.5).then_inc(th_done, 1)
            for j in range(NB):
                if j == 2:
                    act.wait_ge(ct_ps, f + 1)
                    nc.scalar.activation(partsT[:, :], banks[RTB][0:96, 0:T // 2].bitcast(BF16), ACT.Copy).then_inc(ct_sb, 1)
                act.wait_ge(gu_ps, NB * f + j + 1)
                at_least(act, h_done, NB * f + max(j - 1, 0))
                m = BLK[j]
                nc.scalar.activation(gact[0:m, j % 2, :], bank(GUB[j % 3])[0:m, 0:T], ACT.Silu).then_inc(gact_done, 1)
            if nxt is not None:
                prep_copy(act, c + 1)

        fl = {"lg": tiny(TT, 16), "eq": tiny(TT, E), "oh1": tiny(TT, E), "oh2": tiny(TT, E), "l2": tiny(TT, E),
              "m1": tiny(TT, 1), "m2": tiny(TT, 1), "mw": tiny(TT, 1), "gap": tiny(TT, 2), "th": tiny(TT, 2),
              "wt": tiny(TT, 4), "cmb": tiny(TT, NE), "rest": tiny(TT, NE)}

        HALF = 0.5 ** 0.5
        gt = {n: tiny(TT, NV) for n in ("ad", "neg", "th", "e", "u", "ln", "d", "z", "r", "g", "rest", "alpha")}
        ba = tiny(TT, 2 * NV)
        nbeta, nbeta_walk = tiny(TT, NV), tiny(TT, NV)
        eG, eG_walk = tiny(NV), tiny(NV)
        ssq, rn, rtmp = tiny(4), tiny(4), tiny(4)
        ssx, rx, rxt, bd = tiny(8), tiny(8), tiny(8), tiny(4)

        def ebank(e, pattern=None, **k):
            return bank((E0, E1, E2)[e], pattern, **k)

        def mm4(b, m, n):
            return bank(b, "p (m n) -> p m n", m=4)[:, m, :]

        def gates_pe_ba(pe, g):
            pe.wait_ge(xt_ready, 2 * NBATCH + g + 1)
            at_least(pe, up_done, NK * g)
            b = ebank(1)[:, 0:TT * 2 * NV].rearrange("p (t n) -> p t n", t=TT)
            for t in range(TT):
                for k in range(KD):
                    ins = nc.tensor.matmul(b[:, t, :], xT[:, k, t * P:(t + 1) * P], wba[:, k, :],
                                           start=(k == 0), stop=(k == KD - 1))
            ins.then_inc(ba_ps, 1)

        def gates_dve_ba(dve, g):
            dve.wait_ge(ba_ps, g + 1)
            nc.vector.tensor_copy(ba, ebank(1)[:, 0:TT * 2 * NV].rearrange("p (t n) -> p t n", t=TT)).then_inc(ba_sb, 1)

        def gates_dve(dve, steps, g):
            dve.wait_ge(ba_sb, g + 1)
            steps.link(nc.vector.tensor_tensor(gt["ad"], ba[:, :, NV:], dtb[:, :].unsqueeze(1).to_broadcast([P, TT, NV]), ALU.add))
            steps.link(nc.vector.tensor_scalar(gt["neg"], gt["ad"], -1.0, None, ALU.mult))
            nc.vector.tensor_tensor(gt["neg"], gt["neg"], gt["ad"], ALU.min).then_inc(g_to_act, 1)
            dve.wait_ge(g_to_dve, 3 * g + 1)
            nc.vector.tensor_scalar(gt["u"], gt["e"], 1.0, None, ALU.add).then_inc(g_to_act, 1)
            dve.wait_ge(g_to_act, 2 * g + 2)
            steps.link(nc.vector.tensor_scalar(gt["d"], gt["u"], -1.0, None, ALU.add))
            steps.link(nc.vector.tensor_scalar(gt["z"], gt["d"], 0.0, None, ALU.is_equal))
            steps.link(nc.vector.tensor_tensor(gt["d"], gt["d"], gt["z"], ALU.add))
            steps.link(nc.vector.reciprocal(gt["r"], gt["d"]))
            steps.link(nc.vector.tensor_tensor(gt["r"], gt["r"], gt["e"], ALU.mult))
            dve.wait_ge(g_to_dve, 3 * g + 2)
            steps.link(nc.vector.tensor_tensor(gt["z"], gt["z"], gt["ln"], ALU.add))
            steps.link(nc.vector.tensor_tensor(gt["z"], gt["z"], gt["r"], ALU.mult))
            steps.link(nc.vector.scalar_tensor_tensor(gt["z"], gt["ad"], 0.0, gt["z"], ALU.max, ALU.add))
            nc.vector.tensor_tensor(gt["g"], gt["z"], negA[:, :].unsqueeze(1).to_broadcast([P, TT, NV]), ALU.mult)\
                .then_inc(g_done, 1)
            nc.vector.tensor_scalar(nbeta, gt["th"], -0.5, -0.5, ALU.mult, ALU.add).then_inc(nbeta_done, 1)
            dve.wait_ge(g_to_dve, 3 * g + 3)
            at_least(dve, at_ps, g)
            split_parts(steps, gt["alpha"], gt["rest"], NV).then_inc(gparts_done, 1)

        def gates_act(act, g):
            act.wait_ge(ba_sb, g + 1)
            nc.scalar.activation(gt["th"], ba[:, :, 0:NV], ACT.Tanh, scale=0.5)
            act.wait_ge(g_to_act, 2 * g + 1)
            nc.scalar.activation(gt["e"], gt["neg"], ACT.Exp).then_inc(g_to_dve, 1)
            act.wait_ge(g_to_act, 2 * g + 2)
            nc.scalar.activation(gt["ln"], gt["u"], ACT.Ln).then_inc(g_to_dve, 1)
            act.wait_ge(g_done, g + 1)
            nc.scalar.activation(gt["alpha"], gt["g"], ACT.Exp).then_inc(g_to_dve, 1)

        def gates_pe_rest(pe, g):
            pe.wait_ge(vt_sb, NK * g + 1)
            pe.wait_ge(g_done, g + 1)
            nc.tensor.matmul(ebank(1)[:, 0:NV], upto[:, :], gt["g"][:, 1, :], start=True, stop=True).then_inc(gc_ps, 1)
            pe.wait_ge(gparts_done, g + 1)
            pe.wait_ge(eg_done, g + 1)
            turn_parts(pe, E1).then_inc(at_ps, 1)

        def gates_act_rest(act, g):
            act.wait_ge(gc_ps, g + 1)
            at_least(act, gmove_done, g)
            nc.scalar.activation(eG, ebank(1)[:, 0:NV], ACT.Exp).then_inc(eg_done, 1)
            act.wait_ge(at_ps, g + 1)
            nc.scalar.activation(partsT[:, :], banks[E1][0:96, 0:T // 2].bitcast(BF16), ACT.Copy).then_inc(at_sb, 1)

        def gates_move(dve, g):
            dve.wait_ge(eg_done, g + 1)
            dve.wait_ge(nbeta_done, g + 1)
            at_least(dve, qst_done, NK // 2 * g)
            nc.vector.tensor_copy(nbeta_walk, nbeta)
            nc.vector.tensor_copy(eG_walk, eG).then_inc(gmove_done, 1)
            dve.wait_ge(gmove_done, g + 1)

        def project_pe(pe, H, n, e, gates):
            w0 = (n % NK) * GROUP * P + 2 * e * P
            if e == 0:
                at_least(pe, kq_sb, H)
            else:
                at_least(pe, up_done, H)
                if n % NK == 0:
                    pe.wait_ge(ba_sb, gates)
            b = ebank(e, "p (b n) -> p b n", b=2)
            for j in range(2):
                for k in range(KD):
                    ins = nc.tensor.matmul(b[:, j, :], wz[:, k, w0 + j * P:w0 + (j + 1) * P], xT[:, k, :],
                                           start=(k == 0), stop=(k == KD - 1))
            ins.then_inc((qk_ps, vp_ps)[e], 1)

        def project_z_pe(pe, H, n):
            w0 = (n % NK) * GROUP * P + 4 * P
            pe.wait_ge(dt_done, H + 1)
            b = ebank(1, "p (c n) -> p c n", c=TT)
            for c in range(TT):
                for k in range(KD):
                    ins = nc.tensor.matmul(b[:, c, :], xT[:, k, c * P:(c + 1) * P], wz[:, k, w0:w0 + 2 * P],
                                           start=(k == 0), stop=(k == KD - 1))
            ins.then_inc(z_ps, 1)

        def taps_act(act, H, n, e):
            if e == 0:
                at_least(act, vt_ps, H)
            act.wait_ge((qk_ps, vp_ps)[e], H + 1)
            b = ebank(e, "p (b n) -> p b n", b=2)
            for j in range(2):
                blk = 2 * e + j
                ins = nc.scalar.activation(yc[:, blk, :], b[:, j, :], ACT.Copy, scale=convw[:, n % NK, blk, TAPS - 1:TAPS])
            ins.then_inc((tap_qk, tap_v)[e], 1)

        def conv_dve(dve, steps, H, n, e):
            dve.wait_ge((tap_qk, tap_v)[e], H + 1)
            b = ebank(e, "p (b n) -> p b n", b=2)
            for back in range(1, TAPS):
                for j in range(2):
                    blk = 2 * e + j
                    ins = nc.vector.scalar_tensor_tensor(yc[:, blk, back:], b[:, j, 0:T - back],
                                                         convw[:, n % NK, blk, TAPS - 1 - back:TAPS - back],
                                                         yc[:, blk, back:], ALU.mult, ALU.add)
                if back < TAPS - 1:
                    steps.link(ins)
            ins.then_inc((conv_qk, conv_v)[e], 1)

        def z_act(act, H, n):
            act.wait_ge(z_ps, H + 1)
            nc.scalar.activation(sz[:, n % 4, :, :].rearrange("p m n -> p (m n)"), ebank(1), ACT.Silu).then_inc(z_sb, 1)

        def silu_act(act, H, n):
            act.wait_ge(conv_qk, H + 1)
            act.wait_ge(conv_v, H + 1)
            nc.scalar.activation(yc[:, :, :], yc[:, :, :], ACT.Silu).then_inc(yc_done, 1)

        def turn_pe(pe, H, n):
            pe.wait_ge(yc_done, H + 1)
            for j in range(2):
                for c in range(TT):
                    ins = nc.tensor.transpose(mm4(E0, 2 * j + c, P), yc[:, j, c * P:(c + 1) * P], ident[:, :])
            ins.then_inc(qkt_ps, 1)
            for c in range(TT):
                for r in range(R):
                    ins = nc.tensor.transpose(mm4(E1, 2 * c + r, P), yc[:, 2 + r, c * P:(c + 1) * P], ident[:, :])
            ins.then_inc(vt_ps, 1)

        def squares_act(act, H, n):
            act.wait_ge(qkt_ps, H + 1)
            at_least(act, qkn_done, H)
            nc.scalar.activation(sq, ebank(0), ACT.Square, scale=HALF).then_inc(sq_done, 1)
            act.wait_ge(vt_ps, H + 1)
            nc.scalar.activation(vt[:, n % 4, :, :].rearrange("p m n -> p (m n)"), ebank(1), ACT.Copy).then_inc(vt_sb, 1)

        def sum_dve(dve, H, n):
            dve.wait_ge(sq_done, H + 1)
            nc.vector.tensor_reduce(ssq, sq.rearrange("p (m n) -> p m n", m=4), AX.X, ALU.add).then_inc(ssq_done, 1)

        def norm_dve(dve, H, n):
            dve.wait_ge(rn_done, H + 1)
            nc.vector.tensor_tensor(qkn[:, n % 4, :, :], ebank(0, "p (m n) -> p m n", m=4),
                                    rn.unsqueeze(2).to_broadcast([P, 4, P]), ALU.mult).then_inc(qkn_done, 1)

        def norm_pool(pool, psteps, H, n):
            pool.wait_ge(ssq_done, H + 1)
            rsqrt_pool(psteps, rn, ssq, eps_qk[:, :], rtmp)
            psteps.link(nc.gpsimd.tensor_tensor(rn, rn, rtmp, ALU.mult))
            nc.gpsimd.tensor_tensor(rn, rn, scale_qk[:, :], ALU.mult).then_inc(rn_done, 1)

        def turn_back_pe(pe, H, n):
            pe.wait_ge(qkn_done, H + 1)
            for c in range(TT):
                for a in range(2):
                    ins = nc.tensor.transpose(mm4(E0, 2 * c + a, P), qkn[:, n % 4, 2 * (1 - a) + c, :], ident[:, :])
            ins.then_inc(kq_ps, 1)

        def turn_back_act(act, H, n):
            act.wait_ge(kq_ps, H + 1)
            nc.scalar.activation(kqT[:, n % 4, :, :, :].rearrange("p c a n -> p (c a n)"), ebank(0), ACT.Copy).then_inc(kq_sb, 1)

        def decays_pe(pe, H, n, gates):
            pe.wait_ge(vt_sb, H + 1)
            if n % NK == 0:
                pe.wait_ge(at_sb, gates)
            b = ebank(1, "p (r n) -> p r n", r=R)
            for r in range(R):
                ins = nc.tensor.matmul(b[:, r, :], selG[:, R * (n % NK) + r, :], partsT[:, :], start=True, stop=True)
            ins.then_inc(ab_ps, 1)

        def products_pe(pe, H, n):
            pe.wait_ge(kq_sb, H + 1)
            pe.wait_ge(z_sb, H + 1)
            b = ebank(1, "p (c n) -> p c n", c=TT)
            for c in range(TT):
                ins = nc.tensor.matmul(b[:, c, :], kqT[:, n % 4, c, 0, :],
                                       kqT[:, n % 4, c, :, :].rearrange("p a n -> p (a n)"), start=True, stop=True)
            ins.then_inc(kk_ps, 1)

        def decay_dve(dve, H, n):
            dve.wait_ge(ab_ps, H + 1)
            at_least(dve, up_done, H)
            b = ebank(1, "p (r c n) -> p r c n", r=R, c=TT)
            for c in range(TT):
                for r in range(R):
                    ins = nc.vector.tensor_tensor_scan(DT[:, 2 * c + r, :], b[:, r, c, :], ident[:, :], 0.0, ALU.mult, ALU.add)
            ins.then_inc(dt_done, 1)

        def weigh_dve(dve, H, n, gates):
            dve.wait_ge(kk_ps, H + 1)
            dve.wait_ge(dt_done, H + 1)
            if n % NK == 0:
                dve.wait_ge(nbeta_done, gates)
            b = ebank(1, "p (c a n) -> p c a n", c=TT, a=2)
            for c in range(TT):
                for r in range(R):
                    hh = R * (n % NK) + r
                    nc.vector.scalar_tensor_tensor(UP[:, n % 4, 2 * c + r, :, :], b[:, c, :, :], nbeta[:, c, hh:hh + 1],
                                                   DT[:, 2 * c + r, :].unsqueeze(1).to_broadcast([P, 2, P]), ALU.mult, ALU.mult)
            nc.vector.tensor_copy(dlast[:, n % 4, :].unsqueeze(2), DT[:, :, P - 1:P]).then_inc(up_done, 1)

        def first_pool(pool, H, n):
            pool.wait_ge(up_done, H + 1)
            yy = Y[:, n % 4, :, :]
            nc.gpsimd.tensor_tensor(yy, UP[:, n % 4, :, 0, :], merge0[:, :].unsqueeze(1).to_broadcast([P, 4, P]), ALU.mult)\
                .then_inc(y_first, 1)
            pool.wait_ge(y_first, H + 1)
            nc.gpsimd.tensor_tensor(yy, yy, ident[:, :].unsqueeze(1).to_broadcast([P, 4, P]), ALU.add).then_inc(y_pre, 1)

        def turn_of(H, n, k):
            return MID * (H - n % 2) + 2 * k + n % 2 + 1

        def x_pe(pe, H, n, lv):
            if lv == 0:
                pe.wait_ge(y_pre, H + 1)
            else:
                pe.wait_ge(y_done, turn_of(H, n, lv - 1))
            for m in range(4):
                ins = nc.tensor.transpose(mm4(2 * (n % 2), m, P), Y[:, n % 4, m, :], ident[:, :])
            ins.then_inc(xx_ps, 1)

        def x_act(act, H, n, lv):
            act.wait_ge(xx_ps, turn_of(H, n, lv))
            nc.scalar.activation(X[:, n % 2, :, :].rearrange("p m n -> p (m n)"), bank(2 * (n % 2)), ACT.Copy).then_inc(xx_sb, 1)

        def nx_pe(pe, H, n, lv):
            pe.wait_ge(xx_sb, turn_of(H, n, lv - 1))
            for m in range(4):
                ins = nc.tensor.matmul(mm4(2 * (n % 2), m, P), UP[:, n % 4, m, 0, :], X[:, n % 2, m, :], start=True, stop=True)
            ins.then_inc(nx_ps, 1)

        def nx_act(act, H, n, lv):
            act.wait_ge(nx_ps, turn_of(H, n, lv - 1))
            nc.scalar.activation(NX[:, n % 2, :, :].rearrange("p m n -> p (m n)"), bank(2 * (n % 2)), ACT.Copy).then_inc(nx_sb, 1)

        def yuy_pe(pe, H, n, lv):
            pe.wait_ge(nx_sb, turn_of(H, n, lv - 1))
            for m in range(4):
                ins = nc.tensor.matmul(mm4(2 * (n % 2) + 1, m, P), NX[:, n % 2, m, :], Y[:, n % 4, m, :], start=True, stop=True)
            ins.then_inc(yuy_ps, 1)

        def merge_dve(dve, H, n, lv):
            dve.wait_ge(yuy_ps, turn_of(H, n, lv - 1))
            dve.wait_ge(y_pre, H + 1)
            if lv > 1:
                dve.wait_ge(y_done, turn_of(H, n, lv - 2))
            nc.vector.tensor_copy(carried[:, n % 2:n % 2 + 1], ident[:, 0:1])
            nc.vector.copy_predicated(Y[:, n % 4, :, :], merge[:, lv, :].unsqueeze(1).to_broadcast([P, 4, P]),
                                      bank(2 * (n % 2) + 1, "p (m n) -> p m n", m=4)).then_inc(y_done, 1)

        def w0_pe(pe, W, s4):
            pe.wait_ge(y_done, 2 * MID * (W + 1))
            at_least(pe, xnt_sb, 2 * W)
            b = ebank(2, "p (s r n) -> p s r n", s=2, r=R)
            for s in range(2):
                for r in range(R):
                    ins = nc.tensor.matmul(b[:, s, r, :], Y[:, s4 + s, r, :], vt[:, s4 + s, r, :], start=True, stop=True)
            ins.then_inc(w0_ps, 1)

        def w0_dve(dve, steps, W, s4, n):
            steps.link(nc.vector.tensor_tensor(bd.rearrange("p (s r) -> p s r", s=2), dlast[:, s4:s4 + 2, 0:R],
                                               nbeta_walk[:, 0, R * n:R * n + 4].rearrange("p (s r) -> p s r", s=2), ALU.mult))
            dve.wait_ge(w0_ps, W + 1)
            b = ebank(2, "p (s r n) -> p s (r n)", s=2, r=R)
            nc.vector.tensor_copy(w01[:, :, 0, :, :].rearrange("p s r n -> p s (r n)"), b)
            nc.vector.tensor_tensor(w0s.rearrange("p s r n -> p (s r) n"), ebank(2, "p (m n) -> p m n", m=4),
                                    bd.unsqueeze(2).to_broadcast([P, 4, P]), ALU.mult).then_inc(w0_sb, 1)

        def state_pe(pe, W, s4):
            pe.wait_ge(w0_sb, W + 1)
            for s in range(2):
                ins = nc.tensor.matmul(ebank(2, "p (s n) -> p s n", s=2)[:, s, :], qkn[:, s4 + s, 2, :],
                                       w0s[:, s, :, :].rearrange("p r n -> p (r n)"), start=True, stop=True)
            ins.then_inc(st_ps, 1)

        def state_act(act, W):
            act.wait_ge(st_ps, W + 1)
            nc.scalar.activation(st, ebank(2, "p (s n) -> p s n", s=2), ACT.Copy).then_inc(st_sb, 1)

        def from_state_pe(pe, W, s4, a):
            if a == 0:
                pe.wait_ge(st_sb, W + 1)
            else:
                pe.wait_ge(r_done, W + 1)
            for s in range(2):
                ins = nc.tensor.matmul(ebank(2, "p (s n) -> p s n", s=2)[:, s, :], kqT[:, s4 + s, 1, a, :], st[:, s, :],
                                       start=True, stop=True)
            ins.then_inc((ks_ps, qs_ps)[a], 1)

        def rhs_dve(dve, W, s4, n):
            dve.wait_ge(ks_ps, W + 1)
            b = ebank(2, "p (s r n) -> p s r n", s=2, r=R)
            for s in range(2):
                for r in range(R):
                    hh = R * (n + s) + r
                    ins = nc.vector.scalar_tensor_tensor(rhs1[:, s, r, :], b[:, s, r, :], eG_walk[:, hh:hh + 1],
                                                         vt[:, s4 + s, 2 + r, :], ALU.mult, ALU.add)
            ins.then_inc(r_done, 1)

        def qs_dve(dve, W, n):
            dve.wait_ge(qs_ps, W + 1)
            nc.vector.tensor_tensor(qst.rearrange("p s r n -> p (s r) n"), ebank(2, "p (m n) -> p m n", m=4),
                                    eG_walk[:, R * n:R * n + 4].unsqueeze(2).to_broadcast([P, 4, P]), ALU.mult)\
                .then_inc(qst_done, 1)

        def w1_pe(pe, W, s4):
            pe.wait_ge(qst_done, W + 1)
            b = ebank(2, "p (s r n) -> p s r n", s=2, r=R)
            for s in range(2):
                for r in range(R):
                    ins = nc.tensor.matmul(b[:, s, r, :], Y[:, s4 + s, 2 + r, :], rhs1[:, s, r, :], start=True, stop=True)
            ins.then_inc(w1_ps, 1)

        def w1_act(act, W):
            act.wait_ge(w1_ps, W + 1)
            nc.scalar.activation(w01[:, :, 1, :, :].rearrange("p s r n -> p s (r n)"),
                                 ebank(2, "p (s n) -> p s n", s=2), ACT.Copy).then_inc(w1_sb, 1)

        def out_pe(pe, W, s4, s):
            if s == 0:
                pe.wait_ge(w1_sb, W + 1)
            else:
                pe.wait_ge(xf_done, 2 * W + 1)
            for m in range(4):
                ins = nc.tensor.matmul(mm4(E2, m, P), UP[:, s4 + s, m, 1, :], w01[:, s, m // 2, m % 2, :], start=True, stop=True)
            ins.then_inc(og_ps, 1)

        def gate_dve(dve, steps, W, s4, s):
            if s == 0:
                dve.wait_ge(qst_done, W + 1)
                at_least(dve, xfn_done, W)
            dve.wait_ge(og_ps, 2 * W + s + 1)
            b = ebank(2, "p (m n) -> p m n", m=4)
            steps.link(nc.vector.tensor_tensor(xf[:, s, 1, :, :], b[:, 2:4, :], qst[:, s, :, :], ALU.add))
            nc.vector.tensor_tensor(xf[:, s, 0, :, :], b[:, 0:2, :], sz[:, s4 + s, 0:2, :], ALU.mult)
            nc.vector.tensor_tensor(xf[:, s, 1, :, :], xf[:, s, 1, :, :], sz[:, s4 + s, 2:4, :], ALU.mult).then_inc(xf_done, 1)

        def squares_x_act(act, W):
            act.wait_ge(xf_done, 2 * W + 2)
            nc.scalar.activation(xfn.rearrange("p s c r n -> p (s c r n)"), xf.rearrange("p s c r n -> p (s c r n)"),
                                 ACT.Square, scale=HALF).then_inc(sqx_done, 1)

        def sum_x_dve(dve, W):
            dve.wait_ge(sqx_done, W + 1)
            nc.vector.tensor_reduce(ssx, xfn.rearrange("p s c r n -> p (s c r) n"), AX.X, ALU.add).then_inc(ssx_done, 1)

        def norm_x_pool(pool, psteps, W):
            pool.wait_ge(ssx_done, W + 1)
            rsqrt_pool(psteps, rx, ssx, eps_x[:, :], rxt)
            psteps.link(nc.gpsimd.tensor_tensor(rx, rx, rxt, ALU.mult))
            nc.gpsimd.tensor_tensor(xfn.rearrange("p s c r n -> p (s c r) n"), xf.rearrange("p s c r n -> p (s c r) n"),
                                    rx.unsqueeze(2).to_broadcast([P, 8, P]), ALU.mult).then_inc(xfn_done, 1)

        def turn_x_pe(pe, W, s):
            if s == 0:
                pe.wait_ge(xfn_done, W + 1)
            else:
                pe.wait_ge(xnt_sb, 2 * W + 1)
            for r in range(R):
                for c in range(TT):
                    ins = nc.tensor.transpose(mm4(E2, 2 * r + c, P), xfn[:, s, c, r, :], ident[:, :])
            ins.then_inc(xnt_ps, 1)

        def turn_x_act(act, W, s):
            act.wait_ge(xnt_ps, 2 * W + s + 1)
            nc.scalar.activation(xnT[:, s, :, :].rearrange("p r n -> p (r n)"), ebank(2), ACT.Copy).then_inc(xnt_sb, 1)

        def project_out_pe(pe, W, n, s, c_x):
            pe.wait_ge(xnt_sb, 2 * W + s + 1)
            if n + s == 0:
                pe.wait_ge(x_done, c_x)
            b = bank(ACC, "p (t n) -> p t n", t=TT)
            for r in range(R):
                for t in range(TT):
                    ins = nc.tensor.matmul(b[:, t, :], xnT[:, s, r, t * P:(t + 1) * P], wout[:, R * (n + s) + r, :],
                                           start=(n + s == 0 and r == 0 and t == 0), stop=(n + s == NK - 1 and r == R - 1),
                                           skip_group_check=True)
            ins.then_inc(acc_done, 1)

        def add_x_dve(dve, g, i):
            dve.wait_ge(acc_done, NK * (g + 1))
            xs = x[:, bass.ds(2 * i, TT), :]
            nc.vector.tensor_tensor(xs, bank(ACC, "p (t n) -> p t n", t=TT), xs, ALU.add).then_inc(x_done, 1)

        SLOTS = 3 * MID

        def round_pe(pe, g, p, stage1, walk, prep):
            H = NK * g + 2 * p
            A, B, n = 2 * p + 2, 2 * p + 3, (2 * p - 2) % NK
            W, s4 = (NK // 2) * g + p - 1, (2 * p - 2) % 4
            c_x = 2 * NBATCH + g - (1 if p == 0 else 0)
            for k in range(SLOTS):
                lv = k // 3 + 1
                if k == 0:
                    x_pe(pe, H, 2 * p, 0)
                    if stage1:
                        if A == NK:
                            gates_pe_ba(pe, g + 1)
                        project_pe(pe, H + 2, A, 0, g + 2)
                    x_pe(pe, H + 1, 2 * p + 1, 0)
                for s in range(2):
                    (nx_pe, yuy_pe, x_pe)[k % 3](pe, H + s, 2 * p + s, lv) if not (k % 3 == 2 and lv == MID) else None
                if walk:
                    if k == 0:
                        w0_pe(pe, W, s4)
                    if k == 1:
                        state_pe(pe, W, s4)
                    if k in (2, 3):
                        from_state_pe(pe, W, s4, k - 2)
                    if k == 4:
                        w1_pe(pe, W, s4)
                    if k in (5, 7):
                        out_pe(pe, W, s4, (k - 5) // 2)
                    if k in (12, 13):
                        turn_x_pe(pe, W, k - 12)
                    if k in (13, 14):
                        project_out_pe(pe, W, n, k - 13, c_x)
                if stage1:
                    if k == 1:
                        project_pe(pe, H + 2, A, 1, g + 2)
                    if k == 4:
                        turn_pe(pe, H + 2, A)
                    if k == 6:
                        if A == NK:
                            gates_pe_rest(pe, g + 1)
                        decays_pe(pe, H + 2, A, g + 2)
                    if k == 8:
                        project_z_pe(pe, H + 2, A)
                        turn_back_pe(pe, H + 2, A)
                    if k == 9:
                        project_pe(pe, H + 3, B, 0, g + 2)
                    if k == 10:
                        products_pe(pe, H + 2, A)
                    if k == 11:
                        project_pe(pe, H + 3, B, 1, g + 2)
                    if k == 14:
                        turn_pe(pe, H + 3, B)
                    if k == 15:
                        decays_pe(pe, H + 3, B, g + 2)
                    if k == 16:
                        project_z_pe(pe, H + 3, B)
                    if k == 17:
                        turn_back_pe(pe, H + 3, B)
                        products_pe(pe, H + 3, B)
            if prep:
                pe.wait_ge(kq_sb, H + 4)
                prep_turn(pe, 2 * NBATCH + g + 1)

        def round_dve(dve, steps, g, p, i, stage1, walk, prep):
            H = NK * g + 2 * p
            A, B, n = 2 * p + 2, 2 * p + 3, (2 * p - 2) % NK
            W, s4 = (NK // 2) * g + p - 1, (2 * p - 2) % 4
            if stage1 and A == NK:
                gates_dve_ba(dve, g + 1)
            for k in range(SLOTS):
                if k % 3 == 1:
                    for s in range(2):
                        merge_dve(dve, H + s, 2 * p + s, k // 3 + 1)
                if walk:
                    if k == 0:
                        w0_dve(dve, steps, W, s4, n)
                    if k == 2:
                        rhs_dve(dve, W, s4, n)
                    if k == 3:
                        qs_dve(dve, W, n)
                    if k in (5, 7):
                        gate_dve(dve, steps, W, s4, (k - 5) // 2)
                    if k == 8:
                        sum_x_dve(dve, W)
                    if k == 15 and p == 0:
                        add_x_dve(dve, g - 1, i - 1)
                if k == 4 and p == 0:
                    gates_move(dve, g)
                if stage1:
                    if k == 1:
                        conv_dve(dve, steps, H + 2, A, 0)
                    if k == 2:
                        conv_dve(dve, steps, H + 2, A, 1)
                    if k == 3 and A == NK:
                        gates_dve(dve, steps, g + 1)
                    if k == 5:
                        sum_dve(dve, H + 2, A)
                    if k == 6:
                        decay_dve(dve, H + 2, A)
                    if k == 8:
                        norm_dve(dve, H + 2, A)
                    if k == 10:
                        weigh_dve(dve, H + 2, A, g + 2)
                        conv_dve(dve, steps, H + 3, B, 0)
                    if k == 12:
                        conv_dve(dve, steps, H + 3, B, 1)
                    if k == 14:
                        sum_dve(dve, H + 3, B)
                    if k == 15:
                        decay_dve(dve, H + 3, B)
                    if k == 17:
                        norm_dve(dve, H + 3, B)
                        weigh_dve(dve, H + 3, B, g + 2)
                if k == 13 and prep is not None:
                    prep_norm(dve, steps, 2 * NBATCH + g + 1, prep)

        def round_act(act, g, p, stage1, walk, prep):
            H = NK * g + 2 * p
            A, B = 2 * p + 2, 2 * p + 3
            W = (NK // 2) * g + p - 1
            for k in range(SLOTS):
                if k == 0:
                    x_act(act, H, 2 * p, 0)
                    if stage1:
                        taps_act(act, H + 2, A, 0)
                    x_act(act, H + 1, 2 * p + 1, 0)
                if k % 3 == 0 or (k % 3 == 2 and k < SLOTS - 1):
                    for s in range(2):
                        (nx_act, None, x_act)[k % 3](act, H + s, 2 * p + s, k // 3 + 1)
                if walk:
                    if k == 1:
                        state_act(act, W)
                    if k == 4:
                        w1_act(act, W)
                    if k == 7:
                        squares_x_act(act, W)
                    if k in (12, 13):
                        turn_x_act(act, W, k - 12)
                if stage1:
                    if k == 1:
                        taps_act(act, H + 2, A, 1)
                    if k == 3 and A == NK:
                        gates_act(act, g + 1)
                    if k == 3:
                        silu_act(act, H + 2, A)
                    if k == 4:
                        squares_act(act, H + 2, A)
                    if k == 6 and A == NK:
                        gates_act_rest(act, g + 1)
                    if k == 8:
                        z_act(act, H + 2, A)
                        turn_back_act(act, H + 2, A)
                    if k == 9:
                        taps_act(act, H + 3, B, 0)
                    if k == 11:
                        taps_act(act, H + 3, B, 1)
                    if k == 13:
                        silu_act(act, H + 3, B)
                    if k == 14:
                        squares_act(act, H + 3, B)
                    if k == 16:
                        z_act(act, H + 3, B)
                    if k == 17:
                        turn_back_act(act, H + 3, B)
            if prep:
                prep_copy(act, 2 * NBATCH + g + 1)

        def round_pool(pool, psteps, g, p, stage1, walk):
            H = NK * g + 2 * p
            A, B = 2 * p + 2, 2 * p + 3
            W = (NK // 2) * g + p - 1
            if stage1:
                norm_pool(pool, psteps, H + 2, A)
            if walk:
                norm_x_pool(pool, psteps, W)
            if stage1:
                first_pool(pool, H + 2, A)
                norm_pool(pool, psteps, H + 3, B)
                first_pool(pool, H + 3, B)

        ROUNDS = NK // 2
        PREP = ROUNDS - 2

        def gdn_pe(pe, g, first=False, last=False):
            for p in range(ROUNDS):
                round_pe(pe, g, p, not (last and p == ROUNDS - 1), not (first and p == 0),
                         p == PREP and (not last or stages > 3))

        def gdn_dve(dve, steps, g, first=False, last=False):
            nxt = (0 if stages > 3 else None) if last else g + 1
            for p in range(ROUNDS):
                round_dve(dve, steps, g, p, g, not (last and p == ROUNDS - 1), not (first and p == 0),
                          nxt if p == PREP else None)

        def gdn_act(act, g, first=False, last=False):
            for p in range(ROUNDS):
                round_act(act, g, p, not (last and p == ROUNDS - 1), not (first and p == 0),
                          p == PREP and (not last or stages > 3))

        def gdn_pool(pool, psteps, g, first=False, last=False):
            for p in range(ROUNDS):
                round_pool(pool, psteps, g, p, not (last and p == ROUNDS - 1), not (first and p == 0))

        LASTW = NBATCH * ROUNDS - 1

        def gdn_all_pe(pe):
            pe.wait_ge(x_done, 2 * NBATCH)
            pe.wait_ge(w_gdn, 4 * 16)
            pe.wait_ge(wout_scaled, 1)
            gates_pe_ba(pe, 0)
            for n in range(2):
                project_pe(pe, n, n, 0, 1)
                project_pe(pe, n, n, 1, 1)
                turn_pe(pe, n, n)
                if n == 0:
                    gates_pe_rest(pe, 0)
                decays_pe(pe, n, n, 1)
                project_z_pe(pe, n, n)
                turn_back_pe(pe, n, n)
                products_pe(pe, n, n)
            gdn_pe(pe, 0, first=True)
            with pe.Fori(1, NBATCH - 1) as g:
                gdn_pe(pe, g)
            gdn_pe(pe, NBATCH - 1, last=True)
            n, s4 = NK - 2, 2
            w0_pe(pe, LASTW, s4)
            state_pe(pe, LASTW, s4)
            from_state_pe(pe, LASTW, s4, 0)
            from_state_pe(pe, LASTW, s4, 1)
            w1_pe(pe, LASTW, s4)
            out_pe(pe, LASTW, s4, 0)
            out_pe(pe, LASTW, s4, 1)
            turn_x_pe(pe, LASTW, 0)
            turn_x_pe(pe, LASTW, 1)
            project_out_pe(pe, LASTW, n, 0, 0)
            project_out_pe(pe, LASTW, n, 1, 0)

        def gdn_all_dve(dve, steps):
            dve.wait_ge(x_done, 2 * NBATCH)
            dve.wait_ge(pconsts, 1)
            gates_dve_ba(dve, 0)
            gates_dve(dve, steps, 0)
            for n in range(2):
                conv_dve(dve, steps, n, n, 0)
                conv_dve(dve, steps, n, n, 1)
                sum_dve(dve, n, n)
                decay_dve(dve, n, n)
                norm_dve(dve, n, n)
                weigh_dve(dve, n, n, 1)
            base = steps.base + steps.n
            steps.turn(base)
            gdn_dve(dve, steps, 0, first=True)
            base = base + steps.n
            with dve.Fori(1, NBATCH - 1) as g:
                steps.turn(base + STEPS_GDN * (g - 1))
                gdn_dve(dve, steps, g)
            assert steps.n == STEPS_GDN, steps.n
            steps.turn(base + STEPS_GDN * (NBATCH - 2))
            gdn_dve(dve, steps, NBATCH - 1, last=True)
            n, s4 = NK - 2, 2
            w0_dve(dve, steps, LASTW, s4, n)
            rhs_dve(dve, LASTW, s4, n)
            qs_dve(dve, LASTW, n)
            gate_dve(dve, steps, LASTW, s4, 0)
            gate_dve(dve, steps, LASTW, s4, 1)
            sum_x_dve(dve, LASTW)
            add_x_dve(dve, NBATCH - 1, NBATCH - 1)

        def gdn_all_act(act):
            act.wait_ge(x_done, 2 * NBATCH)
            act.wait_ge(w_gdn, 4 * 16)
            gates_act(act, 0)
            for n in range(2):
                taps_act(act, n, n, 0)
                taps_act(act, n, n, 1)
                silu_act(act, n, n)
                squares_act(act, n, n)
                if n == 0:
                    gates_act_rest(act, 0)
                z_act(act, n, n)
                turn_back_act(act, n, n)
            gdn_act(act, 0, first=True)
            with act.Fori(1, NBATCH - 1) as g:
                gdn_act(act, g)
            gdn_act(act, NBATCH - 1, last=True)
            state_act(act, LASTW)
            w1_act(act, LASTW)
            squares_x_act(act, LASTW)
            turn_x_act(act, LASTW, 0)
            turn_x_act(act, LASTW, 1)

        def gdn_all_pool(pool):
            psteps = Steps(pool, pstep)
            for n in range(2):
                norm_pool(pool, psteps, n, n)
                first_pool(pool, n, n)
            base = psteps.n
            psteps.turn(base)
            gdn_pool(pool, psteps, 0, first=True)
            base = base + psteps.n
            with pool.Fori(1, NBATCH - 1) as g:
                psteps.turn(base + STEPS_POOL * (g - 1))
                gdn_pool(pool, psteps, g)
            assert psteps.n == STEPS_POOL, psteps.n
            psteps.turn(base + STEPS_POOL * (NBATCH - 2))
            gdn_pool(pool, psteps, NBATCH - 1, last=True)
            norm_x_pool(pool, psteps, LASTW)

        @block.gpsimd
        def _(pool):
            pool.wait_ge(w_attn, 8 * 16)
            pool.wait_ge(x_in, 32)

            def add_bo(i):
                pool.wait_ge(normed, i + 1)
                for t in range(TT):
                    ins = nc.gpsimd.tensor_tensor(x[:, 2 * i + t, :], x[:, 2 * i + t, :], bo, ALU.add)
                ins.then_inc(xb_done, 1)
            with pool.Fori(0, NBATCH) as i:
                add_bo(i)
            nc.gpsimd.memset(onehalf[:, :], 1.5)
            nc.gpsimd.memset(eps_qk[:, :], L2_EPS / 2)
            nc.gpsimd.memset(eps_x[:, :], P * NORM_EPS / 2)
            nc.gpsimd.memset(scale_qk[:, 0:2], float(P) ** -0.5)
            nc.gpsimd.memset(scale_qk[:, 2:4], 1.0).then_inc(pconsts, 1)
            pool.wait_ge(pconsts, 1)
            pool.wait_ge(w_gdn, 4 * 16)
            pool.wait_ge(consts, 1)
            pool.wait_ge(c_in, 8 * 16)
            nc.gpsimd.tensor_scalar(wout[:, :, :], wout[:, :, :], normw[:, 0:1], -float(P) ** 0.5, ALU.mult, ALU.mult)\
                .then_inc(wout_scaled, 1)
            if stages > 2:
                gdn_all_pool(pool)

        ffn_layers = [(1, 0)] + ([(3, 1)] if stages > 3 else [])

        @block.tensor
        def _(pe):
            pe.wait_ge(consts, 1)
            pe.wait_ge(w_attn, 8 * 16)
            prep_turn(pe, 0)
            attn_pe(pe, 0, True)
            with pe.Fori(1, NBATCH - 1) as i:
                attn_pe(pe, i, True)
            attn_pe(pe, NBATCH - 1, True if stages > 1 else None)
            for layer, rep in ffn_layers:
                if layer >= stages:
                    break
                if layer == 3:
                    gdn_all_pe(pe)
                pe.wait_ge(x_done, layer * NBATCH)
                pe.wait_ge(*((w_ffn, 4 * 16) if rep == 0 else (w_ffn2, 3 * 16)))
                ffn_pe(pe, layer * NBATCH, rep * NBATCH, ffnw[rep], True)
                with pe.Fori(1, NBATCH - 1) as i:
                    ffn_pe(pe, layer * NBATCH + i, rep * NBATCH + i, ffnw[rep], True)
                ffn_pe(pe, layer * NBATCH + 7, rep * NBATCH + 7, ffnw[rep], True if layer + 1 < stages else None)
            if stages == 3:
                gdn_all_pe(pe)

        @block.vector
        def _(dve):
            steps = Steps(dve, vstep)
            nc.vector.memset(parts[:, :, :], 0.0)
            dve.wait_ge(c_in, 8 * 16)
            nc.vector.tensor_copy(identb[:, :], ident[:, :])
            nc.vector.tensor_copy(merge0[:, :], merge[:, 0, :])
            nc.vector.tensor_copy(selF[:, :, :], pick[:, 0:NE].unsqueeze(2).to_broadcast([96, NE, HID]))
            nc.vector.tensor_copy(selG[:, :, :], pick[:, 0:NV].unsqueeze(2).to_broadcast([96, NV, P])).then_inc(consts, 1)
            dve.wait_ge(astep, 1)
            steps.link(nc.vector.tensor_scalar(negA[:, :], negA[:, :], -1.0, None, ALU.mult))
            dve.wait_ge(x_in, 32)
            dve.wait_ge(w_attn, 8 * 16)
            prep_norm(dve, steps, 0, 0)
            start = steps.n
            steps.turn(start)
            attn_dve(dve, steps, 0, 0, 1)
            with dve.Fori(1, NBATCH - 1) as i:
                steps.turn(start + STEPS_ATTN * i)
                attn_dve(dve, steps, i, i, i + 1)
            assert steps.n == STEPS_ATTN, steps.n
            steps.turn(start + STEPS_ATTN * (NBATCH - 1))
            attn_dve(dve, steps, NBATCH - 1, NBATCH - 1, 0 if stages > 1 else None)
            for layer, rep in ffn_layers:
                if layer >= stages:
                    break
                if layer == 3:
                    gdn_all_dve(dve, steps)
                start = steps.base + steps.n
                dve.wait_ge(x_done, layer * NBATCH)
                steps.turn(start)
                ffn_dve(dve, steps, layer * NBATCH, rep * NBATCH, 0, 1)
                with dve.Fori(1, NBATCH - 1) as i:
                    steps.turn(start + STEPS_FFN * i)
                    ffn_dve(dve, steps, layer * NBATCH + i, rep * NBATCH + i, i, i + 1)
                assert steps.n == STEPS_FFN, steps.n
                steps.turn(start + STEPS_FFN * (NBATCH - 1))
                ffn_dve(dve, steps, layer * NBATCH + 7, rep * NBATCH + 7, 7, 0 if layer + 1 < stages else None)
            if stages == 3:
                gdn_all_dve(dve, steps)

        @block.scalar
        def _(act):
            act.wait_ge(c_in, 8 * 16)
            nc.scalar.activation(negA[:, :], negA[:, :], ACT.Exp).then_inc(astep, 1)
            act.wait_ge(w_attn, 8 * 16)
            prep_copy(act, 0)
            attn_act(act, 0, True)
            with act.Fori(1, NBATCH - 1) as i:
                attn_act(act, i, True)
            attn_act(act, NBATCH - 1, True if stages > 1 else None)
            for layer, rep in ffn_layers:
                if layer >= stages:
                    break
                if layer == 3:
                    gdn_all_act(act)
                act.wait_ge(x_done, layer * NBATCH)
                ffn_act(act, layer * NBATCH, rep * NBATCH, True)
                with act.Fori(1, NBATCH - 1) as i:
                    ffn_act(act, layer * NBATCH + i, rep * NBATCH + i, True)
                ffn_act(act, layer * NBATCH + 7, rep * NBATCH + 7, True if layer + 1 < stages else None)
            if stages == 3:
                gdn_all_act(act)


def consts():
    p = np.arange(P)
    upto = (p[:, None] <= p[None, :]).astype(np.float32)
    merge = np.zeros((P, LEVELS, P), np.int32)
    for lv in range(LEVELS):
        b = 1 << lv
        same = p[:, None] // (2 * b) == p[None, :] // (2 * b)
        merge[:, lv, :] = same & ((p[:, None] // b) % 2 == 0) & ((p[None, :] // b) % 2 == 1)
    pick = (np.arange(96)[:, None] % 32 == np.arange(16)[None, :]).astype(np.float32)
    desc = np.ascontiguousarray(np.broadcast_to(np.arange(E, 0, -1, dtype=np.float32), (P, TT, E)))
    return {"ident": np.eye(P, dtype=np.float32), "upto": upto, "merge": merge, "pick": pick, "desc": desc}


def laid_out(inp):
    def g(n):
        return np.asarray(inp[n])

    def by_rows(w):
        return np.ascontiguousarray(w.reshape(KD, P, -1).transpose(1, 0, 2))

    def padded(w):
        out = np.zeros((w.shape[0], HEADS, HP), w.dtype)
        out[:, :, :HD] = w.reshape(-1, HEADS, HD)
        return out.reshape(w.shape[0], HEADS * HP)

    def spread(v):
        return np.ascontiguousarray(np.broadcast_to(v, (P, v.shape[-1])))

    a = "L0_attn_a_"
    b = "L0_attn_b_"
    f = "L0_ffn_"
    r = {"x": np.ascontiguousarray(g(a + "x").reshape(NBATCH * T, D))}
    r["wq"], r["wk"] = by_rows(padded(g(a + "Wq").T)), by_rows(padded(g(a + "Wk").T))
    r["wv"], r["wo"] = by_rows(g(a + "Wv").T), by_rows(g(a + "Wo").T)
    for n in ("bq", "bk"):
        r[n] = np.ascontiguousarray(padded(g(a + n)[None, :]).reshape(QB, P).T)
    r["bv"], r["bo"] = spread(g(a + "bv")), spread(g(a + "bo"))
    for n, ew, sw in (("wg", "w_gate", "shw_gate"), ("wu", "w_up", "shw_up")):
        r[n] = by_rows(np.concatenate([g(f + ew).transpose(1, 0, 2).reshape(D, E * HID), g(f + sw)], 1))
    wd = np.zeros((NB * P, D), np.float32)
    wd[:E * HID] = g(f + "w_down").reshape(E * HID, D)
    wd[E * HID:FH] = g(f + "shw_down")
    r["wd"] = np.ascontiguousarray(wd.reshape(NB, P, D).transpose(1, 0, 2))
    r["wr"] = by_rows(np.concatenate([g(f + "gate_w"), g(f + "shgate_w")[None]], 0).T)
    r["wz"] = by_rows(g(b + "w_qkvz").T)
    ba = g(b + "w_ba").reshape(NK, 2, R, D).transpose(1, 0, 2, 3).reshape(2 * NV, D)
    r["wba"] = by_rows(ba.T)
    r["wout"] = np.ascontiguousarray(g(b + "w_out").T.reshape(NV, P, D).transpose(1, 0, 2))
    cw = g(b + "conv_w")
    r["convw"] = np.ascontiguousarray(np.concatenate([
        cw[:NK * P].reshape(NK, 1, P, TAPS), cw[NK * P:2 * NK * P].reshape(NK, 1, P, TAPS),
        cw[2 * NK * P:].reshape(NK, R, P, TAPS)], 1).transpose(2, 0, 1, 3))
    r["dt_bias"], r["A_log"] = spread(g(b + "dt_bias")), spread(g(b + "A_log"))
    r["normw"] = np.ascontiguousarray(g(b + "norm_weight")[:, None])
    r.update(consts())
    return r


def kernel(**inputs):
    import concourse.bacc as bacc
    from concourse.bass_utils import run_bass_kernel_spmd as run

    nc = bacc.Bacc("TRN2", target_bir_lowering=False, num_devices=1)
    arrays, io = {}, {}
    for name, a in laid_out(inputs).items():
        arrays[f"in_{name}"] = a
        io[name] = nc.dram_tensor(f"in_{name}", a.shape, mybir.dt.from_np(a.dtype), kind="ExternalInput").ap()
    io["out"] = nc.dram_tensor("out", (NBATCH * T, D), F32, kind="ExternalOutput").ap()
    build(nc, io)
    r = run(nc, [arrays], core_ids=[0])
    return r.results[0]["out"].reshape(NBATCH, T, D)
```

```python
from contextlib import ExitStack

import numpy as np

import concourse.bass as bass
from concourse import mybir
from concourse.alu_op_type import AluOpType as ALU

F32 = mybir.dt.float32
BF16 = mybir.dt.bfloat16
I32 = mybir.dt.int32
ACT = mybir.ActivationFunctionType
AX = mybir.AxisListType

P = 128
NBATCH = 8
T = 256
D = 256
KD = D // P
TT = T // P
NTILE = NBATCH * TT
LN_EPS = 1e-5

HEADS, HD = 16, 16
HP = 32
QB = HEADS * HP // P
HB = P // HD
SM_SCALE = 0.5

E, HID, HSH = 8, 176, 352
NE = E + HSH // HID
FH = NE * HID
NB = -(-FH // P)
BLK = [min(P, FH - P * j) for j in range(NB)]

NK, R, NV = 8, 2, 16
GROUP = 2 + 2 * R
TAPS = 4
L2_EPS = 1e-6
NORM_EPS = 1e-6
LEVELS = 7
MID = LEVELS - 1

STEPS_ATTN, STEPS_FFN, STEPS_GDN, STEPS_POOL = 17, 36, 75, 168


class Steps:

    def __init__(self, eng, sem):
        self.eng, self.sem, self.base, self.n = eng, sem, 0, 0

    def link(self, ins):
        self.n += 1
        ins.then_inc(self.sem, 1)
        self.eng.wait_ge(self.sem, self.base + self.n)

    def turn(self, base):
        self.base, self.n = base, 0


def build(nc, io, stages=4):
    ctx = ExitStack()
    with ctx:
        def sb(name, shape, dt=F32):
            return ctx.enter_context(nc.sbuf_tensor(name, shape, dt))

        def sem(name):
            return ctx.enter_context(nc.semaphore(name))

        x = sb("x", [P, NTILE, D])
        xT2 = sb("xT2", [P, 2, KD, T])
        xT = xT2[:, 0, :, :]
        xn = sb("xn", [P, TT, D])
        stats = sb("stats", [P, TT, 6])
        mean = sb("mean", [P, TT, 1])
        varp, newt, rstd = sb("varp", [P, TT, 1]), sb("newt", [P, TT, 1]), sb("rstd", [P, TT, 1])
        ident = sb("ident", [P, P])
        identb = sb("identb", [P, P], BF16)
        upto = sb("upto", [P, P])
        merge = sb("merge", [P, LEVELS, P], I32)
        merge0 = sb("merge0", [P, P])
        carried = sb("carried", [P, 4])
        onehalf = sb("onehalf", [P, 8])
        eps_qk, eps_x = sb("eps_qk", [P, 4]), sb("eps_x", [P, 8])
        scale_qk = sb("scale_qk", [P, 4])
        pick = sb("pick", [96, 16])
        selF = sb("selF", [96, NE, HID], BF16)
        selG = sb("selG", [96, NV, P], BF16)
        desc = sb("desc", [P, TT, E])
        parts = sb("parts", [P, TT, 96], BF16)
        partsT2 = sb("partsT2", [96, 2, T], BF16)
        wout = sb("wout", [P, NV, D])
        wba = sb("wba", [P, KD, 2 * NV])
        convw = sb("convw", [P, NK, 4, TAPS])
        dtb = sb("dtb", [P, NV])
        negA = sb("negA", [P, NV])
        normw = sb("normw", [P, 1])
        big = sb("big", [P, KD * NK * GROUP * P])
        small = sb("small", [P, 1280])
        ARENA = 24640
        arena = sb("arena", [P, ARENA])

        used = {"arena": 0, "small": 0}

        def carve(n, where="arena"):
            a = used[where]
            used[where] = a + n
            t = arena if where == "arena" else small
            assert used[where] <= (ARENA if where == "arena" else 1280), used
            return t[:, a:a + n]

        def view(ap, pattern, **k):
            return ap.rearrange(pattern, **k)

        NW = KD * FH

        def ffn_weights(t):
            return (view(t[:, 0:NW], "p (k n) -> p k n", k=KD), view(t[:, NW:2 * NW], "p (k n) -> p k n", k=KD),
                    view(t[:, 2 * NW:2 * NW + NB * D], "p (j n) -> p j n", j=NB))
        wr = sb("wr", [P, KD, E + 1])
        ffnw = [ffn_weights(carve(2 * NW + NB * D)), ffn_weights(big)]
        wq = view(carve(KD * D), "p (k n) -> p k n", k=KD)
        wk = view(carve(KD * D), "p (k n) -> p k n", k=KD)
        wv = view(carve(KD * D), "p (k n) -> p k n", k=KD)
        wo = view(carve(QB * D), "p (k n) -> p k n", k=QB)
        bq, bk = carve(KD), carve(KD)
        bv, bo = carve(D), carve(D)
        after_attn_weights = used["arena"]
        qT = view(carve(HEADS * T), "p (h n) -> p h n", h=HEADS)
        kT = view(carve(KD * T), "p (b n) -> p b n", b=KD)
        v = view(carve(TT * D), "p (t n) -> p t n", t=TT)
        probs = view(carve(4 * TT * T), "p (s t n) -> p s t n", s=4, t=TT)
        probsT = view(carve(2 * TT * T), "p (s t n) -> p s t n", s=2, t=TT)
        oT = view(carve(QB * T), "p (k n) -> p k n", k=QB)
        negmax = sb("negmax", [P, 4, TT])
        sums = sb("sums", [P, 4, TT])
        rsums = sb("rsums", [P, 4, TT])
        qmask = sb("qmask", [P, HB])
        bqm = sb("bqm", [P, HEADS])
        used["arena"] = after_attn_weights
        gact = view(carve(2 * T), "p (s n) -> p s n", s=2)
        hid = view(carve(2 * T), "p (s n) -> p s n", s=2)
        hidT = view(carve(2 * T), "p (s n) -> p s n", s=2)
        used["arena"] = 0
        yc = view(carve(4 * T), "p (b n) -> p b n", b=4)
        sq = carve(4 * P)
        qkn = view(carve(4 * 4 * P), "p (s m n) -> p s m n", s=4, m=4)
        vt = view(carve(4 * 4 * P), "p (s m n) -> p s m n", s=4, m=4)
        kqT = view(carve(4 * 4 * P), "p (s c m n) -> p s c m n", s=4, c=2, m=2)
        UP = view(carve(4 * 8 * P), "p (s m a n) -> p s m a n", s=4, m=4, a=2)
        sz = view(carve(4 * 4 * P), "p (s m n) -> p s m n", s=4, m=4)
        DT = view(carve(4 * P), "p (m n) -> p m n", m=4)
        dlast = view(carve(4 * 4), "p (s m) -> p s m", s=4)
        Y = view(carve(4 * 4 * P), "p (s m n) -> p s m n", s=4, m=4)
        X = view(carve(2 * 4 * P), "p (s m n) -> p s m n", s=2, m=4)
        NX = view(carve(2 * 4 * P), "p (s m n) -> p s m n", s=2, m=4)
        w01 = view(carve(8 * P), "p (s c r n) -> p s c r n", s=2, c=TT, r=R)
        w0s = view(carve(4 * P), "p (s r n) -> p s r n", s=2, r=R)
        st = view(carve(4 * P), "p (s n) -> p s n", s=2)
        rhs1 = view(carve(4 * P), "p (s r n) -> p s r n", s=2, r=R)
        qst = view(carve(4 * P), "p (s r n) -> p s r n", s=2, r=R)
        xf = view(carve(8 * P), "p (s c r n) -> p s c r n", s=2, c=TT, r=R)
        xfn = view(carve(8 * P), "p (s c r n) -> p s c r n", s=2, c=TT, r=R)
        xnT = view(carve(4 * T), "p (s r n) -> p s r n", s=2, r=R)

        def tiny(*shape):
            n = int(np.prod(shape))
            ap = carve(n, "small")
            return view(ap, "p (a b) -> p a b", a=shape[0]) if len(shape) == 2 else ap

        wz = view(big[:, :], "p (k n) -> p k n", k=KD)

        banks = [ctx.enter_context(nc.psum_tensor(f"bank{n}", [P, 512], F32)) for n in range(8)]

        def bank(n, pattern=None, **k):
            return banks[n][:, :] if pattern is None else banks[n][:, :].rearrange(pattern, **k)

        x_in, w_attn, w_ffn, w_ffn2, w_gdn, c_in = (sem(n) for n in ("x_in", "w_attn", "w_ffn", "w_ffn2", "w_gdn", "c_in"))
        consts, out_done = sem("consts"), sem("out_done")
        vstep, astep = sem("vstep"), sem("astep")
        normed, xt_ps, xt_ready, x_done = (sem(n) for n in ("normed", "xt_ps", "xt_ready", "x_done"))
        qk_in, v_ps, q_sb, v_sb, bank_clear, rs_done, pn_done = (
            sem(n) for n in ("qk_in", "v_ps", "q_sb", "v_sb", "bank_clear", "rs_done", "pn_done"))
        s_ps, mx_done, exp_done, pt_ps, pt_sb, pv_done = (sem(n) for n in ("s_ps", "mx_done", "exp_done", "pt_ps", "pt_sb", "pv_done"))
        o_sb, out_ps, xb_done = (sem(n) for n in ("o_sb", "out_ps", "xb_done"))
        rt_ps, gap_done, th_done, parts_done, ct_ps, ct_sb = (sem(n) for n in ("rt_ps", "gap_done", "th_done", "parts_done", "ct_ps", "ct_sb"))
        gu_ps, gact_done, h_done, cb_ps, ht_done, dn_done = (sem(n) for n in ("gu_ps", "gact_done", "h_done", "cb_ps", "ht_done", "dn_done"))
        ba_ps, ba_sb, g_to_act, g_to_dve, g_done, gc_ps, eg_done = (sem(n) for n in ("ba_ps", "ba_sb", "g_to_act", "g_to_dve", "g_done", "gc_ps", "eg_done"))
        gparts_done, at_ps, at_sb, nbeta_done = (sem(n) for n in ("gparts_done", "at_ps", "at_sb", "nbeta_done"))
        qk_ps, vp_ps, z_ps, tap_qk, tap_v, conv_qk, conv_v, yc_done, z_sb = (
            sem(n) for n in ("qk_ps", "vp_ps", "z_ps", "tap_qk", "tap_v", "conv_qk", "conv_v", "yc_done", "z_sb"))
        qkt_ps, vt_ps, sq_done, vt_sb, qkn_done, kq_ps, kq_sb, kk_ps, ab_ps, dt_done, up_done = (
            sem(n) for n in ("qkt_ps", "vt_ps", "sq_done", "vt_sb", "qkn_done", "kq_ps", "kq_sb", "kk_ps", "ab_ps", "dt_done", "up_done"))
        y_pre, y_done, xx_ps, xx_sb, nx_ps, nx_sb, yuy_ps = (
            sem(n) for n in ("y_pre", "y_done", "xx_ps", "xx_sb", "nx_ps", "nx_sb", "yuy_ps"))
        y_first = sem("y_first")
        w0_ps, w0_sb, st_ps, st_sb, ks_ps, r_done, w1_ps, w1_sb, og_ps, xf_done, sqx_done, xfn_done, xnt_ps, xnt_sb, acc_done = (
            sem(n) for n in ("w0_ps", "w0_sb", "st_ps", "st_sb", "ks_ps", "r_done", "w1_ps", "w1_sb", "og_ps", "xf_done",
                             "sqx_done", "xfn_done", "xnt_ps", "xnt_sb", "acc_done"))

        ssq_done, rn_done, ssx_done, pstep, gmove_done, wout_scaled = (
            sem(n) for n in ("ssq_done", "rn_done", "ssx_done", "pstep", "gmove_done", "wout_scaled"))
        qs_ps, qst_done, pconsts = (sem(n) for n in ("qs_ps", "qst_done", "pconsts"))

        def at_least(eng, s, value):
            if not isinstance(value, int) or value > 0:
                eng.wait_ge(s, value)

        XT_BANK = 7
        E0, E1, E2, ACC = 7, 6, 5, 4

        block = ctx.enter_context(nc.Block())

        @block.sync
        def _(sp):
            xin = io["x"].rearrange("(n p) d -> p n d", p=P)
            sp.dma_start(x[:, 0:TT, :], xin[:, 0:TT, :]).then_inc(x_in, 16)
            for name, dst in (("ident", ident[:, :]), ("upto", upto[:, :]), ("merge", merge[:, :, :]), ("pick", pick[:, :]),
                              ("desc", desc[:, :, :]), ("qmask", qmask[:, :]), ("normw", normw[:, :]), ("A_log", negA[:, :]), ("dt_bias", dtb[:, :])):
                sp.dma_start(dst, io[name]).then_inc(c_in, 16)
            for name, dst in (("wq", wq), ("wk", wk), ("wv", wv), ("bq", bq), ("bk", bk), ("bv", bv), ("bo", bo), ("wo", wo)):
                sp.dma_start(dst, io[name]).then_inc(w_attn, 16)
            sp.dma_start(x[:, TT:, :], xin[:, TT:, :]).then_inc(x_in, 16)
            for name, dst in (("wg", ffnw[0][0]), ("wu", ffnw[0][1]), ("wd", ffnw[0][2]), ("wr", wr[:, :, :])):
                sp.dma_start(dst, io[name]).then_inc(w_ffn, 16)
            for name, dst in (("wout", wout[:, :, :]), ("wba", wba[:, :, :]), ("convw", convw[:, :, :, :]), ("wz", wz)):
                sp.dma_start(dst, io[name]).then_inc(w_gdn, 16)
            if stages > 3:
                sp.wait_ge(z_ps, NK * NBATCH)
                for name, dst in (("wg", ffnw[1][0]), ("wu", ffnw[1][1]), ("wd", ffnw[1][2])):
                    sp.dma_start(dst, io[name]).then_inc(w_ffn2, 16)
            out = io["out"].rearrange("(n p) d -> p n d", p=P)
            with sp.Fori(0, NBATCH) as i:
                sp.wait_ge(x_done, (stages - 1) * NBATCH + 1 + i)
                sp.dma_start(out[:, bass.ds(2 * i, TT), :], x[:, bass.ds(2 * i, TT), :]).then_inc(out_done, 16)
            sp.wait_ge(out_done, 16 * NBATCH)

        def pool_waits():
            nc.gpsimd.tensor_tensor(carried[:, 2:3], ident[:, 0:1], ident[:, 0:1], ALU.add)

        def rsqrt(steps, vec, y, val, t):
            steps.link(vec.tensor_scalar(y.bitcast(I32), val.bitcast(I32), -0.5, float(0x5F375A86), ALU.mult, ALU.add))
            for step in range(3):
                steps.link(vec.tensor_tensor(t, y, y, ALU.mult))
                steps.link(vec.tensor_tensor(t, t, val, ALU.mult))
                steps.link(vec.tensor_scalar(t, t, -0.5, 1.5, ALU.mult, ALU.add))
                steps.link(vec.tensor_tensor(y, y, t, ALU.mult))

        def rsqrt_pool(steps, y, half, eps, t):
            steps.link(nc.gpsimd.tensor_tensor(half, half, eps, ALU.add))
            pool_waits()
            steps.link(nc.gpsimd.tensor_scalar(y.bitcast(I32), half.bitcast(I32), -0.5, float(0x5F375A86 - (1 << 22)),
                                               ALU.mult, ALU.add))
            for step in range(3):
                steps.link(nc.gpsimd.tensor_tensor(t, y, y, ALU.mult))
                steps.link(nc.gpsimd.tensor_tensor(t, t, half, ALU.mult))
                steps.link(nc.gpsimd.tensor_tensor(t, onehalf[:, 0:t.shape[1]], t, ALU.subtract))
                if step < 2:
                    steps.link(nc.gpsimd.tensor_tensor(y, y, t, ALU.mult))

        def prep_stats(dve, steps, b):
            for t in range(TT):
                ins = nc.vector.bn_stats(stats[:, t, :], x[:, 2 * b + t, :])
            steps.link(ins)
            nc.vector.tensor_tensor(mean[:, :, :], stats[:, :, 1:2], stats[:, :, 4:5], ALU.add)
            nc.vector.tensor_tensor(newt[:, :, :], stats[:, :, 1:2], stats[:, :, 4:5], ALU.subtract)
            steps.link(nc.vector.tensor_tensor(varp[:, :, :], stats[:, :, 2:3], stats[:, :, 5:6], ALU.add))
            nc.vector.tensor_scalar(mean[:, :, :], mean[:, :, :], 0.5, None, ALU.mult)
            nc.vector.tensor_scalar(varp[:, :, :], varp[:, :, :], 1.0 / D, LN_EPS, ALU.mult, ALU.add)
            steps.link(nc.vector.scalar_tensor_tensor(newt[:, :, :], newt[:, :, :], 0.25, newt[:, :, :], ALU.mult, ALU.mult))
            steps.link(nc.vector.tensor_tensor(varp[:, :, :], varp[:, :, :], newt[:, :, :], ALU.add))

        def prep_rsqrt(steps):
            rsqrt(steps, nc.vector, rstd[:, :, :], varp[:, :, :], newt[:, :, :])

        def prep_apply(dve, c, b):
            at_least(dve, xt_ps, c)
            for t in range(TT):
                ins = nc.vector.tensor_scalar(xn[:, t, :], x[:, 2 * b + t, :], mean[:, t, 0:1], rstd[:, t, 0:1],
                                              ALU.subtract, ALU.mult)
            ins.then_inc(normed, 1)

        def prep_norm(dve, steps, c, b):
            prep_stats(dve, steps, b)
            prep_rsqrt(steps)
            prep_apply(dve, c, b)

        def prep_turn(pe, c, xbank=XT_BANK):
            pe.wait_ge(normed, c + 1)
            at_least(pe, xt_ready, c)
            b = bank(xbank, "p (k n) -> p k n", k=KD)
            for t in range(TT):
                for k in range(KD):
                    ins = nc.tensor.transpose(b[:, k, t * P:(t + 1) * P], xn[:, t, k * P:(k + 1) * P], ident[:, :])
            ins.then_inc(xt_ps, 1)

        def prep_copy(act, c, xbank=XT_BANK, par=0):
            act.wait_ge(xt_ps, c + 1)
            nc.scalar.activation(xT2[:, par, :, :], bank(xbank, "p (k n) -> p k n", k=KD), ACT.Copy).then_inc(xt_ready, 1)

        def split_parts(steps, src, rest, n):
            steps.link(nc.vector.tensor_copy(parts[:, :, 0:n], src))
            steps.link(nc.vector.tensor_tensor(rest, src, parts[:, :, 0:n], ALU.subtract))
            steps.link(nc.vector.tensor_copy(parts[:, :, 32:32 + n], rest))
            steps.link(nc.vector.tensor_tensor(rest, rest, parts[:, :, 32:32 + n], ALU.subtract))
            return nc.vector.tensor_copy(parts[:, :, 64:64 + n], rest)

        def turn_parts(pe, b):
            bb = banks[b][0:96, 0:T // 2].bitcast(BF16)
            for t in range(TT):
                ins = nc.tensor.transpose(bb[:, t * P:(t + 1) * P], parts[:, t, :], identb[:, :])
            return ins

        SBANK, PBANK, OBANK, FBANK = (0, 2, 3, 7), (4, 5), 6, 1
        TURN_LAG, VALUES_LAG = 3, 4
        AT_QK1, AT_V1, AT_PREP, AT_OUT, AT_QK0, AT_V0 = 0, 4, 5, 7, 9, 13

        def qk_pe(pe, a, half):
            if half == 0:
                pe.wait_ge(xt_ready, a + 1)
                at_least(pe, x_done, a - 1)
            else:
                pe.wait_ge(v_sb, 2 * a + 1)
            b = bank(FBANK, "p (w n) -> p w n", w=2)
            for j, w in enumerate((wq, wk)):
                for k in range(KD):
                    ins = nc.tensor.matmul(b[:, j, :], w[:, k, half * P:(half + 1) * P], xT[:, k, :],
                                           start=(k == 0), stop=(k == KD - 1))
            ins.then_inc(qk_in, 1)

        def v_pe(pe, a, half):
            pe.wait_ge(q_sb, 2 * a + half + 1)
            b = bank(FBANK)[:, 0:TT * P].rearrange("p (t n) -> p t n", t=TT)
            for t in range(TT):
                for k in range(KD):
                    ins = nc.tensor.matmul(b[:, t, :], xT[:, k, t * P:(t + 1) * P], wv[:, k, half * P:(half + 1) * P],
                                           start=(k == 0), stop=(k == KD - 1))
            ins.then_inc(v_ps, 1)

        def scores_pe(pe, a, h):
            if h % HB == 0:
                pe.wait_ge(q_sb, 2 * a + h // HB + 1)
            at_least(pe, exp_done, HEADS * a + h - 3)
            b = bank(SBANK[h % 4], "p (t n) -> p t n", t=TT)
            for t in range(TT):
                ins = nc.tensor.matmul(b[:, t, :], qT[:, h, t * P:(t + 1) * P], kT[:, h // HB, :], start=True, stop=True)
            ins.then_inc(s_ps, 1)

        def turn_probs_pe(pe, a, h):
            pe.wait_ge(pn_done, HEADS * a + h + 1)
            at_least(pe, pt_sb, HEADS * a + h - 1)
            b = bank(PBANK[h % 2], "p (t n) -> p t n", t=TT)
            for t in range(TT):
                for kt in range(TT):
                    ins = nc.tensor.transpose(b[:, kt, t * P:(t + 1) * P], probs[:, h % 4, t, kt * P:(kt + 1) * P], ident[:, :])
            ins.then_inc(pt_ps, 1)

        def values_pe(pe, a, h):
            pe.wait_ge(pt_sb, HEADS * a + h + 1)
            if h % HB == 0:
                at_least(pe, o_sb, 2 * a + h // HB)
                pe.wait_ge(v_sb, 2 * a + h // HB + 1)
            r = HP * (h % 4)
            b = bank(OBANK, "p (g n) -> p g n", g=2)[r:r + HD, h // 4 % 2, :]
            for kt in range(TT):
                ins = nc.tensor.matmul(b, v[:, kt, h * HD:(h + 1) * HD], probsT[:, h % 2, kt, :],
                                       start=(kt == 0), stop=(kt == TT - 1))
            ins.then_inc(pv_done, 1)

        def out_pe(pe, a, prepped, tail):
            pe.wait_ge(o_sb, 2 * a + 2)
            if prepped:
                pe.wait_ge(xt_ready, a + 3)
            if tail:
                pe.wait_ge(x_done, a)
            b = bank(FBANK, "p (t n) -> p t n", t=TT)
            for t in range(TT):
                for k in range(QB):
                    ins = nc.tensor.matmul(b[:, t, :], oT[:, k, t * P:(t + 1) * P], wo[:, k, :],
                                           start=(k == 0), stop=(k == QB - 1))
            ins.then_inc(out_ps, 1)

        def attn_pe(pe, a, prev, nxt, prep):
            for s in range(HEADS):
                scores_pe(pe, a, s)
                if s == AT_QK1:
                    qk_pe(pe, a, 1)
                if s == AT_V1:
                    v_pe(pe, a, 1)
                if s == AT_PREP and prep:
                    pe.wait_ge(v_sb, 2 * a + 2)
                    prep_turn(pe, a + 1, FBANK)
                if s == AT_OUT and prev:
                    out_pe(pe, a - 1, prep, False)
                if s == AT_QK0 and nxt:
                    qk_pe(pe, a + 1, 0)
                if s == AT_V0 and nxt:
                    v_pe(pe, a + 1, 0)
                if s >= VALUES_LAG:
                    values_pe(pe, a, s - VALUES_LAG)
                elif prev:
                    values_pe(pe, a - 1, HEADS + s - VALUES_LAG)
                if s >= TURN_LAG:
                    turn_probs_pe(pe, a, s - TURN_LAG)
                elif prev:
                    turn_probs_pe(pe, a - 1, HEADS + s - TURN_LAG)

        def attn_all_pe(pe):
            pe.wait_ge(bank_clear, 1)
            prep_turn(pe, 0, FBANK)
            qk_pe(pe, 0, 0)
            v_pe(pe, 0, 0)
            attn_pe(pe, 0, False, True, True)
            with pe.Fori(1, NBATCH - 1) as a:
                attn_pe(pe, a, True, True, True)
            last = NBATCH - 1
            attn_pe(pe, last, True, False, stages > 1)
            for s in range(VALUES_LAG):
                values_pe(pe, last, HEADS + s - VALUES_LAG)
                if s < TURN_LAG:
                    turn_probs_pe(pe, last, HEADS + s - TURN_LAG)
            out_pe(pe, last, False, True)

        def v_dve(dve, a, half):
            dve.wait_ge(v_ps, 2 * a + half + 1)
            b = bank(FBANK)[:, 0:TT * P].rearrange("p (t n) -> p t n", t=TT)
            cols = slice(half * P, (half + 1) * P)
            nc.vector.tensor_tensor(v[:, :, cols], b, bv[:, cols].unsqueeze(1).to_broadcast([P, TT, P]), ALU.add)\
                .then_inc(v_sb, 1)

        def top_dve(dve, a, h):
            dve.wait_ge(s_ps, HEADS * a + h + 1)
            nc.vector.tensor_reduce(negmax[:, h % 4, :], bank(SBANK[h % 4], "p (t n) -> p t n", t=TT), AX.X, ALU.max,
                                    negate=True).then_inc(mx_done, 1)

        def sums_dve(dve, a, h):
            dve.wait_ge(exp_done, HEADS * a + h + 1)
            nc.vector.reciprocal(rsums[:, h % 4, :], sums[:, h % 4, :]).then_inc(rs_done, 1)

        def probs_dve(dve, a, h):
            dve.wait_ge(pt_ps, HEADS * a + h + 1)
            at_least(dve, pv_done, HEADS * a + h - 1)
            nc.vector.tensor_copy(probsT[:, h % 2, :, :], bank(PBANK[h % 2], "p (t n) -> p t n", t=TT)).then_inc(pt_sb, 1)

        def attn_x_dve(dve, a):
            dve.wait_ge(out_ps, a + 1)
            dve.wait_ge(xb_done, a + 1)
            xs = x[:, bass.ds(2 * a, TT), :]
            nc.vector.tensor_tensor(xs, bank(FBANK, "p (t n) -> p t n", t=TT), xs, ALU.add).then_inc(x_done, 1)

        def attn_dve(dve, steps, a, prev, nxt, prep):
            for s in range(HEADS):
                top_dve(dve, a, s)
                if s >= 1:
                    sums_dve(dve, a, s - 1)
                elif prev:
                    sums_dve(dve, a - 1, HEADS - 1)
                if s >= TURN_LAG:
                    probs_dve(dve, a, s - TURN_LAG)
                elif prev:
                    probs_dve(dve, a - 1, HEADS + s - TURN_LAG)
                if s == AT_V1:
                    v_dve(dve, a, 1)
                if s == AT_PREP - 5 and prep is not None:
                    prep_stats(dve, steps, prep)
                if s == AT_PREP - 4 and prep is not None:
                    prep_rsqrt(steps)
                if s == AT_PREP - 3 and prep is not None:
                    prep_apply(dve, a + 1, prep)
                if s == AT_OUT and prev:
                    attn_x_dve(dve, a - 1)
                if s == AT_V0 and nxt:
                    v_dve(dve, a + 1, 0)

        def attn_all_dve(dve, steps):
            nc.vector.memset(bank(OBANK), 0.0)
            for half in range(KD):
                ins = nc.vector.tensor_tensor(bqm[:, half * HB:(half + 1) * HB], qmask[:, :],
                                              bq[:, half:half + 1].to_broadcast([P, HB]), ALU.mult)
            ins.then_inc(bank_clear, 1)
            prep_norm(dve, steps, 0, 0)
            v_dve(dve, 0, 0)
            attn_dve(dve, steps, 0, False, True, 1)
            start = steps.n
            with dve.Fori(1, NBATCH - 1) as a:
                steps.turn(start + STEPS_ATTN * (a - 1))
                attn_dve(dve, steps, a, True, True, a + 1)
            assert steps.n == STEPS_ATTN, steps.n
            last = NBATCH - 1
            steps.turn(start + STEPS_ATTN * (last - 1))
            attn_dve(dve, steps, last, True, False, 0 if stages > 1 else None)
            sums_dve(dve, last, HEADS - 1)
            for h in range(HEADS - TURN_LAG, HEADS):
                probs_dve(dve, last, h)
            attn_x_dve(dve, last)

        def qk_act(act, a, half, part):
            if part == 0:
                act.wait_ge(qk_in, 2 * a + half + 1)
            b = bank(FBANK, "p (w n) -> p w n", w=2)
            for h in range(*QPART[part]):
                hh = HB * half + h
                ins = nc.scalar.activation(qT[:, hh, :], b[:, 0, :], ACT.Identity, bias=bqm[:, hh:hh + 1],
                                           scale=qmask[:, h:h + 1])
            if part == 0:
                nc.scalar.activation(kT[:, half, :], b[:, 1, :], ACT.Identity, bias=bk[:, half:half + 1])
            if part == len(QPART) - 1:
                ins.then_inc(q_sb, 1)

        QPART = ((0, 2), (2, 5), (5, HB))

        def exp_act(act, a, h):
            act.wait_ge(mx_done, HEADS * a + h + 1)
            at_least(act, pt_ps, HEADS * a + h - 3)
            b = bank(SBANK[h % 4], "p (t n) -> p t n", t=TT)
            for t in range(TT):
                ins = nc.scalar.activation(probs[:, h % 4, t, :], b[:, t, :], ACT.Exp, bias=negmax[:, h % 4, t:t + 1],
                                           accum_out=sums[:, h % 4, t:t + 1])
            ins.then_inc(exp_done, 1)

        def o_act(act, a, half):
            act.wait_ge(pv_done, HEADS * a + HB * (half + 1))
            nc.scalar.activation(oT[:, 2 * half:2 * half + 2, :], bank(OBANK, "p (g n) -> p g n", g=2), ACT.Copy)\
                .then_inc(o_sb, 1)

        def attn_act(act, a, prev, nxt, prep):
            for s in range(HEADS):
                exp_act(act, a, s)
                if 0 <= s - AT_QK1 < len(QPART):
                    qk_act(act, a, 1, s - AT_QK1)
                if s == VALUES_LAG - 1 and prev:
                    o_act(act, a - 1, 1)
                if s == HB + VALUES_LAG - 1:
                    o_act(act, a, 0)
                if s == AT_PREP and prep:
                    prep_copy(act, a + 1, FBANK)
                if 0 <= s - AT_QK0 < len(QPART) and nxt:
                    qk_act(act, a + 1, 0, s - AT_QK0)

        def attn_all_act(act):
            prep_copy(act, 0, FBANK)
            act.wait_ge(bank_clear, 1)
            for part in range(len(QPART)):
                qk_act(act, 0, 0, part)
            attn_act(act, 0, False, True, True)
            with act.Fori(1, NBATCH - 1) as a:
                attn_act(act, a, True, True, True)
            attn_act(act, NBATCH - 1, True, False, stages > 1)
            o_act(act, NBATCH - 1, 1)

        def add_bo_pool(pool, a):
            pool.wait_ge(normed, a + 1)
            for t in range(TT):
                ins = nc.gpsimd.tensor_tensor(x[:, 2 * a + t, :], x[:, 2 * a + t, :], bo, ALU.add)
            ins.then_inc(xb_done, 1)

        def scale_pool(pool, a, h):
            pool.wait_ge(rs_done, HEADS * a + h + 1)
            nc.gpsimd.tensor_tensor(probs[:, h % 4, :, :], probs[:, h % 4, :, :],
                                    rsums[:, h % 4, :].unsqueeze(2).to_broadcast([P, TT, T]), ALU.mult).then_inc(pn_done, 1)

        def attn_pool(pool, a, nxt):
            for s in range(HEADS):
                scale_pool(pool, a, s)
                if s == AT_PREP and nxt:
                    add_bo_pool(pool, a + 1)

        def attn_all_pool(pool):
            add_bo_pool(pool, 0)
            with pool.Fori(0, NBATCH - 1) as a:
                attn_pool(pool, a, True)
            attn_pool(pool, NBATCH - 1, False)

        GUB, CBB, DNB, RTB = (0, 1, 2), (3, 4), 5, 6
        SPREAD_LAG, DOWN_LAG = 2, 3
        AT_TURN, AT_ROUTE, AT_PARTS = 5, 6, 12

        def route_pe(pe, c, f, par):
            pe.wait_ge(xt_ready, c + 1)
            at_least(pe, ct_sb, f)
            rt = banks[RTB][:, 0:TT * 16].rearrange("p (t n) -> p t n", t=TT)
            for t in range(TT):
                for k in range(KD):
                    ins = nc.tensor.matmul(rt[:, t, 0:E + 1], xT2[:, par, k, t * P:(t + 1) * P], wr[:, k, :],
                                           start=(k == 0), stop=(k == KD - 1))
            ins.then_inc(rt_ps, 1)

        def parts_pe(pe, f):
            pe.wait_ge(parts_done, f + 1)
            turn_parts(pe, RTB).then_inc(ct_ps, 1)

        def gate_up_pe(pe, f, j, w, par):
            at_least(pe, h_done, NB * f + (j - 2 if j >= 3 else min(j - 1, 0)))
            b = bank(GUB[j % 3], "p (g n) -> p g n", g=2)
            m = BLK[j]
            for g in range(2):
                for k in range(KD):
                    ins = nc.tensor.matmul(b[0:m, g, :], w[g][:, k, j * P:j * P + m], xT2[:, par, k, :],
                                           start=(k == 0), stop=(k == KD - 1))
            ins.then_inc(gu_ps, 1)

        def spread_pe(pe, f, j, par):
            if j == 0:
                pe.wait_ge(ct_sb, f + 1)
            at_least(pe, ht_done, NB * f + j - 1)
            m = BLK[j]
            sel = selF[:, :, :].rearrange("p e n -> p (e n)")[:, j * P:j * P + m]
            nc.tensor.matmul(banks[CBB[j % 2]][0:m, 0:T], sel, partsT2[:, par, :], start=True, stop=True).then_inc(cb_ps, 1)

        def down_pe(pe, c, f, j, w):
            pe.wait_ge(ht_done, NB * f + j + 1)
            if j == 0:
                at_least(pe, x_done, c)
            b = bank(DNB, "p (t n) -> p t n", t=TT)
            m = BLK[j]
            for t in range(TT):
                ins = nc.tensor.matmul(b[:, t, :], hidT[0:m, j % 2, t * P:(t + 1) * P], w[2][0:m, j, :],
                                       start=(j == 0 and t == 0), stop=(j == NB - 1), skip_group_check=True)
            ins.then_inc(dn_done, 1)

        def ffn_pe(pe, c, f, w, par, prev, more, prep):
            for s in range(NB):
                gate_up_pe(pe, f, s, w, par)
                if s == SPREAD_LAG and not prev:
                    parts_pe(pe, f)
                if s >= SPREAD_LAG:
                    spread_pe(pe, f, s - SPREAD_LAG, par)
                elif prev:
                    spread_pe(pe, f - 1, NB + s - SPREAD_LAG, 1 - par)
                if s >= DOWN_LAG:
                    down_pe(pe, c, f, s - DOWN_LAG, w)
                elif prev:
                    down_pe(pe, c - 1, f - 1, NB + s - DOWN_LAG, w)
                if s == AT_TURN and prep:
                    prep_turn(pe, c + 1)
                if s == AT_ROUTE and more:
                    route_pe(pe, c + 1, f + 1, 1 - par)
                if s == AT_PARTS and more:
                    parts_pe(pe, f + 1)

        def ffn_layer_pe(pe, c, f, w, prep):
            route_pe(pe, c, f, 0)
            ffn_pe(pe, c, f, w, 0, False, True, True)
            with pe.Fori(0, NBATCH // 2 - 1) as pair:
                for i in (1, 2):
                    ffn_pe(pe, 2 * pair + (c + i), 2 * pair + (f + i), w, i % 2, True, True, True)
            last = NBATCH - 1
            ffn_pe(pe, c + last, f + last, w, 1, True, False, prep)
            for s in range(DOWN_LAG):
                if s < SPREAD_LAG:
                    spread_pe(pe, f + last, NB + s - SPREAD_LAG, 1)
                down_pe(pe, c + last, f + last, NB + s - DOWN_LAG, w)

        lg, eq, oh1, oh2 = (tiny(TT, n) for n in (16, E, E, E))
        l8 = lg[:, :, 0:E]

        def first_max(steps, m, src, oh):
            steps.link(nc.vector.tensor_reduce(m, src, AX.X, ALU.max))
            steps.link(nc.vector.tensor_tensor(eq, src, m.to_broadcast([P, TT, E]), ALU.is_equal))
            steps.link(nc.vector.tensor_tensor(eq, eq, desc[:, :, :], ALU.mult))
            steps.link(nc.vector.tensor_reduce(fl["mw"], eq, AX.X, ALU.max))
            steps.link(nc.vector.tensor_tensor(oh, eq, fl["mw"].to_broadcast([P, TT, E]), ALU.is_equal))

        def route_dve(dve, steps, f):
            dve.wait_ge(rt_ps, f + 1)
            rt = banks[RTB][:, 0:TT * 16].rearrange("p (t n) -> p t n", t=TT)
            steps.link(nc.vector.tensor_copy(lg[:, :, 0:E + 1], rt[:, :, 0:E + 1]))
            first_max(steps, fl["m1"], l8, oh1)

        def gap_dve(steps):
            steps.link(nc.vector.scalar_tensor_tensor(fl["l2"], oh1, -1e30, l8, ALU.mult, ALU.add))
            first_max(steps, fl["m2"], fl["l2"], oh2)
            nc.vector.tensor_copy(fl["gap"][:, :, 1:2], lg[:, :, E:E + 1])
            nc.vector.tensor_tensor(fl["gap"][:, :, 0:1], fl["m1"], fl["m2"], ALU.subtract).then_inc(gap_done, 1)

        def combine_dve(dve, steps, f):
            dve.wait_ge(th_done, f + 1)
            nc.vector.tensor_scalar(fl["wt"][:, :, 0:2], fl["th"], 0.5, 0.5, ALU.mult, ALU.add)
            steps.link(nc.vector.tensor_scalar(fl["wt"][:, :, 2:3], fl["th"][:, :, 0:1], -0.5, 0.5, ALU.mult, ALU.add))
            wt = fl["wt"]
            cmb = fl["cmb"]
            nc.vector.tensor_copy(cmb[:, :, E:NE], wt[:, :, 1:2].to_broadcast([P, TT, NE - E]))
            nc.vector.tensor_tensor(oh1, oh1, wt[:, :, 0:1].to_broadcast([P, TT, E]), ALU.mult)
            steps.link(nc.vector.tensor_tensor(oh2, oh2, wt[:, :, 2:3].to_broadcast([P, TT, E]), ALU.mult))
            steps.link(nc.vector.tensor_tensor(cmb[:, :, 0:E], oh1, oh2, ALU.add))

        def combine_parts_dve(steps):
            split_parts(steps, fl["cmb"], fl["rest"], NE).then_inc(parts_done, 1)

        def mul_up_dve(dve, f, j):
            dve.wait_ge(gact_done, NB * f + j + 1)
            at_least(dve, ht_done, NB * f + j - 1)
            m = BLK[j]
            nc.vector.tensor_tensor(hid[0:m, j % 2, :], gact[0:m, j % 2, :], bank(GUB[j % 3])[0:m, T:2 * T], ALU.mult)\
                .then_inc(h_done, 1)

        def weigh_hid_dve(dve, f, j):
            dve.wait_ge(cb_ps, NB * f + j + 1)
            dve.wait_ge(h_done, NB * f + j + 1)
            at_least(dve, dn_done, NB * f + j - 1)
            m = BLK[j]
            nc.vector.tensor_tensor(hidT[0:m, j % 2, :], hid[0:m, j % 2, :], banks[CBB[j % 2]][0:m, 0:T], ALU.mult)\
                .then_inc(ht_done, 1)

        def ffn_x_dve(dve, f, i):
            dve.wait_ge(dn_done, NB * f + NB)
            xs = x[:, bass.ds(2 * i, TT), :]
            nc.vector.tensor_tensor(xs, bank(DNB, "p (t n) -> p t n", t=TT), xs, ALU.add).then_inc(x_done, 1)

        def ffn_dve(dve, steps, c, f, i, prev, more, prep):
            for s in range(NB):
                if s == DOWN_LAG and prev:
                    ffn_x_dve(dve, f - 1, i - 1)
                mul_up_dve(dve, f, s)
                if s >= 1:
                    weigh_hid_dve(dve, f, s - 1)
                elif prev:
                    weigh_hid_dve(dve, f - 1, NB - 1)
                if s == AT_TURN - 3 and prep is not None:
                    prep_stats(dve, steps, prep)
                if s == AT_TURN - 2 and prep is not None:
                    prep_rsqrt(steps)
                if s == AT_TURN - 1 and prep is not None:
                    prep_apply(dve, c + 1, prep)
                if s == AT_ROUTE + 1 and more:
                    route_dve(dve, steps, f + 1)
                if s == AT_ROUTE + 2 and more:
                    gap_dve(steps)
                if s == AT_PARTS - 2 and more:
                    combine_dve(dve, steps, f + 1)
                if s == AT_PARTS - 1 and more:
                    combine_parts_dve(steps)

        def ffn_layer_dve(dve, steps, c, f, prep):
            route_dve(dve, steps, f)
            gap_dve(steps)
            combine_dve(dve, steps, f)
            combine_parts_dve(steps)
            ffn_dve(dve, steps, c, f, 0, False, True, 1)
            start = steps.base + steps.n
            with dve.Fori(0, NBATCH // 2 - 1) as pair:
                for i in (1, 2):
                    steps.turn(start + STEPS_FFN * (2 * pair + (i - 1)))
                    ffn_dve(dve, steps, 2 * pair + (c + i), 2 * pair + (f + i), 2 * pair + i, True, True, 2 * pair + (i + 1))
                    assert steps.n == STEPS_FFN, steps.n
            last = NBATCH - 1
            steps.turn(start + STEPS_FFN * (last - 1))
            ffn_dve(dve, steps, c + last, f + last, last, True, False, prep)
            weigh_hid_dve(dve, f + last, NB - 1)
            ffn_x_dve(dve, f + last, last)

        def route_act(act, f):
            act.wait_ge(gap_done, f + 1)
            nc.scalar.activation(fl["th"], fl["gap"], ACT.Tanh, scale=0.5).then_inc(th_done, 1)

        def parts_act(act, f, par):
            act.wait_ge(ct_ps, f + 1)
            nc.scalar.activation(partsT2[:, par, :], banks[RTB][0:96, 0:T // 2].bitcast(BF16), ACT.Copy).then_inc(ct_sb, 1)

        def ffn_act(act, c, f, par, prev, more, prep):
            for s in range(NB):
                act.wait_ge(gu_ps, NB * f + s + 1)
                at_least(act, h_done, NB * f + s - 1)
                m = BLK[s]
                nc.scalar.activation(gact[0:m, s % 2, :], bank(GUB[s % 3])[0:m, 0:T], ACT.Silu).then_inc(gact_done, 1)
                if s == SPREAD_LAG - 1 and not prev:
                    parts_act(act, f, par)
                if s == AT_TURN and prep:
                    prep_copy(act, c + 1, XT_BANK, 1 - par)
                if s == AT_PARTS - 3 and more:
                    route_act(act, f + 1)
                if s == AT_PARTS and more:
                    parts_act(act, f + 1, 1 - par)

        def ffn_layer_act(act, c, f, prep):
            route_act(act, f)
            ffn_act(act, c, f, 0, False, True, True)
            with act.Fori(0, NBATCH // 2 - 1) as pair:
                for i in (1, 2):
                    ffn_act(act, 2 * pair + (c + i), 2 * pair + (f + i), i % 2, True, True, True)
            last = NBATCH - 1
            ffn_act(act, c + last, f + last, 1, True, False, prep)

        fl = {"l2": tiny(TT, E),
              "m1": tiny(TT, 1), "m2": tiny(TT, 1), "mw": tiny(TT, 1), "gap": tiny(TT, 2), "th": tiny(TT, 2),
              "wt": tiny(TT, 4), "cmb": tiny(TT, NE), "rest": tiny(TT, NE)}

        HALF = 0.5 ** 0.5
        gt = {n: tiny(TT, NV) for n in ("ad", "neg", "th", "e", "u", "ln", "d", "z", "r", "g", "rest", "alpha")}
        ba = tiny(TT, 2 * NV)
        nbeta, nbeta_walk = tiny(TT, NV), tiny(TT, NV)
        eG, eG_walk = tiny(NV), tiny(NV)
        ssq, rn, rtmp = tiny(4), tiny(4), tiny(4)
        ssx, rx, rxt, bd = tiny(8), tiny(8), tiny(8), tiny(4)

        def ebank(e, pattern=None, **k):
            return bank((E0, E1, E2)[e], pattern, **k)

        def mm4(b, m, n):
            return bank(b, "p (m n) -> p m n", m=4)[:, m, :]

        def gates_pe_ba(pe, g):
            pe.wait_ge(xt_ready, 2 * NBATCH + g + 1)
            at_least(pe, up_done, NK * g)
            b = ebank(1)[:, 0:TT * 2 * NV].rearrange("p (t n) -> p t n", t=TT)
            for t in range(TT):
                for k in range(KD):
                    ins = nc.tensor.matmul(b[:, t, :], xT[:, k, t * P:(t + 1) * P], wba[:, k, :],
                                           start=(k == 0), stop=(k == KD - 1))
            ins.then_inc(ba_ps, 1)

        def gates_dve_ba(dve, g):
            dve.wait_ge(ba_ps, g + 1)
            nc.vector.tensor_copy(ba, ebank(1)[:, 0:TT * 2 * NV].rearrange("p (t n) -> p t n", t=TT)).then_inc(ba_sb, 1)

        def gates_dve_0(dve, steps, g):
            dve.wait_ge(ba_sb, g + 1)
            steps.link(nc.vector.tensor_tensor(gt["ad"], ba[:, :, NV:], dtb[:, :].unsqueeze(1).to_broadcast([P, TT, NV]), ALU.add))
            steps.link(nc.vector.tensor_scalar(gt["neg"], gt["ad"], -1.0, None, ALU.mult))
            nc.vector.tensor_tensor(gt["neg"], gt["neg"], gt["ad"], ALU.min).then_inc(g_to_act, 1)

        def gates_dve_1(dve, steps, g):
            dve.wait_ge(g_to_dve, 3 * g + 1)
            nc.vector.tensor_scalar(gt["u"], gt["e"], 1.0, None, ALU.add).then_inc(g_to_act, 1)
            dve.wait_ge(g_to_act, 2 * g + 2)
            steps.link(nc.vector.tensor_scalar(gt["d"], gt["u"], -1.0, None, ALU.add))
            steps.link(nc.vector.tensor_scalar(gt["z"], gt["d"], 0.0, None, ALU.is_equal))
            steps.link(nc.vector.tensor_tensor(gt["d"], gt["d"], gt["z"], ALU.add))
            steps.link(nc.vector.reciprocal(gt["r"], gt["d"]))
            steps.link(nc.vector.tensor_tensor(gt["r"], gt["r"], gt["e"], ALU.mult))

        def gates_dve_2(dve, steps, g):
            dve.wait_ge(g_to_dve, 3 * g + 2)
            steps.link(nc.vector.tensor_tensor(gt["z"], gt["z"], gt["ln"], ALU.add))
            steps.link(nc.vector.tensor_tensor(gt["z"], gt["z"], gt["r"], ALU.mult))
            steps.link(nc.vector.scalar_tensor_tensor(gt["z"], gt["ad"], 0.0, gt["z"], ALU.max, ALU.add))
            nc.vector.tensor_tensor(gt["g"], gt["z"], negA[:, :].unsqueeze(1).to_broadcast([P, TT, NV]), ALU.mult)\
                .then_inc(g_done, 1)
            nc.vector.tensor_scalar(nbeta, gt["th"], -0.5, -0.5, ALU.mult, ALU.add).then_inc(nbeta_done, 1)

        def gates_dve_3(dve, steps, g):
            dve.wait_ge(g_to_dve, 3 * g + 3)
            at_least(dve, at_ps, g)
            split_parts(steps, gt["alpha"], gt["rest"], NV).then_inc(gparts_done, 1)

        GATES_DVE = (gates_dve_0, gates_dve_1, gates_dve_2, gates_dve_3)

        def gates_act_0(act, g):
            act.wait_ge(ba_sb, g + 1)
            nc.scalar.activation(gt["th"], ba[:, :, 0:NV], ACT.Tanh, scale=0.5)
            act.wait_ge(g_to_act, 2 * g + 1)
            nc.scalar.activation(gt["e"], gt["neg"], ACT.Exp).then_inc(g_to_dve, 1)

        def gates_act_1(act, g):
            act.wait_ge(g_to_act, 2 * g + 2)
            nc.scalar.activation(gt["ln"], gt["u"], ACT.Ln).then_inc(g_to_dve, 1)

        def gates_act_2(act, g):
            act.wait_ge(g_done, g + 1)
            nc.scalar.activation(gt["alpha"], gt["g"], ACT.Exp).then_inc(g_to_dve, 1)

        GATES_ACT = (gates_act_0, gates_act_1, gates_act_2)

        def gates_pe_rest(pe, g):
            pe.wait_ge(vt_sb, NK * g + 1)
            pe.wait_ge(g_done, g + 1)
            nc.tensor.matmul(ebank(1)[:, 0:NV], upto[:, :], gt["g"][:, 1, :], start=True, stop=True).then_inc(gc_ps, 1)
            pe.wait_ge(gparts_done, g + 1)
            pe.wait_ge(eg_done, g + 1)
            turn_parts(pe, E1).then_inc(at_ps, 1)

        def gates_act_rest(act, g):
            act.wait_ge(gc_ps, g + 1)
            at_least(act, gmove_done, g)
            nc.scalar.activation(eG, ebank(1)[:, 0:NV], ACT.Exp).then_inc(eg_done, 1)
            act.wait_ge(at_ps, g + 1)
            nc.scalar.activation(partsT2[:, 0, :], banks[E1][0:96, 0:T // 2].bitcast(BF16), ACT.Copy).then_inc(at_sb, 1)

        def gates_move(dve, g):
            dve.wait_ge(eg_done, g + 1)
            dve.wait_ge(nbeta_done, g + 1)
            at_least(dve, qst_done, NK // 2 * g)
            nc.vector.tensor_copy(nbeta_walk, nbeta)
            nc.vector.tensor_copy(eG_walk, eG).then_inc(gmove_done, 1)
            dve.wait_ge(gmove_done, g + 1)

        def project_pe(pe, H, n, e, gates):
            w0 = (n % NK) * GROUP * P + 2 * e * P
            if e == 0:
                at_least(pe, kq_sb, H)
            else:
                at_least(pe, up_done, H)
                if n % NK == 0:
                    pe.wait_ge(ba_sb, gates)
            b = ebank(e, "p (b n) -> p b n", b=2)
            for j in range(2):
                for k in range(KD):
                    ins = nc.tensor.matmul(b[:, j, :], wz[:, k, w0 + j * P:w0 + (j + 1) * P], xT[:, k, :],
                                           start=(k == 0), stop=(k == KD - 1))
            ins.then_inc((qk_ps, vp_ps)[e], 1)

        def project_z_pe(pe, H, n):
            w0 = (n % NK) * GROUP * P + 4 * P
            pe.wait_ge(dt_done, H + 1)
            b = ebank(1, "p (c n) -> p c n", c=TT)
            for c in range(TT):
                for k in range(KD):
                    ins = nc.tensor.matmul(b[:, c, :], xT[:, k, c * P:(c + 1) * P], wz[:, k, w0:w0 + 2 * P],
                                           start=(k == 0), stop=(k == KD - 1))
            ins.then_inc(z_ps, 1)

        def taps_act(act, H, n, e):
            if e == 0:
                at_least(act, vt_ps, H)
            act.wait_ge((qk_ps, vp_ps)[e], H + 1)
            b = ebank(e, "p (b n) -> p b n", b=2)
            for j in range(2):
                blk = 2 * e + j
                ins = nc.scalar.activation(yc[:, blk, :], b[:, j, :], ACT.Copy, scale=convw[:, n % NK, blk, TAPS - 1:TAPS])
            ins.then_inc((tap_qk, tap_v)[e], 1)

        def conv_dve(dve, steps, H, n, e):
            dve.wait_ge((tap_qk, tap_v)[e], H + 1)
            b = ebank(e, "p (b n) -> p b n", b=2)
            for back in range(1, TAPS):
                for j in range(2):
                    blk = 2 * e + j
                    ins = nc.vector.scalar_tensor_tensor(yc[:, blk, back:], b[:, j, 0:T - back],
                                                         convw[:, n % NK, blk, TAPS - 1 - back:TAPS - back],
                                                         yc[:, blk, back:], ALU.mult, ALU.add)
                if back < TAPS - 1:
                    steps.link(ins)
            ins.then_inc((conv_qk, conv_v)[e], 1)

        def z_act(act, H, n):
            act.wait_ge(z_ps, H + 1)
            nc.scalar.activation(sz[:, n % 4, :, :].rearrange("p m n -> p (m n)"), ebank(1), ACT.Silu).then_inc(z_sb, 1)

        def silu_act(act, H, n):
            act.wait_ge(conv_qk, H + 1)
            act.wait_ge(conv_v, H + 1)
            nc.scalar.activation(yc[:, :, :], yc[:, :, :], ACT.Silu).then_inc(yc_done, 1)

        def turn_pe(pe, H, n):
            pe.wait_ge(yc_done, H + 1)
            for j in range(2):
                for c in range(TT):
                    ins = nc.tensor.transpose(mm4(E0, 2 * j + c, P), yc[:, j, c * P:(c + 1) * P], ident[:, :])
            ins.then_inc(qkt_ps, 1)
            for c in range(TT):
                for r in range(R):
                    ins = nc.tensor.transpose(mm4(E1, 2 * c + r, P), yc[:, 2 + r, c * P:(c + 1) * P], ident[:, :])
            ins.then_inc(vt_ps, 1)

        def squares_act(act, H, n):
            act.wait_ge(qkt_ps, H + 1)
            at_least(act, qkn_done, H)
            nc.scalar.activation(sq, ebank(0), ACT.Square, scale=HALF).then_inc(sq_done, 1)
            act.wait_ge(vt_ps, H + 1)
            nc.scalar.activation(vt[:, n % 4, :, :].rearrange("p m n -> p (m n)"), ebank(1), ACT.Copy).then_inc(vt_sb, 1)

        def sum_dve(dve, H, n):
            dve.wait_ge(sq_done, H + 1)
            nc.vector.tensor_reduce(ssq, sq.rearrange("p (m n) -> p m n", m=4), AX.X, ALU.add).then_inc(ssq_done, 1)

        def norm_dve(dve, H, n):
            dve.wait_ge(rn_done, H + 1)
            nc.vector.tensor_tensor(qkn[:, n % 4, :, :], ebank(0, "p (m n) -> p m n", m=4),
                                    rn.unsqueeze(2).to_broadcast([P, 4, P]), ALU.mult).then_inc(qkn_done, 1)

        def norm_pool(pool, psteps, H, n):
            pool.wait_ge(ssq_done, H + 1)
            rsqrt_pool(psteps, rn, ssq, eps_qk[:, :], rtmp)
            psteps.link(nc.gpsimd.tensor_tensor(rn, rn, rtmp, ALU.mult))
            nc.gpsimd.tensor_tensor(rn, rn, scale_qk[:, :], ALU.mult).then_inc(rn_done, 1)

        def turn_back_pe(pe, H, n):
            pe.wait_ge(qkn_done, H + 1)
            for c in range(TT):
                for a in range(2):
                    ins = nc.tensor.transpose(mm4(E0, 2 * c + a, P), qkn[:, n % 4, 2 * (1 - a) + c, :], ident[:, :])
            ins.then_inc(kq_ps, 1)

        def turn_back_act(act, H, n):
            act.wait_ge(kq_ps, H + 1)
            nc.scalar.activation(kqT[:, n % 4, :, :, :].rearrange("p c a n -> p (c a n)"), ebank(0), ACT.Copy).then_inc(kq_sb, 1)

        def decays_pe(pe, H, n, gates):
            pe.wait_ge(vt_sb, H + 1)
            if n % NK == 0:
                pe.wait_ge(at_sb, gates)
            b = ebank(1, "p (r n) -> p r n", r=R)
            for r in range(R):
                ins = nc.tensor.matmul(b[:, r, :], selG[:, R * (n % NK) + r, :], partsT2[:, 0, :], start=True, stop=True)
            ins.then_inc(ab_ps, 1)

        def products_pe(pe, H, n):
            pe.wait_ge(kq_sb, H + 1)
            pe.wait_ge(z_sb, H + 1)
            b = ebank(1, "p (c n) -> p c n", c=TT)
            for c in range(TT):
                ins = nc.tensor.matmul(b[:, c, :], kqT[:, n % 4, c, 0, :],
                                       kqT[:, n % 4, c, :, :].rearrange("p a n -> p (a n)"), start=True, stop=True)
            ins.then_inc(kk_ps, 1)

        def decay_dve(dve, H, n):
            dve.wait_ge(ab_ps, H + 1)
            at_least(dve, up_done, H)
            b = ebank(1, "p (r c n) -> p r c n", r=R, c=TT)
            for c in range(TT):
                for r in range(R):
                    ins = nc.vector.tensor_tensor_scan(DT[:, 2 * c + r, :], b[:, r, c, :], ident[:, :], 0.0, ALU.mult, ALU.add)
            ins.then_inc(dt_done, 1)

        def weigh_dve(dve, H, n, gates):
            dve.wait_ge(kk_ps, H + 1)
            dve.wait_ge(dt_done, H + 1)
            if n % NK == 0:
                dve.wait_ge(nbeta_done, gates)
            b = ebank(1, "p (c a n) -> p c a n", c=TT, a=2)
            for c in range(TT):
                for r in range(R):
                    hh = R * (n % NK) + r
                    nc.vector.scalar_tensor_tensor(UP[:, n % 4, 2 * c + r, :, :], b[:, c, :, :], nbeta[:, c, hh:hh + 1],
                                                   DT[:, 2 * c + r, :].unsqueeze(1).to_broadcast([P, 2, P]), ALU.mult, ALU.mult)
            nc.vector.tensor_copy(dlast[:, n % 4, :].unsqueeze(2), DT[:, :, P - 1:P]).then_inc(up_done, 1)

        def first_pool(pool, H, n):
            pool.wait_ge(up_done, H + 1)
            yy = Y[:, n % 4, :, :]
            nc.gpsimd.tensor_tensor(yy, UP[:, n % 4, :, 0, :], merge0[:, :].unsqueeze(1).to_broadcast([P, 4, P]), ALU.mult)\
                .then_inc(y_first, 1)
            pool.wait_ge(y_first, H + 1)
            nc.gpsimd.tensor_tensor(yy, yy, ident[:, :].unsqueeze(1).to_broadcast([P, 4, P]), ALU.add).then_inc(y_pre, 1)

        def turn_of(H, n, k):
            return MID * (H - n % 2) + 2 * k + n % 2 + 1

        def x_pe(pe, H, n, lv):
            if lv == 0:
                pe.wait_ge(y_pre, H + 1)
            else:
                pe.wait_ge(y_done, turn_of(H, n, lv - 1))
            for m in range(4):
                ins = nc.tensor.transpose(mm4(2 * (n % 2), m, P), Y[:, n % 4, m, :], ident[:, :])
            ins.then_inc(xx_ps, 1)

        def x_act(act, H, n, lv):
            act.wait_ge(xx_ps, turn_of(H, n, lv))
            nc.scalar.activation(X[:, n % 2, :, :].rearrange("p m n -> p (m n)"), bank(2 * (n % 2)), ACT.Copy).then_inc(xx_sb, 1)

        def nx_pe(pe, H, n, lv):
            pe.wait_ge(xx_sb, turn_of(H, n, lv - 1))
            for m in range(4):
                ins = nc.tensor.matmul(mm4(2 * (n % 2), m, P), UP[:, n % 4, m, 0, :], X[:, n % 2, m, :], start=True, stop=True)
            ins.then_inc(nx_ps, 1)

        def nx_act(act, H, n, lv):
            act.wait_ge(nx_ps, turn_of(H, n, lv - 1))
            nc.scalar.activation(NX[:, n % 2, :, :].rearrange("p m n -> p (m n)"), bank(2 * (n % 2)), ACT.Copy).then_inc(nx_sb, 1)

        def yuy_pe(pe, H, n, lv):
            pe.wait_ge(nx_sb, turn_of(H, n, lv - 1))
            for m in range(4):
                ins = nc.tensor.matmul(mm4(2 * (n % 2) + 1, m, P), NX[:, n % 2, m, :], Y[:, n % 4, m, :], start=True, stop=True)
            ins.then_inc(yuy_ps, 1)

        def merge_dve(dve, H, n, lv):
            dve.wait_ge(yuy_ps, turn_of(H, n, lv - 1))
            dve.wait_ge(y_pre, H + 1)
            if lv > 1:
                dve.wait_ge(y_done, turn_of(H, n, lv - 2))
            nc.vector.tensor_copy(carried[:, n % 2:n % 2 + 1], ident[:, 0:1])
            nc.vector.copy_predicated(Y[:, n % 4, :, :], merge[:, lv, :].unsqueeze(1).to_broadcast([P, 4, P]),
                                      bank(2 * (n % 2) + 1, "p (m n) -> p m n", m=4)).then_inc(y_done, 1)

        def w0_pe(pe, W, s4):
            pe.wait_ge(y_done, 2 * MID * (W + 1))
            at_least(pe, xnt_sb, 2 * W)
            b = ebank(2, "p (s r n) -> p s r n", s=2, r=R)
            for s in range(2):
                for r in range(R):
                    ins = nc.tensor.matmul(b[:, s, r, :], Y[:, s4 + s, r, :], vt[:, s4 + s, r, :], start=True, stop=True)
            ins.then_inc(w0_ps, 1)

        def w0_dve(dve, steps, W, s4, n):
            steps.link(nc.vector.tensor_tensor(bd.rearrange("p (s r) -> p s r", s=2), dlast[:, s4:s4 + 2, 0:R],
                                               nbeta_walk[:, 0, R * n:R * n + 4].rearrange("p (s r) -> p s r", s=2), ALU.mult))
            dve.wait_ge(w0_ps, W + 1)
            b = ebank(2, "p (s r n) -> p s (r n)", s=2, r=R)
            nc.vector.tensor_copy(w01[:, :, 0, :, :].rearrange("p s r n -> p s (r n)"), b)
            nc.vector.tensor_tensor(w0s.rearrange("p s r n -> p (s r) n"), ebank(2, "p (m n) -> p m n", m=4),
                                    bd.unsqueeze(2).to_broadcast([P, 4, P]), ALU.mult).then_inc(w0_sb, 1)

        def state_pe(pe, W, s4):
            pe.wait_ge(w0_sb, W + 1)
            for s in range(2):
                ins = nc.tensor.matmul(ebank(2, "p (s n) -> p s n", s=2)[:, s, :], qkn[:, s4 + s, 2, :],
                                       w0s[:, s, :, :].rearrange("p r n -> p (r n)"), start=True, stop=True)
            ins.then_inc(st_ps, 1)

        def state_act(act, W):
            act.wait_ge(st_ps, W + 1)
            nc.scalar.activation(st, ebank(2, "p (s n) -> p s n", s=2), ACT.Copy).then_inc(st_sb, 1)

        def from_state_pe(pe, W, s4, a):
            if a == 0:
                pe.wait_ge(st_sb, W + 1)
            else:
                pe.wait_ge(r_done, W + 1)
            for s in range(2):
                ins = nc.tensor.matmul(ebank(2, "p (s n) -> p s n", s=2)[:, s, :], kqT[:, s4 + s, 1, a, :], st[:, s, :],
                                       start=True, stop=True)
            ins.then_inc((ks_ps, qs_ps)[a], 1)

        def rhs_dve(dve, W, s4, n):
            dve.wait_ge(ks_ps, W + 1)
            b = ebank(2, "p (s r n) -> p s r n", s=2, r=R)
            for s in range(2):
                for r in range(R):
                    hh = R * (n + s) + r
                    ins = nc.vector.scalar_tensor_tensor(rhs1[:, s, r, :], b[:, s, r, :], eG_walk[:, hh:hh + 1],
                                                         vt[:, s4 + s, 2 + r, :], ALU.mult, ALU.add)
            ins.then_inc(r_done, 1)

        def qs_dve(dve, W, n):
            dve.wait_ge(qs_ps, W + 1)
            nc.vector.tensor_tensor(qst.rearrange("p s r n -> p (s r) n"), ebank(2, "p (m n) -> p m n", m=4),
                                    eG_walk[:, R * n:R * n + 4].unsqueeze(2).to_broadcast([P, 4, P]), ALU.mult)\
                .then_inc(qst_done, 1)

        def w1_pe(pe, W, s4):
            pe.wait_ge(qst_done, W + 1)
            b = ebank(2, "p (s r n) -> p s r n", s=2, r=R)
            for s in range(2):
                for r in range(R):
                    ins = nc.tensor.matmul(b[:, s, r, :], Y[:, s4 + s, 2 + r, :], rhs1[:, s, r, :], start=True, stop=True)
            ins.then_inc(w1_ps, 1)

        def w1_act(act, W):
            act.wait_ge(w1_ps, W + 1)
            nc.scalar.activation(w01[:, :, 1, :, :].rearrange("p s r n -> p s (r n)"),
                                 ebank(2, "p (s n) -> p s n", s=2), ACT.Copy).then_inc(w1_sb, 1)

        def chunk_out_pe(pe, W, s4, s):
            if s == 0:
                pe.wait_ge(w1_sb, W + 1)
            else:
                pe.wait_ge(xf_done, 2 * W + 1)
            for m in range(4):
                ins = nc.tensor.matmul(mm4(E2, m, P), UP[:, s4 + s, m, 1, :], w01[:, s, m // 2, m % 2, :], start=True, stop=True)
            ins.then_inc(og_ps, 1)

        def gate_dve(dve, steps, W, s4, s):
            if s == 0:
                dve.wait_ge(qst_done, W + 1)
                at_least(dve, xfn_done, W)
            dve.wait_ge(og_ps, 2 * W + s + 1)
            b = ebank(2, "p (m n) -> p m n", m=4)
            steps.link(nc.vector.tensor_tensor(xf[:, s, 1, :, :], b[:, 2:4, :], qst[:, s, :, :], ALU.add))
            nc.vector.tensor_tensor(xf[:, s, 0, :, :], b[:, 0:2, :], sz[:, s4 + s, 0:2, :], ALU.mult)
            nc.vector.tensor_tensor(xf[:, s, 1, :, :], xf[:, s, 1, :, :], sz[:, s4 + s, 2:4, :], ALU.mult).then_inc(xf_done, 1)

        def squares_x_act(act, W):
            act.wait_ge(xf_done, 2 * W + 2)
            nc.scalar.activation(xfn.rearrange("p s c r n -> p (s c r n)"), xf.rearrange("p s c r n -> p (s c r n)"),
                                 ACT.Square, scale=HALF).then_inc(sqx_done, 1)

        def sum_x_dve(dve, W):
            dve.wait_ge(sqx_done, W + 1)
            nc.vector.tensor_reduce(ssx, xfn.rearrange("p s c r n -> p (s c r) n"), AX.X, ALU.add).then_inc(ssx_done, 1)

        def norm_x_pool(pool, psteps, W):
            pool.wait_ge(ssx_done, W + 1)
            rsqrt_pool(psteps, rx, ssx, eps_x[:, :], rxt)
            psteps.link(nc.gpsimd.tensor_tensor(rx, rx, rxt, ALU.mult))
            nc.gpsimd.tensor_tensor(xfn.rearrange("p s c r n -> p (s c r) n"), xf.rearrange("p s c r n -> p (s c r) n"),
                                    rx.unsqueeze(2).to_broadcast([P, 8, P]), ALU.mult).then_inc(xfn_done, 1)

        def turn_x_pe(pe, W, s):
            if s == 0:
                pe.wait_ge(xfn_done, W + 1)
            else:
                pe.wait_ge(xnt_sb, 2 * W + 1)
            for r in range(R):
                for c in range(TT):
                    ins = nc.tensor.transpose(mm4(E2, 2 * r + c, P), xfn[:, s, c, r, :], ident[:, :])
            ins.then_inc(xnt_ps, 1)

        def turn_x_act(act, W, s):
            act.wait_ge(xnt_ps, 2 * W + s + 1)
            nc.scalar.activation(xnT[:, s, :, :].rearrange("p r n -> p (r n)"), ebank(2), ACT.Copy).then_inc(xnt_sb, 1)

        def project_out_pe(pe, W, n, s, c_x):
            pe.wait_ge(xnt_sb, 2 * W + s + 1)
            if n + s == 0:
                pe.wait_ge(x_done, c_x)
            b = bank(ACC, "p (t n) -> p t n", t=TT)
            for r in range(R):
                for t in range(TT):
                    ins = nc.tensor.matmul(b[:, t, :], xnT[:, s, r, t * P:(t + 1) * P], wout[:, R * (n + s) + r, :],
                                           start=(n + s == 0 and r == 0 and t == 0), stop=(n + s == NK - 1 and r == R - 1),
                                           skip_group_check=True)
            ins.then_inc(acc_done, 1)

        def add_x_dve(dve, g, i):
            dve.wait_ge(acc_done, NK * (g + 1))
            xs = x[:, bass.ds(2 * i, TT), :]
            nc.vector.tensor_tensor(xs, bank(ACC, "p (t n) -> p t n", t=TT), xs, ALU.add).then_inc(x_done, 1)

        SLOTS = 3 * MID

        def round_pe(pe, g, p, stage1, walk, prep):
            H = NK * g + 2 * p
            A, B, n = 2 * p + 2, 2 * p + 3, (2 * p - 2) % NK
            W, s4 = (NK // 2) * g + p - 1, (2 * p - 2) % 4
            c_x = 2 * NBATCH + g - (1 if p == 0 else 0)
            for k in range(SLOTS):
                lv = k // 3 + 1
                if k == 0:
                    x_pe(pe, H, 2 * p, 0)
                    if stage1:
                        if A == NK:
                            gates_pe_ba(pe, g + 1)
                        project_pe(pe, H + 2, A, 0, g + 2)
                    x_pe(pe, H + 1, 2 * p + 1, 0)
                for s in range(2):
                    (nx_pe, yuy_pe, x_pe)[k % 3](pe, H + s, 2 * p + s, lv) if not (k % 3 == 2 and lv == MID) else None
                if walk:
                    if k == 0:
                        w0_pe(pe, W, s4)
                    if k == 1:
                        state_pe(pe, W, s4)
                    if k in (2, 3):
                        from_state_pe(pe, W, s4, k - 2)
                    if k == 4:
                        w1_pe(pe, W, s4)
                    if k in (5, 7):
                        chunk_out_pe(pe, W, s4, (k - 5) // 2)
                    if k in (12, 13):
                        turn_x_pe(pe, W, k - 12)
                    if k in (13, 14):
                        project_out_pe(pe, W, n, k - 13, c_x)
                if stage1:
                    if k == 1:
                        project_pe(pe, H + 2, A, 1, g + 2)
                    if k == 4:
                        turn_pe(pe, H + 2, A)
                    if k == 6:
                        if A == NK:
                            gates_pe_rest(pe, g + 1)
                        decays_pe(pe, H + 2, A, g + 2)
                    if k == 8:
                        project_z_pe(pe, H + 2, A)
                        turn_back_pe(pe, H + 2, A)
                    if k == 9:
                        project_pe(pe, H + 3, B, 0, g + 2)
                    if k == 10:
                        products_pe(pe, H + 2, A)
                    if k == 11:
                        project_pe(pe, H + 3, B, 1, g + 2)
                    if k == 14:
                        turn_pe(pe, H + 3, B)
                    if k == 15:
                        decays_pe(pe, H + 3, B, g + 2)
                    if k == 16:
                        project_z_pe(pe, H + 3, B)
                    if k == 17:
                        turn_back_pe(pe, H + 3, B)
                        products_pe(pe, H + 3, B)
            if prep:
                pe.wait_ge(kq_sb, H + 4)
                prep_turn(pe, 2 * NBATCH + g + 1)

        def round_dve(dve, steps, g, p, i, stage1, walk, prep):
            H = NK * g + 2 * p
            A, B, n = 2 * p + 2, 2 * p + 3, (2 * p - 2) % NK
            W, s4 = (NK // 2) * g + p - 1, (2 * p - 2) % 4
            if stage1 and A == NK:
                gates_dve_ba(dve, g + 1)
            for k in range(SLOTS):
                if k % 3 == 1:
                    for s in range(2):
                        merge_dve(dve, H + s, 2 * p + s, k // 3 + 1)
                if walk:
                    if k == 0:
                        w0_dve(dve, steps, W, s4, n)
                    if k == 2:
                        rhs_dve(dve, W, s4, n)
                    if k == 3:
                        qs_dve(dve, W, n)
                    if k in (5, 7):
                        gate_dve(dve, steps, W, s4, (k - 5) // 2)
                    if k == 8:
                        sum_x_dve(dve, W)
                    if k == 15 and p == 0:
                        add_x_dve(dve, g - 1, i - 1)
                if k == 4 and p == 0:
                    gates_move(dve, g)
                if stage1:
                    if 1 <= k <= len(GATES_DVE) and A == NK:
                        GATES_DVE[k - 1](dve, steps, g + 1)
                    if k == 1:
                        conv_dve(dve, steps, H + 2, A, 0)
                    if k == 2:
                        conv_dve(dve, steps, H + 2, A, 1)
                    if k == 5:
                        sum_dve(dve, H + 2, A)
                    if k == 6:
                        decay_dve(dve, H + 2, A)
                    if k == 8:
                        norm_dve(dve, H + 2, A)
                    if k == 10:
                        weigh_dve(dve, H + 2, A, g + 2)
                        conv_dve(dve, steps, H + 3, B, 0)
                    if k == 12:
                        conv_dve(dve, steps, H + 3, B, 1)
                    if k == 14:
                        sum_dve(dve, H + 3, B)
                    if k == 15:
                        decay_dve(dve, H + 3, B)
                    if k == 17:
                        norm_dve(dve, H + 3, B)
                        weigh_dve(dve, H + 3, B, g + 2)
                if k == 12 and prep is not None:
                    prep_stats(dve, steps, prep)
                if k == 13 and prep is not None:
                    prep_rsqrt(steps)
                if k == 15 and prep is not None:
                    prep_apply(dve, 2 * NBATCH + g + 1, prep)

        def round_act(act, g, p, stage1, walk, prep):
            H = NK * g + 2 * p
            A, B = 2 * p + 2, 2 * p + 3
            W = (NK // 2) * g + p - 1
            for k in range(SLOTS):
                if k == 0:
                    x_act(act, H, 2 * p, 0)
                    if stage1:
                        taps_act(act, H + 2, A, 0)
                    x_act(act, H + 1, 2 * p + 1, 0)
                if k % 3 == 0 or (k % 3 == 2 and k < SLOTS - 1):
                    for s in range(2):
                        (nx_act, None, x_act)[k % 3](act, H + s, 2 * p + s, k // 3 + 1)
                if walk:
                    if k == 1:
                        state_act(act, W)
                    if k == 4:
                        w1_act(act, W)
                    if k == 7:
                        squares_x_act(act, W)
                    if k in (12, 13):
                        turn_x_act(act, W, k - 12)
                if stage1:
                    if k == 1:
                        taps_act(act, H + 2, A, 1)
                    if 1 <= k <= len(GATES_ACT) and A == NK:
                        GATES_ACT[k - 1](act, g + 1)
                    if k == 3:
                        silu_act(act, H + 2, A)
                    if k == 4:
                        squares_act(act, H + 2, A)
                    if k == 6 and A == NK:
                        gates_act_rest(act, g + 1)
                    if k == 8:
                        z_act(act, H + 2, A)
                        turn_back_act(act, H + 2, A)
                    if k == 9:
                        taps_act(act, H + 3, B, 0)
                    if k == 11:
                        taps_act(act, H + 3, B, 1)
                    if k == 13:
                        silu_act(act, H + 3, B)
                    if k == 14:
                        squares_act(act, H + 3, B)
                    if k == 16:
                        z_act(act, H + 3, B)
                    if k == 17:
                        turn_back_act(act, H + 3, B)
            if prep:
                prep_copy(act, 2 * NBATCH + g + 1)

        def round_pool(pool, psteps, g, p, stage1, walk):
            H = NK * g + 2 * p
            A, B = 2 * p + 2, 2 * p + 3
            W = (NK // 2) * g + p - 1
            if stage1:
                norm_pool(pool, psteps, H + 2, A)
            if walk:
                norm_x_pool(pool, psteps, W)
            if stage1:
                first_pool(pool, H + 2, A)
                norm_pool(pool, psteps, H + 3, B)
                first_pool(pool, H + 3, B)

        ROUNDS = NK // 2
        PREP = ROUNDS - 2

        def gdn_pe(pe, g, first=False, last=False):
            for p in range(ROUNDS):
                round_pe(pe, g, p, not (last and p == ROUNDS - 1), not (first and p == 0),
                         p == PREP and (not last or stages > 3))

        def gdn_dve(dve, steps, g, first=False, last=False):
            nxt = (0 if stages > 3 else None) if last else g + 1
            for p in range(ROUNDS):
                round_dve(dve, steps, g, p, g, not (last and p == ROUNDS - 1), not (first and p == 0),
                          nxt if p == PREP else None)

        def gdn_act(act, g, first=False, last=False):
            for p in range(ROUNDS):
                round_act(act, g, p, not (last and p == ROUNDS - 1), not (first and p == 0),
                          p == PREP and (not last or stages > 3))

        def gdn_pool(pool, psteps, g, first=False, last=False):
            for p in range(ROUNDS):
                round_pool(pool, psteps, g, p, not (last and p == ROUNDS - 1), not (first and p == 0))

        LASTW = NBATCH * ROUNDS - 1

        def gdn_all_pe(pe):
            pe.wait_ge(x_done, 2 * NBATCH)
            pe.wait_ge(w_gdn, 4 * 16)
            pe.wait_ge(wout_scaled, 1)
            gates_pe_ba(pe, 0)
            for n in range(2):
                project_pe(pe, n, n, 0, 1)
                project_pe(pe, n, n, 1, 1)
                turn_pe(pe, n, n)
                if n == 0:
                    gates_pe_rest(pe, 0)
                decays_pe(pe, n, n, 1)
                project_z_pe(pe, n, n)
                turn_back_pe(pe, n, n)
                products_pe(pe, n, n)
            gdn_pe(pe, 0, first=True)
            with pe.Fori(1, NBATCH - 1) as g:
                gdn_pe(pe, g)
            gdn_pe(pe, NBATCH - 1, last=True)
            n, s4 = NK - 2, 2
            w0_pe(pe, LASTW, s4)
            state_pe(pe, LASTW, s4)
            from_state_pe(pe, LASTW, s4, 0)
            from_state_pe(pe, LASTW, s4, 1)
            w1_pe(pe, LASTW, s4)
            chunk_out_pe(pe, LASTW, s4, 0)
            chunk_out_pe(pe, LASTW, s4, 1)
            turn_x_pe(pe, LASTW, 0)
            turn_x_pe(pe, LASTW, 1)
            project_out_pe(pe, LASTW, n, 0, 0)
            project_out_pe(pe, LASTW, n, 1, 0)

        def gdn_all_dve(dve, steps):
            dve.wait_ge(x_done, 2 * NBATCH)
            dve.wait_ge(pconsts, 1)
            gates_dve_ba(dve, 0)
            for part in GATES_DVE:
                part(dve, steps, 0)
            for n in range(2):
                conv_dve(dve, steps, n, n, 0)
                conv_dve(dve, steps, n, n, 1)
                sum_dve(dve, n, n)
                decay_dve(dve, n, n)
                norm_dve(dve, n, n)
                weigh_dve(dve, n, n, 1)
            base = steps.base + steps.n
            steps.turn(base)
            gdn_dve(dve, steps, 0, first=True)
            base = base + steps.n
            with dve.Fori(1, NBATCH - 1) as g:
                steps.turn(base + STEPS_GDN * (g - 1))
                gdn_dve(dve, steps, g)
            assert steps.n == STEPS_GDN, steps.n
            steps.turn(base + STEPS_GDN * (NBATCH - 2))
            gdn_dve(dve, steps, NBATCH - 1, last=True)
            n, s4 = NK - 2, 2
            w0_dve(dve, steps, LASTW, s4, n)
            rhs_dve(dve, LASTW, s4, n)
            qs_dve(dve, LASTW, n)
            gate_dve(dve, steps, LASTW, s4, 0)
            gate_dve(dve, steps, LASTW, s4, 1)
            sum_x_dve(dve, LASTW)
            add_x_dve(dve, NBATCH - 1, NBATCH - 1)

        def gdn_all_act(act):
            act.wait_ge(x_done, 2 * NBATCH)
            act.wait_ge(w_gdn, 4 * 16)
            for part in GATES_ACT:
                part(act, 0)
            for n in range(2):
                taps_act(act, n, n, 0)
                taps_act(act, n, n, 1)
                silu_act(act, n, n)
                squares_act(act, n, n)
                if n == 0:
                    gates_act_rest(act, 0)
                z_act(act, n, n)
                turn_back_act(act, n, n)
            gdn_act(act, 0, first=True)
            with act.Fori(1, NBATCH - 1) as g:
                gdn_act(act, g)
            gdn_act(act, NBATCH - 1, last=True)
            state_act(act, LASTW)
            w1_act(act, LASTW)
            squares_x_act(act, LASTW)
            turn_x_act(act, LASTW, 0)
            turn_x_act(act, LASTW, 1)

        def gdn_all_pool(pool):
            psteps = Steps(pool, pstep)
            for n in range(2):
                norm_pool(pool, psteps, n, n)
                first_pool(pool, n, n)
            base = psteps.n
            psteps.turn(base)
            gdn_pool(pool, psteps, 0, first=True)
            base = base + psteps.n
            with pool.Fori(1, NBATCH - 1) as g:
                psteps.turn(base + STEPS_POOL * (g - 1))
                gdn_pool(pool, psteps, g)
            assert psteps.n == STEPS_POOL, psteps.n
            psteps.turn(base + STEPS_POOL * (NBATCH - 2))
            gdn_pool(pool, psteps, NBATCH - 1, last=True)
            norm_x_pool(pool, psteps, LASTW)

        @block.gpsimd
        def _(pool):
            pool.wait_ge(w_attn, 8 * 16)
            pool.wait_ge(x_in, 32)

            attn_all_pool(pool)
            nc.gpsimd.memset(onehalf[:, :], 1.5)
            nc.gpsimd.memset(eps_qk[:, :], L2_EPS / 2)
            nc.gpsimd.memset(eps_x[:, :], P * NORM_EPS / 2)
            nc.gpsimd.memset(scale_qk[:, 0:2], float(P) ** -0.5)
            nc.gpsimd.memset(scale_qk[:, 2:4], 1.0).then_inc(pconsts, 1)
            pool.wait_ge(pconsts, 1)
            pool.wait_ge(w_gdn, 4 * 16)
            pool.wait_ge(consts, 1)
            pool.wait_ge(c_in, 9 * 16)
            nc.gpsimd.tensor_scalar(wout[:, :, :], wout[:, :, :], normw[:, 0:1], -float(P) ** 0.5, ALU.mult, ALU.mult)\
                .then_inc(wout_scaled, 1)
            if stages > 2:
                gdn_all_pool(pool)

        ffn_layers = [(1, 0)] + ([(3, 1)] if stages > 3 else [])

        @block.tensor
        def _(pe):
            pe.wait_ge(consts, 1)
            pe.wait_ge(w_attn, 8 * 16)
            attn_all_pe(pe)
            for layer, rep in ffn_layers:
                if layer >= stages:
                    break
                if layer == 3:
                    gdn_all_pe(pe)
                pe.wait_ge(x_done, layer * NBATCH)
                pe.wait_ge(*((w_ffn, 4 * 16) if rep == 0 else (w_ffn2, 3 * 16)))
                ffn_layer_pe(pe, layer * NBATCH, rep * NBATCH, ffnw[rep], layer + 1 < stages)
            if stages == 3:
                gdn_all_pe(pe)

        @block.vector
        def _(dve):
            steps = Steps(dve, vstep)
            nc.vector.memset(parts[:, :, :], 0.0)
            dve.wait_ge(c_in, 9 * 16)
            nc.vector.tensor_copy(identb[:, :], ident[:, :])
            nc.vector.tensor_copy(merge0[:, :], merge[:, 0, :])
            nc.vector.tensor_copy(selF[:, :, :], pick[:, 0:NE].unsqueeze(2).to_broadcast([96, NE, HID]))
            nc.vector.tensor_copy(selG[:, :, :], pick[:, 0:NV].unsqueeze(2).to_broadcast([96, NV, P])).then_inc(consts, 1)
            dve.wait_ge(astep, 1)
            steps.link(nc.vector.tensor_scalar(negA[:, :], negA[:, :], -1.0, None, ALU.mult))
            dve.wait_ge(x_in, 32)
            dve.wait_ge(w_attn, 8 * 16)
            attn_all_dve(dve, steps)
            for layer, rep in ffn_layers:
                if layer >= stages:
                    break
                if layer == 3:
                    gdn_all_dve(dve, steps)
                dve.wait_ge(x_done, layer * NBATCH)
                ffn_layer_dve(dve, steps, layer * NBATCH, rep * NBATCH, 0 if layer + 1 < stages else None)
            if stages == 3:
                gdn_all_dve(dve, steps)

        @block.scalar
        def _(act):
            act.wait_ge(c_in, 9 * 16)
            nc.scalar.activation(negA[:, :], negA[:, :], ACT.Exp).then_inc(astep, 1)
            act.wait_ge(w_attn, 8 * 16)
            attn_all_act(act)
            for layer, rep in ffn_layers:
                if layer >= stages:
                    break
                if layer == 3:
                    gdn_all_act(act)
                act.wait_ge(x_done, layer * NBATCH)
                ffn_layer_act(act, layer * NBATCH, rep * NBATCH, layer + 1 < stages)
            if stages == 3:
                gdn_all_act(act)


def consts():
    p = np.arange(P)
    upto = (p[:, None] <= p[None, :]).astype(np.float32)
    merge = np.zeros((P, LEVELS, P), np.int32)
    for lv in range(LEVELS):
        b = 1 << lv
        same = p[:, None] // (2 * b) == p[None, :] // (2 * b)
        merge[:, lv, :] = same & ((p[:, None] // b) % 2 == 0) & ((p[None, :] // b) % 2 == 1)
    pick = (np.arange(96)[:, None] % 32 == np.arange(16)[None, :]).astype(np.float32)
    desc = np.ascontiguousarray(np.broadcast_to(np.arange(E, 0, -1, dtype=np.float32), (P, TT, E)))
    qmask = SM_SCALE * (p[:, None] // HD == np.arange(HB)[None, :]).astype(np.float32)
    return {"ident": np.eye(P, dtype=np.float32), "qmask": qmask.astype(np.float32), "upto": upto, "merge": merge, "pick": pick, "desc": desc}


def laid_out(inp):
    def g(n):
        return np.asarray(inp[n])

    def by_rows(w):
        return np.ascontiguousarray(w.reshape(KD, P, -1).transpose(1, 0, 2))

    def padded(w):
        out = np.zeros((HEADS, HP, w.shape[1]), w.dtype)
        out[:, :HD] = w.reshape(HEADS, HD, -1)
        return out.reshape(HEADS * HP, -1)

    def spread(v):
        return np.ascontiguousarray(np.broadcast_to(v, (P, v.shape[-1])))

    a = "L0_attn_a_"
    b = "L0_attn_b_"
    f = "L0_ffn_"
    r = {"x": np.ascontiguousarray(g(a + "x").reshape(NBATCH * T, D))}
    for n, key in (("wq", "Wq"), ("wk", "Wk"), ("wv", "Wv")):
        r[n] = by_rows(g(a + key).T)
    r["wo"] = np.ascontiguousarray(padded(g(a + "Wo").T).reshape(QB, P, D).transpose(1, 0, 2))
    for n in ("bq", "bk"):
        r[n] = np.ascontiguousarray(g(a + n).reshape(KD, P).T)
    r["bv"], r["bo"] = spread(g(a + "bv")), spread(g(a + "bo"))
    for n, ew, sw in (("wg", "w_gate", "shw_gate"), ("wu", "w_up", "shw_up")):
        r[n] = by_rows(np.concatenate([g(f + ew).transpose(1, 0, 2).reshape(D, E * HID), g(f + sw)], 1))
    wd = np.zeros((NB * P, D), np.float32)
    wd[:E * HID] = g(f + "w_down").reshape(E * HID, D)
    wd[E * HID:FH] = g(f + "shw_down")
    r["wd"] = np.ascontiguousarray(wd.reshape(NB, P, D).transpose(1, 0, 2))
    r["wr"] = by_rows(np.concatenate([g(f + "gate_w"), g(f + "shgate_w")[None]], 0).T)
    r["wz"] = by_rows(g(b + "w_qkvz").T)
    ba = g(b + "w_ba").reshape(NK, 2, R, D).transpose(1, 0, 2, 3).reshape(2 * NV, D)
    r["wba"] = by_rows(ba.T)
    r["wout"] = np.ascontiguousarray(g(b + "w_out").T.reshape(NV, P, D).transpose(1, 0, 2))
    cw = g(b + "conv_w")
    r["convw"] = np.ascontiguousarray(np.concatenate([
        cw[:NK * P].reshape(NK, 1, P, TAPS), cw[NK * P:2 * NK * P].reshape(NK, 1, P, TAPS),
        cw[2 * NK * P:].reshape(NK, R, P, TAPS)], 1).transpose(2, 0, 1, 3))
    r["dt_bias"], r["A_log"] = spread(g(b + "dt_bias")), spread(g(b + "A_log"))
    r["normw"] = np.ascontiguousarray(g(b + "norm_weight")[:, None])
    r.update(consts())
    return r


def kernel(**inputs):
    import concourse.bacc as bacc
    from concourse.bass_utils import run_bass_kernel_spmd as run

    nc = bacc.Bacc("TRN2", target_bir_lowering=False, num_devices=1)
    arrays, io = {}, {}
    for name, a in laid_out(inputs).items():
        arrays[f"in_{name}"] = a
        io[name] = nc.dram_tensor(f"in_{name}", a.shape, mybir.dt.from_np(a.dtype), kind="ExternalInput").ap()
    io["out"] = nc.dram_tensor("out", (NBATCH * T, D), F32, kind="ExternalOutput").ap()
    build(nc, io)
    r = run(nc, [arrays], core_ids=[0])
    return r.results[0]["out"].reshape(NBATCH, T, D)
```
